# Optimizing a Trainium2 kernel written in Bass

```python
import numpy as np
import jax
import jax.numpy as jnp

def _softmax(x, axis=-1):
    return jax.nn.softmax(x, axis=axis)

def _gelu(x):
    return jax.nn.gelu(x, approximate=True)

def _silu(x):
    return jax.nn.silu(x)

def _sigmoid(x):
    return jax.nn.sigmoid(x)

def _layernorm(x, axis=-1, eps=1e-05):
    m = jnp.mean(x, axis=axis, keepdims=True)
    v = jnp.var(x, axis=axis, keepdims=True)
    return (x - m) / jnp.sqrt(v + eps)

def _scatter_add(tgt, idx, src, axis=0):
    return tgt.at[idx].add(src)

def _segment_sum(src, seg, n):
    return jax.ops.segment_sum(src, seg, n)
kernel_name = 'mk_hybrid_d1_jaxref_r8_5054dd'

def setup_inputs(seed: int=0):
    np.random.seed(seed)
    _w = jnp.asarray

    def _L0_attn_a_setup():
        import jax, jax.numpy as jnp
        import numpy as np
        NUM_HEADS = 16
        BLOCK_SIZE = 64
        key = jax.random.key(seed)
        ks = jax.random.split(key, 4)
        B, S, D = (4, 1024, 128)
        x = jax.random.normal(ks[0], (B, S, D), dtype=jnp.float32)
        Wq = jax.random.normal(ks[1], (D, D), dtype=jnp.float32) * 0.02
        Wk = jax.random.normal(ks[2], (D, D), dtype=jnp.float32) * 0.02
        Wv = jax.random.normal(ks[3], (D, D), dtype=jnp.float32) * 0.02
        bq = jnp.zeros((D,), dtype=jnp.float32)
        bk = jnp.zeros((D,), dtype=jnp.float32)
        bv = jnp.zeros((D,), dtype=jnp.float32)
        return {'x': x, 'Wq': Wq, 'bq': bq, 'Wk': Wk, 'bk': bk, 'Wv': Wv, 'bv': bv}
    _L0_attn_a_in = _L0_attn_a_setup()

    def _L0_attn_b_setup():
        import jax, jax.numpy as jnp
        import numpy as np
        H = 16

        def _toroidal_bias(S, dtype):
            eye = jnp.eye(S, dtype=dtype)
            return eye + jnp.roll(eye, 1, axis=1) + jnp.roll(eye, -1, axis=1)
        key = jax.random.key(seed)
        ks = jax.random.split(key, 7)
        E = 128
        S, B = (256, 2)
        sc = 0.02
        return {'x': jax.random.normal(ks[0], (S, B, E), dtype=jnp.float32), 'w_tor': jax.random.normal(ks[1], (E, E), dtype=jnp.float32) * sc, 'b_tor': jax.random.normal(ks[2], (E,), dtype=jnp.float32) * sc, 'in_proj_w': jax.random.normal(ks[3], (3 * E, E), dtype=jnp.float32) * sc, 'in_proj_b': jax.random.normal(ks[4], (3 * E,), dtype=jnp.float32) * sc, 'out_w': jax.random.normal(ks[5], (E, E), dtype=jnp.float32) * sc, 'out_b': jax.random.normal(ks[6], (E,), dtype=jnp.float32) * sc}
    _L0_attn_b_in = _L0_attn_b_setup()

    def _L0_ffn_setup():
        import jax, jax.numpy as jnp
        import numpy as np
        D_MODEL = 128
        HIDDEN = 512
        NUM_EXPERTS = 8
        TOP_K = 2
        DEPTH = 12
        DEPTH_SCALE = 1.0 / np.sqrt(DEPTH)
        key = jax.random.key(seed)
        k_x, k_r, k_g, k_u, k_d = jax.random.split(key, 5)
        s_in = 1.0 / np.sqrt(D_MODEL)
        s_hid = 1.0 / np.sqrt(HIDDEN)
        return {'x': jax.random.normal(k_x, (2, 256, D_MODEL), dtype=jnp.float32), 'Wr': jax.random.normal(k_r, (D_MODEL, NUM_EXPERTS), dtype=jnp.float32) * s_in, 'Wg': jax.random.normal(k_g, (NUM_EXPERTS, D_MODEL, HIDDEN), dtype=jnp.float32) * s_in, 'Wu': jax.random.normal(k_u, (NUM_EXPERTS, D_MODEL, HIDDEN), dtype=jnp.float32) * s_in, 'Wd': jax.random.normal(k_d, (NUM_EXPERTS, HIDDEN, D_MODEL), dtype=jnp.float32) * s_hid}
    _L0_ffn_in = _L0_ffn_setup()
    _d = {'L0_attn_a_x': _L0_attn_a_in['x'], 'L0_attn_a_Wq': _L0_attn_a_in['Wq'], 'L0_attn_a_bq': _L0_attn_a_in['bq'], 'L0_attn_a_Wk': _L0_attn_a_in['Wk'], 'L0_attn_a_bk': _L0_attn_a_in['bk'], 'L0_attn_a_Wv': _L0_attn_a_in['Wv'], 'L0_attn_a_bv': _L0_attn_a_in['bv'], 'L0_attn_b_w_tor': _L0_attn_b_in['w_tor'], 'L0_attn_b_b_tor': _L0_attn_b_in['b_tor'], 'L0_attn_b_in_proj_w': _L0_attn_b_in['in_proj_w'], 'L0_attn_b_in_proj_b': _L0_attn_b_in['in_proj_b'], 'L0_attn_b_out_w': _L0_attn_b_in['out_w'], 'L0_attn_b_out_b': _L0_attn_b_in['out_b'], 'L0_ffn_Wr': _L0_ffn_in['Wr'], 'L0_ffn_Wg': _L0_ffn_in['Wg'], 'L0_ffn_Wu': _L0_ffn_in['Wu'], 'L0_ffn_Wd': _L0_ffn_in['Wd']}
    _x0 = _d['L0_attn_a_x']
    _d['L0_attn_a_x'] = jax.random.normal(jax.random.fold_in(jax.random.key(seed), 1), (16, 256, 128), dtype=_x0.dtype)
    del _x0
    return _d

def reference(L0_attn_a_x, L0_attn_a_Wq, L0_attn_a_bq, L0_attn_a_Wk, L0_attn_a_bk, L0_attn_a_Wv, L0_attn_a_bv, L0_attn_b_w_tor, L0_attn_b_b_tor, L0_attn_b_in_proj_w, L0_attn_b_in_proj_b, L0_attn_b_out_w, L0_attn_b_out_b, L0_ffn_Wr, L0_ffn_Wg, L0_ffn_Wu, L0_ffn_Wd):

    def _L0_attn_a_ref(x, Wq, bq, Wk, bk, Wv, bv):
        import jax, jax.numpy as jnp
        import numpy as np
        NUM_HEADS = 16
        BLOCK_SIZE = 64
        B, S, D = x.shape
        H, bs = (NUM_HEADS, BLOCK_SIZE)
        d = D // H
        nb = S // bs
        q = (x @ Wq + bq).reshape(B, nb, bs, H, d)
        k = (x @ Wk + bk).reshape(B, nb, bs, H, d)
        v = (x @ Wv + bv).reshape(B, nb, bs, H, d)
        scale = 1.0 / jnp.sqrt(jnp.asarray(d, dtype=x.dtype))
        scores = jnp.einsum('bnihd,bnjhd->bnhij', q, k) * scale
        attn = jax.nn.softmax(scores, axis=-1)
        out = jnp.einsum('bnhij,bnjhd->bnihd', attn, v)
        return out.reshape(B, S, D)

    def _L0_attn_b_ref(x, w_tor, b_tor, in_proj_w, in_proj_b, out_w, out_b):
        import jax, jax.numpy as jnp
        import numpy as np
        H = 16

        def _toroidal_bias(S, dtype):
            eye = jnp.eye(S, dtype=dtype)
            return eye + jnp.roll(eye, 1, axis=1) + jnp.roll(eye, -1, axis=1)
        S, B, E = x.shape
        hd = E // H
        scale = 1.0 / jnp.sqrt(jnp.asarray(hd, dtype=x.dtype))
        xt = x @ w_tor.T + b_tor
        qkv = xt @ in_proj_w.T + in_proj_b
        q, k, v = jnp.split(qkv, 3, axis=-1)

        def to_heads(t):
            return t.reshape(S, B, H, hd).transpose(1, 2, 0, 3)
        q, k, v = (to_heads(q), to_heads(k), to_heads(v))
        bias = _toroidal_bias(S, x.dtype)
        scores = jnp.einsum('bhqd,bhkd->bhqk', q * scale, k) + bias
        attn = jax.nn.softmax(scores, axis=-1)
        o = jnp.einsum('bhqk,bhkd->bhqd', attn, v)
        o = o.transpose(2, 0, 1, 3).reshape(S, B, E)
        return o @ out_w.T + out_b

    def _L0_ffn_ref(x, Wr, Wg, Wu, Wd):
        import jax, jax.numpy as jnp
        import numpy as np
        D_MODEL = 128
        HIDDEN = 512
        NUM_EXPERTS = 8
        TOP_K = 2
        DEPTH = 12
        DEPTH_SCALE = 1.0 / np.sqrt(DEPTH)
        B, T, C = x.shape
        flat_x = x.reshape(-1, C)
        logits = flat_x @ Wr
        top_vals, top_idx = jax.lax.top_k(logits, TOP_K)
        rw = jax.nn.softmax(top_vals.astype(jnp.float32), axis=-1).astype(x.dtype)
        combine = jnp.sum(rw[..., None] * jax.nn.one_hot(top_idx, NUM_EXPERTS, dtype=x.dtype), axis=1)
        g = jnp.einsum('nc,ech->neh', flat_x, Wg)
        u = jnp.einsum('nc,ech->neh', flat_x, Wu)
        h = jax.nn.silu(g) * u
        eo = jnp.einsum('neh,ehc->nec', h, Wd) * DEPTH_SCALE
        out = jnp.einsum('ne,nec->nc', combine, eo)
        return out.reshape(B, T, C)
    x = L0_attn_a_x
    x = x + _L0_attn_a_ref(_layernorm(x, axis=-1), L0_attn_a_Wq, L0_attn_a_bq, L0_attn_a_Wk, L0_attn_a_bk, L0_attn_a_Wv, L0_attn_a_bv)
    x = x + _L0_ffn_ref(_layernorm(x, axis=-1), L0_ffn_Wr, L0_ffn_Wg, L0_ffn_Wu, L0_ffn_Wd)
    x = x + _L0_attn_b_ref(_layernorm(x, axis=-1), L0_attn_b_w_tor, L0_attn_b_b_tor, L0_attn_b_in_proj_w, L0_attn_b_in_proj_b, L0_attn_b_out_w, L0_attn_b_out_b)
    x = x + _L0_ffn_ref(_layernorm(x, axis=-1), L0_ffn_Wr, L0_ffn_Wg, L0_ffn_Wu, L0_ffn_Wd)
    return x

_drawn_inputs = setup_inputs


def setup_inputs(seed=0):
    import zlib

    import numpy as np

    out = dict(_drawn_inputs(seed))
    spreads = {'L0_attn_a_bq': (0.0, 0.8), 'L0_attn_a_bk': (0.0, 2.0), 'L0_attn_a_bv': (0.0, 0.1)}
    factors = {'L0_attn_a_Wq': 8.0,
     'L0_attn_a_Wk': 8.0,
     'L0_attn_b_w_tor': 8.0,
     'L0_attn_b_b_tor': 8.0,
     'L0_attn_b_in_proj_w': 8.0,
     'L0_attn_b_in_proj_b': 8.0,
     'L0_attn_b_out_w': 7.375,
     'L0_attn_b_out_b': 8.0}
    for name, (base, spread) in spreads.items():
        noise = np.random.default_rng([zlib.crc32(name.encode()), seed]).standard_normal(out[name].shape)
        drawn = base * np.exp(spread * noise) if base else spread * noise
        out[name] = jnp.asarray(drawn.astype(out[name].dtype))
    for name, factor in factors.items():
        out[name] = (out[name] * factor).astype(out[name].dtype)
    return out
```

```python
from contextlib import ExitStack

import numpy as np
import concourse.bass as bass
from concourse import mybir

F32 = mybir.dt.float32
F32R = mybir.dt.float32r
BF16 = mybir.dt.bfloat16
I32 = mybir.dt.int32
U32 = mybir.dt.uint32
ALU = mybir.AluOpType
ACT = mybir.ActivationFunctionType
X = mybir.AxisListType.X

P = 128
ROWS, POSITIONS, D = 16, 256, 128
TOKENS = ROWS * POSITIONS
TILES = TOKENS // P
HEADS, HD = 16, 8
SCALE = 1.0 / float(np.sqrt(np.float32(HD)))
EPS = 1e-5
BATCH = 4
TB = BATCH * P
BATCHES = TILES // BATCH
SLOTS = 6
STACK = SLOTS * HD
EXPERTS, HIDDEN, TOPK = 8, 512, 2
CHUNKS = HIDDEN // P
DEPTH_SCALE = float(1.0 / np.sqrt(12))
REGION = TOKENS + P
STEPS = 72
SPARE = STEPS - TOPK * TOKENS // P
REGION_ROWS = EXPERTS * REGION + SPARE * P
PAIR = 2 * P

C_IDENT, C_UPPER, C_BIAS, C_MASK_A, C_MASK_B, C_EXPERT, C_BASE, C_STEP, C_ROOT, C_END = (int(x) for x in np.cumsum(
    [0, P, P, 32, 64, 64, EXPERTS, EXPERTS, STEPS, 1]))


def constants():
    c = np.zeros((P, C_END), np.float32)
    p = np.arange(P)
    c[:, C_IDENT:C_UPPER] = np.eye(P)
    c[:, C_UPPER:C_BIAS] = p[:, None] < p[None, :]
    key = np.arange(32)
    same = (p[:, None] // 16) % 2 == key[None, :] // 16
    turn = (key[None, :] % 16 - p[:, None] % 16) % 16
    near = (turn == 0).astype(np.float32) + (turn == 1) + (turn == 15)
    c[:, C_BIAS:C_MASK_A] = np.where(same, near, np.float32(-1e30))
    head = np.repeat(np.arange(8), HD)
    c[:, C_MASK_A:C_MASK_B] = p[:, None] // 64 == head[None, :] % 2
    c[:, C_MASK_B:C_EXPERT] = p[:, None] // 32 == head[None, :] % 4
    c[:, C_EXPERT:C_BASE] = np.arange(EXPERTS)
    c[:, C_BASE:C_STEP] = np.arange(EXPERTS) * REGION
    c[:, C_STEP:C_ROOT] = np.arange(STEPS)
    c[:, C_ROOT] = -0.5
    return c


class Signal:

    def __init__(self, sem, per=1):
        self.sem, self.per = sem, per

    def start(self, eng):
        eng.sem_inc(self.sem, 2 * self.per)

    def wait(self, eng, n, part=None):
        eng.wait_ge(self.sem, n * self.per + (2 * self.per + (self.per if part is None else part)))

    def before(self, eng, n, back):
        eng.wait_ge(self.sem, n * self.per + (3 - back) * self.per)


class Chain:

    def __init__(self, sem, eng, per):
        self.sem, self.eng, self.per = sem, eng, per
        self.count = 0

    def item(self, n):
        self.n, self.count = n, 0

    def link(self, ins):
        ins.then_inc(self.sem, 1)
        self.count += 1
        self.eng.wait_ge(self.sem, self.n * self.per + self.count)

    def close(self):
        assert self.count == self.per, (self.count, self.per)


def settle(k, eng):
    eng.sem_inc(k.idle, 1)


def emptied(eng, sem, n, s, per):
    if s >= 2:
        eng.wait_ge(sem, (n - s % 2) * (per // 2))


def loop(eng, step, first, unroll, passes, end):
    for t in range(first):
        step(t, t)
    if passes:
        with eng.Fori(0, passes) as i:
            for v in range(unroll):
                step(i * unroll + (first + v), first + v)
    for t in range(first + unroll * passes, end):
        step(t, t)


class Kernel:
    pass


def allocate(nc, ctx):
    k = Kernel()
    k.nc = nc

    def sb(name, shape, dt=F32):
        return ctx.enter_context(nc.sbuf_tensor(name, shape, dt))

    k.idle = ctx.enter_context(nc.semaphore("idle"))
    k.used = []

    def sem(name):
        k.used.append(nc.alloc_semaphore(name))
        return k.used[-1]

    k.sem = sem
    k.bank = [ctx.enter_context(nc.psum_tensor(f"bank{i}", [P, 512], F32)) for i in range(8)]
    k.stream = sb("stream", [P, TILES, D])
    k.const = sb("const", [P, C_END])
    k.ident = k.const[:, C_IDENT:C_UPPER]
    k.upper = sb("upper", [P, P], BF16)
    k.ones = sb("ones", [P, P], BF16)
    k.zeros = sb("zeros", [P, D])
    k.table = sb("table", [1, STEPS, 2], I32)
    k.split = sb("split", [P, 5, 2, D], F32R)
    k.wv = [sb("wv_a", [P, D]), sb("wv_b", [P, D])]
    k.wout = sb("wout", [P, D])
    k.wr = sb("wr", [P, EXPERTS])
    k.cols = sb("cols", [P, 5])
    k.rows = sb("rows", [P, 3, D])
    k.wgu = sb("wgu", [P, EXPERTS, 2, 2, HIDDEN], F32R)
    k.wd = sb("wd", [P, EXPERTS, CHUNKS, D])
    k.norm_x = [sb(f"norm_x{u}", [P, BATCH, D]) for u in range(2)]
    k.stats = [sb(f"stats{u}", [P, BATCH, 6]) for u in range(2)]
    k.moments = [sb(f"moments{u}", [P, BATCH, 2]) for u in range(2)]
    k.rstd = [sb(f"rstd{u}", [P, BATCH]) for u in range(2)]
    k.xT = [sb(f"xT{u}", [P, TB]) for u in range(2)]
    return k


def setup(k, d):
    nc = k.nc
    loaded, staged, split_hi, split_lo = (k.sem(f"setup_{x}") for x in ("loaded", "staged", "hi", "lo"))
    stage_sem = [k.sem(f"setup_stage{u}") for u in range(2)]
    with ExitStack() as ctx:
        stage = ctx.enter_context(nc.sbuf_tensor("stage", [P, 2, 2, HIDDEN], F32))
        raw = ctx.enter_context(nc.sbuf_tensor("raw", [P, 5, D], F32))
        block = ctx.enter_context(nc.Block())
        fixed = [(k.const[:, :], d.const[:, :]), (raw[:, :, :], d.w_split.rearrange("w c f -> c w f")),
                 (k.wv[0][:, :], d.wv[0]), (k.wv[1][:, :], d.wv[1]), (k.wout[:, :], d.wout),
                 (k.wr[:, :], d.wr), (k.cols[:, :], d.cols),
                 (k.stream[:, :, :], d.x.rearrange("(t p) c -> p t c", p=P)),
                 (k.wd[:, :, :, :], d.wd.rearrange("e (j p) c -> p e j c", p=P))]

        @block.sync
        def _(sp):
            for dst, src in fixed:
                sp.dma_start(dst, src).then_inc(loaded, 16)
            for r in range(3):
                sp.dma_start(k.rows[:, r, :], d.rows[r:r + 1, :].to_broadcast([P, D])).then_inc(loaded, 16)
            for e in range(EXPERTS):
                if e >= 2:
                    sp.wait_ge(split_lo, e - 1)
                for j, w in enumerate((d.wg, d.wu)):
                    sp.dma_start(stage[:, e % 2, j, :], w[e, :, :]).then_inc(stage_sem[e % 2], 16)
            sp.wait_ge(staged, 1)
            for j in range(SPARE):
                sp.dma_start(d.routed[EXPERTS * REGION + j * P:EXPERTS * REGION + (j + 1) * P, :],
                             k.zeros[:, :]).then_inc(loaded, 16)
            sp.wait_ge(loaded, 16 * (len(fixed) + 3 + SPARE))

        @block.vector
        def _(dve):
            nc.vector.memset(k.ones[:, :], 1.0)
            nc.vector.memset(k.zeros[:, :], 0.0).then_inc(staged, 1)
            dve.wait_ge(loaded, 16 * (len(fixed) + 3))
            nc.vector.tensor_copy(k.upper[:, :], k.const[:, C_UPPER:C_BIAS])
            nc.vector.tensor_copy(k.split[:, :, 0, :], raw[:, :, :]).then_inc(staged, 1)
            dve.wait_ge(staged, 2)
            nc.vector.tensor_tensor(k.split[:, :, 1, :], raw[:, :, :], k.split[:, :, 0, :].bitcast(F32), ALU.subtract)
            for e in range(EXPERTS):
                dve.wait_ge(split_hi, e + 1)
                nc.vector.tensor_tensor(k.wgu[:, e, :, 1, :], stage[:, e % 2, :, :],
                                        k.wgu[:, e, :, 0, :].bitcast(F32), ALU.subtract).then_inc(split_lo, 1)

        @block.scalar
        def _(act):
            for e in range(EXPERTS):
                act.wait_ge(stage_sem[e % 2], 32 * (e // 2 + 1))
                nc.scalar.activation(k.wgu[:, e, :, 0, :], stage[:, e % 2, :, :], ACT.Copy).then_inc(split_hi, 1)


def normalise(k, chain, n, u, src, moments, rooted, ready, free=None):
    nc = k.nc
    for t in range(BATCH):
        last = nc.vector.bn_stats(k.stats[u][:, t, :], src[:, bass.ds(n * BATCH + t, 1), :].rearrange("p a c -> p (a c)"))
    chain.link(last)
    settle(k, chain.eng)
    for t in range(BATCH):
        last = nc.vector.bn_aggr(k.moments[u][:, t, :], k.stats[u][:, t, :])
    last.then_inc(moments.sem, 1)
    rooted.wait(chain.eng, n)
    if free:
        free()
    for t in range(BATCH):
        last = nc.vector.tensor_scalar(
            k.norm_x[u][:, t, :], src[:, bass.ds(n * BATCH + t, 1), :].rearrange("p a c -> p (a c)"),
            k.moments[u][:, t, 0:1], k.rstd[u][:, t:t + 1], ALU.subtract, ALU.mult)
    last.then_inc(ready.sem, 1)


def root_of_variance(k, pool, n, u, moments, rooted):
    moments.wait(pool, n)
    settle(k, pool)
    k.nc.gpsimd.tensor_scalar(k.rstd[u][:, :], k.moments[u][:, :, 1], EPS, None, ALU.add).then_inc(rooted.sem, 1)
    rooted.wait(pool, n, 1)
    k.nc.gpsimd.tensor_tensor(k.rstd[u][:, :], k.rstd[u][:, :], k.const[:, C_ROOT:C_END].to_broadcast([P, BATCH]), ALU.pow).then_inc(rooted.sem, 1)


def project(k, d, half):
    nc = k.nc
    tag = "ab"[half]
    second = half == 1
    W = [2, 3, 4] if second else [None, 0, 1]
    sem = lambda name, per=1: Signal(k.sem(f"proj_{tag}_{name}"), per)
    normed, turned, copied, high, low = (sem(x) for x in ("normed", "turned", "copied", "high", "low"))
    torus, torus_copied, torus_high, torus_low = (sem(x) for x in ("torus", "torus_copied", "torus_high", "torus_low"))
    moments, rooted = sem("moments"), sem("rooted", 2)
    q_ready, k_ready, v_ready = sem("q"), sem("k"), sem("v")
    q_out, k_out, v_out = sem("q_out"), sem("k_out"), sem("v_out")
    part0, rest1, part1, part2 = sem("part0"), sem("rest1"), sem("part1"), sem("part2")
    stored = [k.sem(f"proj_{tag}_stored{u}") for u in range(2)]
    chain_sem = k.sem(f"proj_{tag}_chain")
    stores = 7
    psT = [k.bank[0], k.bank[1]]
    psq, psk, psv, pst = k.bank[2], k.bank[3], k.bank[4], k.bank[5]
    with ExitStack() as ctx:
        sb = lambda name, shape, dt=F32: ctx.enter_context(nc.sbuf_tensor(f"proj_{tag}_{name}", shape, dt))
        hi = [sb(f"hi{u}", [P, TB], F32R) for u in range(2)]
        lo = [sb(f"lo{u}", [P, TB], F32R) for u in range(2)]
        xt = [sb(f"xt{u}", [P, TB]) for u in range(2)] if second else k.xT
        qk = [sb(f"qk{u}", [P, 2, TB]) for u in range(2)]
        parts = [sb(f"parts{u}", [P, 3, 2, TB], BF16) for u in range(2)]
        v = [sb(f"v{u}", [P, BATCH, D]) for u in range(2)]
        block = ctx.enter_context(nc.Block())
        final_copied, final_high, final_low = (torus_copied, torus_high, torus_low) if second else (copied, high, low)

        def three(out, w, u, first=True):
            for j, (a, b) in enumerate(((0, hi), (1, hi), (0, lo))):
                last = nc.tensor.matmul(out[:, :], k.split[:, w, a, :], b[u][:, :], start=j == 0, stop=j == 2)
            return last

        @block.sync
        def _(sp):
            def step(n, s):
                u = s % 2
                part2.wait(sp, n)
                at = bass.ds(n * TB, TB)
                for j, (slot, many) in enumerate(((0, 3), (3, 2), (5, 1))):
                    sp.dma_start(d.stack[0, :, slot:slot + many, at],
                                 parts[u][:, j:j + 1, 0, :].to_broadcast([P, many, TB])).then_inc(stored[u], 16)
                    sp.dma_start(d.stack[1, :, slot:slot + many, at], parts[u][:, 0:many, 1, :]).then_inc(stored[u], 16)
                v_out.wait(sp, n)
                sp.dma_start(d.v[at, :].rearrange("(t p) c -> p t c", p=P), v[u][:, :, :]).then_inc(stored[u], 16)

            loop(sp, step, 0, 2, BATCHES // 2, BATCHES)
            for u in range(2):
                sp.wait_ge(stored[u], 16 * stores * BATCHES // 2)

        @block.vector
        def _(dve):
            chain = Chain(chain_sem, dve, 1)
            for x in (moments, normed, high, torus_high, q_out, part0):
                x.start(dve)

            def step(n, s):
                u = s % 2
                chain.item(n)
                normalise(k, chain, n, u, k.stream, moments, rooted, normed, lambda: turned.before(dve, n, 2))
                chain.close()
                copied.wait(dve, n)
                q_ready.before(dve, n, 2)
                k_ready.before(dve, n, 2)
                nc.vector.tensor_copy(hi[u][:, :], k.xT[u][:, :]).then_inc(high.sem, 1)
                if second:
                    torus.wait(dve, n)
                    torus_copied.wait(dve, n)
                    low.wait(dve, n)
                    nc.vector.tensor_copy(hi[u][:, :], xt[u][:, :]).then_inc(torus_high.sem, 1)
                q_ready.wait(dve, n)
                rest1.before(dve, n, 2)
                part0.before(dve, n, 1)
                nc.vector.tensor_scalar(qk[u][:, 0, :], psq[:, :], k.cols[:, W[1]:W[1] + 1], SCALE,
                                        ALU.add, ALU.mult).then_inc(q_out.sem, 1)
                k_out.wait(dve, n)
                q_out.wait(dve, n)
                emptied(dve, stored[u], n, s, 16 * stores)
                nc.vector.tensor_copy(parts[u][:, 0, :, :], qk[u][:, :, :]).then_inc(part0.sem, 1)

            loop(dve, step, 2, 2, BATCHES // 2 - 1, BATCHES)

        @block.scalar
        def _(act):
            for x in (copied, torus_copied, k_out, v_out, part1):
                x.start(act)

            def step(n, s):
                u = s % 2
                turned.wait(act, n)
                low.before(act, n, 2)
                v_ready.before(act, n, 2)
                nc.scalar.activation(k.xT[u][:, :], psT[u][:, :], ACT.Copy).then_inc(copied.sem, 1)
                if second:
                    torus.wait(act, n)
                    torus_low.before(act, n, 2)
                    nc.scalar.activation(xt[u][:, :], pst[:, :], ACT.Identity, bias=k.cols[:, W[0]:W[0] + 1])\
                        .then_inc(torus_copied.sem, 1)
                k_ready.wait(act, n)
                part0.before(act, n, 2)
                rest1.before(act, n, 2)
                nc.scalar.activation(qk[u][:, 1, :], psk[:, :], ACT.Identity, bias=k.cols[:, W[2]:W[2] + 1])\
                    .then_inc(k_out.sem, 1)
                v_ready.wait(act, n)
                emptied(act, stored[u], n, s, 16 * stores)
                nc.scalar.activation(v[u][:, :, :].rearrange("p t c -> p (t c)"), psv[:, :], ACT.Copy).then_inc(v_out.sem, 1)
                rest1.wait(act, n)
                nc.scalar.activation(parts[u][:, 1, :, :], qk[u][:, :, :], ACT.Copy).then_inc(part1.sem, 1)

            loop(act, step, 2, 2, BATCHES // 2 - 1, BATCHES)

        @block.gpsimd
        def _(pool):
            for x in (rooted, low, torus_low, rest1, part2):
                x.start(pool)

            def step(n, s):
                u = s % 2
                root_of_variance(k, pool, n, u, moments, rooted)
                high.wait(pool, n)
                q_ready.before(pool, n, 2)
                k_ready.before(pool, n, 2)
                nc.gpsimd.tensor_tensor(lo[u][:, :], k.xT[u][:, :], hi[u][:, :].bitcast(F32), ALU.subtract).then_inc(low.sem, 1)
                if second:
                    torus_high.wait(pool, n)
                    nc.gpsimd.tensor_tensor(lo[u][:, :], xt[u][:, :], hi[u][:, :].bitcast(F32), ALU.subtract)\
                        .then_inc(torus_low.sem, 1)
                part0.wait(pool, n)
                nc.gpsimd.tensor_tensor(qk[u][:, :, :], qk[u][:, :, :], parts[u][:, 0, :, :], ALU.subtract).then_inc(rest1.sem, 1)
                part1.wait(pool, n)
                nc.gpsimd.tensor_tensor(parts[u][:, 2, :, :], qk[u][:, :, :], parts[u][:, 1, :, :], ALU.subtract).then_inc(part2.sem, 1)

            loop(pool, step, 0, 2, BATCHES // 2, BATCHES)

        @block.tensor
        def _(pe):
            for x in (turned, torus, q_ready, k_ready, v_ready):
                x.start(pe)

            def step(n, s):
                u = s % 2
                normed.wait(pe, n)
                copied.before(pe, n, 2)
                for t in range(BATCH):
                    last = nc.tensor.transpose(psT[u][:, t * P:(t + 1) * P], k.norm_x[u][:, t, :], k.ident)
                last.then_inc(turned.sem, 1)
                low.wait(pe, n)
                high.wait(pe, n)
                if second:
                    torus_copied.before(pe, n, 1)
                    three(pst, W[0], u).then_inc(torus.sem, 1)
                    torus_high.wait(pe, n)
                    torus_low.wait(pe, n)
                q_out.before(pe, n, 1)
                three(psq, W[1], u).then_inc(q_ready.sem, 1)
                k_out.before(pe, n, 1)
                three(psk, W[2], u).then_inc(k_ready.sem, 1)
                final_copied.wait(pe, n)
                v_out.before(pe, n, 1)
                for t in range(BATCH):
                    last = nc.tensor.matmul(psv[:, t * D:(t + 1) * D], xt[u][:, t * P:(t + 1) * P],
                                            k.wv[half][:, :], start=True, stop=True)
                last.then_inc(v_ready.sem, 1)

            loop(pe, step, 0, 2, BATCHES // 2, BATCHES)


def attend(k, d, half):
    nc = k.nc
    tag = "ab"[half]
    second = half == 1
    blk = 32 if second else 64
    nb = P // blk
    group = P // blk
    rounds = HEADS // 2
    turns = HEADS // group
    width = HEADS * blk
    sem = lambda name, per=1: Signal(k.sem(f"att_{tag}_{name}"), per)
    scored, shifted, risen = sem("scored"), sem("shifted"), sem("risen")
    turned, turned_copied = sem("turned"), sem("turned_copied", 2)
    values, mixed, even, summed, based = sem("values"), sem("mixed"), sem("even"), sem("summed"), sem("based")
    back, back_copied, mapped, mapped_added = sem("back"), sem("back_copied"), sem("mapped"), sem("mapped_added")
    loaded = [k.sem(f"att_{tag}_loaded{u}") for u in range(2)]
    chain_sem = k.sem(f"att_{tag}_chain")
    pool_sem = k.sem(f"att_{tag}_pool")
    loads = 4 + group
    psS = [k.bank[2 * u:2 * u + 2] for u in range(2)]
    psP = k.bank[4:6]
    psO, psE = k.bank[6], k.bank[7]
    mask = k.const[:, C_MASK_B:C_EXPERT] if second else k.const[:, C_MASK_A:C_MASK_B]
    with ExitStack() as ctx:
        sb = lambda name, shape, dt=F32: ctx.enter_context(nc.sbuf_tensor(f"att_{tag}_{name}", shape, dt))
        qs = [sb(f"q{m}", [P, rounds, PAIR], BF16) for m in range(2)]
        ks = [sb(f"k{m}", [P, rounds, PAIR], BF16) for m in range(2)]
        vd = [sb(f"v{m}", [P, 2 * nb, D]) for m in range(2)]
        vx = [sb(f"vx{u}", [P, nb, 2, rounds, HD + 1]) for u in range(2)]
        prob = [sb(f"prob{u}", [P, HEADS, blk]) for u in range(2)]
        probT = [sb(f"probT{u}", [P, turns, P]) for u in range(2)]
        most = [sb(f"most{u}", [P, HEADS]) for u in range(2)]
        inv = [sb(f"inv{u}", [P, HEADS]) for u in range(2)]
        mix = [sb(f"mix{u}", [P, D]) for u in range(2)]
        base = [sb(f"base{u}", [P, D]) for u in range(2)]
        mixT = [sb(f"mixT{u}", [P, P]) for u in range(2)]
        block = ctx.enter_context(nc.Block())

        def scores(u, a):
            return psS[u][a][:, 0:rounds * blk].rearrange("p (h c) -> p h c", c=blk)

        @block.sync
        def _(sp):
            def step(m, s):
                v = s % 2
                if isinstance(m, int) and m < 2:
                    pass
                else:
                    sp.wait_ge(scored.sem, m * 2 + (2 * 1 - 2))
                    sp.wait_ge(values.sem, m * 2 + (2 * 1 - 2))
                at = bass.ds(m * PAIR, PAIR)
                for side, to in ((0, qs), (1, ks)):
                    for a in range(2):
                        src = d.stack[side, :, :, at].rearrange("(h a e) s t -> a (e s) h t", a=2, e=HD)
                        sp.dma_start(to[v][64 * a:64 * a + STACK, :, :], src[a]).then_inc(loaded[v], 16)
                for g in range(group):
                    src = d.v[at, :].rearrange("(b q) c -> q b c", q=blk)
                    sp.dma_start(vd[v][blk * g:blk * (g + 1), :, :], src).then_inc(loaded[v], 16)

            loop(sp, step, 2, 2, (TILES // 2 - 2) // 2, TILES // 2)

        def pair_loaded(eng, n, s):
            eng.wait_ge(loaded[s // 2 % 2], (n - s % 4) * (4 * loads) + 16 * loads)

        @block.gpsimd
        def _(pool):
            for x in (values, summed, based):
                x.start(pool)
            for u in range(2):
                for a in range(2):
                    for b in range(nb):
                        nc.gpsimd.tensor_copy(vx[u][:, b, a, :, HD],
                                              mask.rearrange("p (h e) -> p h e", e=HD)[:, :, 0])
            chain = Chain(pool_sem, pool, 1)

            def step(n, s):
                if s < TILES:
                    pair_loaded(pool, n, s)
                    mixed.before(pool, n, 2)
                    for a in range(2):
                        for b in range(nb):
                            vb = vd[s // 2 % 2][:, (s % 2) * nb + b, :].rearrange("p (h a e) -> p a h e", a=2, e=HD)
                            last = nc.gpsimd.tensor_tensor(vx[s % 2][:, b, a, :, 0:HD], vb[:, a],
                                                           mask.rearrange("p (h e) -> p h e", e=HD), ALU.mult)
                    last.then_inc(values.sem, 1)
                if s >= 2 and s - 2 < TILES:
                    m, u = n - 2, s % 2
                    tile = k.stream[:, bass.ds(m, 1), :].rearrange("p a c -> p (a c)")
                    even.wait(pool, m)
                    if second:
                        back.before(pool, m, 2)
                        nc.gpsimd.tensor_tensor(mix[u][:, :], mix[u][:, :], k.rows[:, 1, :], ALU.add).then_inc(summed.sem, 1)
                        mapped_added.before(pool, m, 2)
                        settle(k, pool)
                        nc.gpsimd.tensor_tensor(base[u][:, :], tile, k.rows[:, 2, :], ALU.add).then_inc(based.sem, 1)
                    else:
                        chain.item(m)
                        settle(k, pool)
                        chain.link(nc.gpsimd.tensor_tensor(base[u][:, :], tile, k.rows[:, 0, :], ALU.add))
                        settle(k, pool)
                        nc.gpsimd.tensor_tensor(tile, mix[u][:, :], base[u][:, :], ALU.add).then_inc(summed.sem, 1)

            loop(pool, step, 4, 4, (TILES - 4) // 4, TILES + 2)

        @block.tensor
        def _(pe):
            for x in (scored, turned, mixed, back, mapped):
                x.start(pe)

            def score(n, s):
                pair_loaded(pe, n, s)
                shifted.before(pe, n, 2)
                settle(k, pe)
                u, v = s % 2, s // 2 % 2
                for h in range(rounds):
                    for a in range(2):
                        for b in range(nb):
                            at = slice((s % 2) * P + b * blk, (s % 2) * P + (b + 1) * blk)
                            rows = slice(64 * a, 64 * a + STACK)
                            last = nc.tensor.matmul(psS[u][a][b * blk:(b + 1) * blk, h * blk:(h + 1) * blk],
                                                    qs[v][rows, h, at], ks[v][rows, h, at], start=True, stop=True,
                                                    tile_position=(64 * a, b * blk))
                last.then_inc(scored.sem, 1)

            def mixing(n, s):
                u = s % 2
                turned_copied.wait(pe, n)
                values.wait(pe, n)
                even.before(pe, n, 1)
                flat = lambda b, i: vx[u][:, b, :, :, :].rearrange("p a h e -> p (a h e)")[
                    :, i * group * (HD + 1):(i + 1) * group * (HD + 1)]
                for b in range(nb):
                    for i in range(turns):
                        last = nc.tensor.matmul(psO[b * blk:(b + 1) * blk, i * group * (HD + 1):(i + 1) * group * (HD + 1)],
                                                probT[u][:, i, b * blk:(b + 1) * blk], flat(b, i), start=True, stop=True,
                                                tile_position=(0, b * blk))
                last.then_inc(mixed.sem, 1)

            def turn(n, s):
                u = s % 2
                risen.wait(pe, n)
                turned_copied.before(pe, n, 1)
                for i in range(turns):
                    last = nc.tensor.transpose(psP[i // 4][:, (i % 4) * P:(i % 4 + 1) * P],
                                               prob[u][:, i * group:(i + 1) * group, :].rearrange("p h c -> p (h c)"), k.ident)
                last.then_inc(turned.sem, 1)

            def turn_back(n, s):
                summed.wait(pe, n)
                back_copied.before(pe, n, 1)
                mapped_added.before(pe, n, 1)
                nc.tensor.transpose(psE[:, 0:P], mix[s % 2][:, :], k.ident).then_inc(back.sem, 1)

            def map_out(n, s):
                back_copied.wait(pe, n)
                nc.tensor.matmul(psE[:, P:2 * P], mixT[s % 2][:, :], k.wout[:, :], start=True, stop=True).then_inc(mapped.sem, 1)

            def step(n, s):
                if s < TILES:
                    score(n, s)
                if second and 3 <= s < TILES + 3:
                    turn_back(n - 3, s - 3)
                if 2 <= s < TILES + 2:
                    mixing(n - 2, s - 2)
                if 1 <= s < TILES + 1:
                    turn(n - 1, s - 1)
                if second and 3 <= s < TILES + 3:
                    map_out(n - 3, s - 3)

            loop(pe, step, 4, 4, (TILES - 4) // 4, TILES + 3)

        @block.vector
        def _(dve):
            for x in (shifted, even, mapped_added):
                x.start(dve)
            chain = Chain(chain_sem, dve, 3 if second else 2)
            bias = k.const[:, C_BIAS:C_MASK_A].unsqueeze(1).to_broadcast([P, rounds, blk]) if second else None

            def soften(n, s):
                u = s % 2
                chain.item(n)
                scored.wait(dve, n)
                if second:
                    turned.before(dve, n, 2)
                    for a in range(2):
                        last = nc.vector.tensor_tensor(prob[u][:, a * rounds:(a + 1) * rounds, :], scores(u, a), bias, ALU.add)
                    chain.link(last)
                    chain.link(nc.vector.tensor_reduce(most[u][:, :], prob[u][:, :, :], X, ALU.max))
                    nc.vector.tensor_tensor(prob[u][:, :, :], prob[u][:, :, :],
                                            most[u][:, :].unsqueeze(2).to_broadcast([P, HEADS, blk]), ALU.subtract)\
                        .then_inc(shifted.sem, 1)
                else:
                    for a in range(2):
                        last = nc.vector.tensor_reduce(most[u][:, a * rounds:(a + 1) * rounds], scores(u, a), X, ALU.max)
                    chain.link(last)
                    turned.before(dve, n, 2)
                    for a in range(2):
                        last = nc.vector.tensor_tensor(
                            prob[u][:, a * rounds:(a + 1) * rounds, :], scores(u, a),
                            most[u][:, a * rounds:(a + 1) * rounds].unsqueeze(2).to_broadcast([P, rounds, blk]), ALU.subtract)
                    last.then_inc(shifted.sem, 1)

            def divide(n, s):
                u = s % 2
                mixed.wait(dve, n)
                out = psO[:, 0:HEADS * (HD + 1)].rearrange("p (a h e) -> p a h e", a=2, e=HD + 1)
                chain.link(nc.vector.reciprocal(inv[u][:, :].rearrange("p (a h) -> p a h", a=2), out[:, :, :, HD]))
                if second:
                    back.before(dve, n, 2)
                else:
                    summed.before(dve, n, 2)
                for a in range(2):
                    last = nc.vector.tensor_tensor(
                        mix[u][:, :].rearrange("p (h a e) -> p a h e", a=2, e=HD)[:, a], out[:, a, :, 0:HD],
                        inv[u][:, a * rounds:(a + 1) * rounds].unsqueeze(2).to_broadcast([P, rounds, HD]), ALU.mult)
                last.then_inc(even.sem, 1)

            def add_map(n, s):
                mapped.wait(dve, n)
                based.wait(dve, n)
                nc.vector.tensor_tensor(k.stream[:, bass.ds(n, 1), :].rearrange("p a c -> p (a c)"), psE[:, P:2 * P],
                                        base[s % 2][:, :], ALU.add).then_inc(mapped_added.sem, 1)

            def step(n, s):
                if s < TILES:
                    soften(n, s)
                if s >= TILES:
                    chain.item(n)
                if 2 <= s < TILES + 2:
                    divide(n - 2, s - 2)
                for _ in range(chain.per - chain.count):
                    dve.sem_inc(chain_sem, 1)
                if second and 3 <= s < TILES + 3:
                    add_map(n - 3, s - 3)

            loop(dve, step, 4, 4, (TILES - 4) // 4, TILES + 3)

        @block.scalar
        def _(act):
            for x in (risen, turned_copied, back_copied):
                x.start(act)

            def step(n, s):
                if s < TILES:
                    shifted.wait(act, n)
                    nc.scalar.activation(prob[s % 2][:, :, :], prob[s % 2][:, :, :], ACT.Exp).then_inc(risen.sem, 1)
                if second and 3 <= s < TILES + 3:
                    m, u = n - 3, (s - 3) % 2
                    back.wait(act, m)
                    nc.scalar.activation(mixT[u][:, :], psE[:, 0:P], ACT.Copy).then_inc(back_copied.sem, 1)
                if 1 <= s < TILES + 1:
                    m, u = n - 1, (s - 1) % 2
                    turned.wait(act, m)
                    mixed.before(act, m, 2)
                    half_turns = turns // 2
                    for j in range(2):
                        b, c = (j, 0) if turns == 8 else (0, j * half_turns * P)
                        nc.scalar.activation(probT[u][:, j * half_turns:(j + 1) * half_turns, :].rearrange("p i t -> p (i t)"),
                                             psP[b][:, c:c + half_turns * P], ACT.Copy).then_inc(turned_copied.sem, 1)

            loop(act, step, 4, 4, (TILES - 4) // 4, TILES + 3)


def route(k, d, layer):
    nc = k.nc
    tag = "ab"[layer]
    sem = lambda name, per=1: Signal(k.sem(f"route_{tag}_{name}"), per)
    normed, turned, copied, moments, rooted = sem("normed"), sem("turned"), sem("copied"), sem("moments"), sem("rooted", 2)
    logits, gap, risen, picked, ranked, placed, read = (sem(x) for x in ("logits", "gap", "risen", "picked", "ranked", "placed", "read"))
    sent = [k.sem(f"route_{tag}_sent{u}") for u in range(2)]
    kept = [k.sem(f"route_{tag}_kept{u}") for u in range(2)]
    chain_sem, table_sem, totals, tails, settled = (
        k.sem(f"route_{tag}_{x}") for x in ("chain", "table", "totals", "tails", "settled"))
    per_batch = TOPK * BATCH
    psT = [k.bank[0], k.bank[1]]
    psL, psR, psC = k.bank[2], k.bank[3], k.bank[4]
    with ExitStack() as ctx:
        sb = lambda name, shape, dt=F32: ctx.enter_context(nc.sbuf_tensor(f"route_{tag}_{name}", shape, dt))
        logit = [sb(f"logit{u}", [P, BATCH, EXPERTS]) for u in range(2)]
        top = [sb(f"top{u}", [P, BATCH, 8]) for u in range(2)]
        index = [sb(f"index{u}", [P, BATCH, 8], U32) for u in range(2)]
        less = [sb(f"less{u}", [P, BATCH]) for u in range(2)]
        rise = [sb(f"rise{u}", [P, BATCH]) for u in range(2)]
        total = [sb(f"total{u}", [P, BATCH]) for u in range(2)]
        hot = [sb(f"hot{u}", [P, BATCH, TOPK, EXPERTS]) for u in range(2)]
        both = [sb(f"both{u}", [P, BATCH, EXPERTS], BF16) for u in range(2)]
        seen = [sb(f"seen{u}", [P, EXPERTS], BF16) for u in range(2)]
        four = [sb(f"four{u}", [P, EXPERTS]) for u in range(2)]
        rank = [sb(f"rank{u}", [P, BATCH, EXPERTS]) for u in range(2)]
        spot = [sb(f"spot{u}", [P, BATCH, TOPK, EXPERTS]) for u in range(2)]
        record = [sb(f"record{u}", [P, BATCH, 6]) for u in range(2)]
        place = [sb(f"place{u}", [P, BATCH, TOPK], U32) for u in range(2)]
        records = sb("records", [P, TILES, 6])
        hots = sb("hots", [P, TILES * TOPK, EXPERTS])
        moves = sb("moves", [P, TILES * TOPK])
        count_i = sb("count_i", [P, EXPERTS], I32)
        tiles_i = sb("tiles_i", [P, EXPERTS], I32)
        tiles_f = sb("tiles_f", [P, EXPERTS])
        upto = sb("upto", [P, EXPERTS])
        shift = sb("shift", [P, EXPERTS])
        past = sb("past", [1, STEPS, EXPERTS])
        jump = sb("jump", [P, EXPERTS])
        far = sb("far", [1, STEPS, EXPERTS])
        row_f = sb("row_f", [1, STEPS])
        expert_f = sb("expert_f", [1, STEPS])
        block = ctx.enter_context(nc.Block())

        @block.sync
        def _(sp):
            def step(n, s):
                u = s % 2
                at = bass.ds(n * TB, TB)
                sp.dma_start(d.kept[at, :].rearrange("(t p) c -> p t c", p=P),
                             k.stream[:, bass.ds(n * BATCH, BATCH), :]).then_inc(kept[u], 16)

            loop(sp, step, 0, 2, BATCHES // 2, BATCHES)
            sp.wait_ge(table_sem, 1)
            for e in range(EXPERTS):
                end = sp.value_load(count_i[0:1, e:e + 1], min_val=0, max_val=TOKENS)
                sp.dma_start(d.routed[bass.ds(end + e * REGION, P), :], k.zeros[:, :]).then_inc(tails, 16)
            sp.wait_ge(settled, 1)
            sp.dma_start(d.route.rearrange("(t p) c -> p t c", p=P), records[:, :, 0:4]).then_inc(tails, 16)
            sp.wait_ge(tails, 16 * (EXPERTS + 1))
            for u in range(2):
                sp.wait_ge(kept[u], 16 * BATCHES // 2)

        @block.gpsimd
        def _(pool):
            rooted.start(pool)

            def step(n, s):
                u = s % 2
                root_of_variance(k, pool, n, u, moments, rooted)
                if isinstance(n, int) and n == 0:
                    return
                send(n - 1, s - 1)

            def send(n, s):
                u = s % 2
                placed.wait(pool, n)
                settle(k, pool)
                for t in range(BATCH):
                    for j in range(TOPK):
                        pool.indirect_dma_start(
                            d.routed[:, :], bass.IndirectOffsetOnAxis(ap=place[u][:, t, j:j + 1], axis=0),
                            k.norm_x[u][:, t, :], None).then_inc(sent[u], 16)

            loop(pool, step, 2, 2, (BATCHES - 2) // 2, BATCHES)
            send(BATCHES - 1, BATCHES - 1)
            for u in range(2):
                pool.wait_ge(sent[u], 16 * per_batch * BATCHES // 2)

        @block.tensor
        def _(pe):
            for x in (turned, logits, ranked):
                x.start(pe)

            def step(n, s):
                u = s % 2
                normed.wait(pe, n)
                copied.before(pe, n, 2)
                for t in range(BATCH):
                    last = nc.tensor.transpose(psT[u][:, t * P:(t + 1) * P], k.norm_x[u][:, t, :], k.ident)
                last.then_inc(turned.sem, 1)
                copied.wait(pe, n)
                read.before(pe, n, 1)
                for t in range(BATCH):
                    last = nc.tensor.matmul(psL[:, t * EXPERTS:(t + 1) * EXPERTS], k.xT[u][:, t * P:(t + 1) * P],
                                            k.wr[:, :], start=True, stop=True)
                last.then_inc(logits.sem, 1)
                picked.wait(pe, n)
                placed.before(pe, n, 1)
                for t in range(BATCH):
                    out = psR[:, t * EXPERTS:(t + 1) * EXPERTS]
                    nc.tensor.matmul(out, k.upper[:, :], both[u][:, t, :], start=True, stop=False)
                    for e in range(t):
                        nc.tensor.matmul(out, k.ones[:, :], both[u][:, e, :], start=False, stop=False)
                    last = nc.tensor.matmul(out, k.ones[:, :], seen[u][:, :], start=False, stop=True)
                last.then_inc(ranked.sem, 1)

            loop(pe, step, 0, 2, BATCHES // 2, BATCHES)
            placed.wait(pe, BATCHES - 1)
            nc.tensor.matmul(psC[:, 0:EXPERTS], k.ones[:, :], seen[BATCHES % 2][:, :], start=True, stop=True).then_inc(totals, 1)

        @block.scalar
        def _(act):
            for x in (copied, risen):
                x.start(act)

            def step(n, s):
                u = s % 2
                turned.wait(act, n)
                logits.before(act, n, 2)
                nc.scalar.activation(k.xT[u][:, :], psT[u][:, :], ACT.Copy).then_inc(copied.sem, 1)
                gap.wait(act, n)
                placed.before(act, n, 2)
                nc.scalar.activation(rise[u][:, :], less[u][:, :], ACT.Exp).then_inc(risen.sem, 1)

            loop(act, step, 0, 2, BATCHES // 2, BATCHES)

        @block.vector
        def _(dve):
            for x in (moments, normed, gap, read, picked, placed):
                x.start(dve)
            chain = Chain(chain_sem, dve, 12)
            nc.vector.memset(seen[0][:, :], 0.0)
            base = k.const[:, C_BASE:C_STEP]
            number = k.const[:, C_EXPERT:C_BASE]

            def step(n, s):
                u = s % 2
                chain.item(n)
                normalise(k, chain, n, u, k.stream, moments, rooted, normed,
                          lambda: emptied(dve, sent[u], n, s, 16 * per_batch))
                logits.wait(dve, n)
                ins = nc.vector.tensor_copy(logit[u][:, :, :], psL[:, 0:BATCH * EXPERTS].rearrange("p (t e) -> p t e", e=EXPERTS))
                ins.then_inc(read.sem, 1)
                read.wait(dve, n)
                settle(k, dve)
                for t in range(BATCH):
                    last = nc.vector.max(top[u][:, t, :], logit[u][:, t, :])
                chain.link(last)
                settle(k, dve)
                for t in range(BATCH):
                    last = nc.vector.max_index(index[u][:, t, :], top[u][:, t, :], logit[u][:, t, :])
                chain.link(last)
                risen.before(dve, n, 2)
                nc.vector.tensor_tensor(less[u][:, :], top[u][:, :, 1], top[u][:, :, 0], ALU.subtract).then_inc(gap.sem, 1)
                chain.link(nc.vector.tensor_copy(record[u][:, :, 4:6], index[u][:, :, 0:TOPK]))
                chain.link(nc.vector.tensor_tensor(
                    hot[u][:, :, :, :], record[u][:, :, 4:6].unsqueeze(3).to_broadcast([P, BATCH, TOPK, EXPERTS]),
                    number.unsqueeze(1).unsqueeze(1).to_broadcast([P, BATCH, TOPK, EXPERTS]), ALU.is_equal))
                ranked.before(dve, n, 2)
                chain.link(nc.vector.tensor_tensor(both[u][:, :, :], hot[u][:, :, 0, :], hot[u][:, :, 1, :], ALU.add))
                nc.vector.tensor_reduce(four[u][:, :], both[u][:, :, :].rearrange("p t e -> p e t"), X, ALU.add).then_inc(picked.sem, 1)
                risen.wait(dve, n)
                chain.link(nc.vector.tensor_scalar(total[u][:, :], rise[u][:, :], 1.0, None, ALU.add))
                ranked.before(dve, n, 1)
                picked.wait(dve, n)
                nc.vector.tensor_tensor(seen[1 - u][:, :], seen[u][:, :], four[u][:, :], ALU.add)
                chain.link(nc.vector.reciprocal(total[u][:, :], total[u][:, :]))
                chain.link(nc.vector.tensor_scalar(record[u][:, :, 2], total[u][:, :], DEPTH_SCALE, None, ALU.mult))
                nc.vector.tensor_tensor(record[u][:, :, 3], record[u][:, :, 2], rise[u][:, :], ALU.mult)
                ranked.wait(dve, n)
                chain.link(nc.vector.tensor_tensor(
                    rank[u][:, :, :], psR[:, 0:BATCH * EXPERTS].rearrange("p (t e) -> p t e", e=EXPERTS),
                    base.unsqueeze(1).to_broadcast([P, BATCH, EXPERTS]), ALU.add))
                chain.link(nc.vector.tensor_tensor(
                    spot[u][:, :, :, :], hot[u][:, :, :, :],
                    rank[u][:, :, :].unsqueeze(2).to_broadcast([P, BATCH, TOPK, EXPERTS]), ALU.mult))
                chain.link(nc.vector.tensor_reduce(record[u][:, :, 0:TOPK], spot[u][:, :, :, :], X, ALU.add))
                nc.vector.tensor_copy(records[:, bass.ds(n * BATCH, BATCH), :], record[u][:, :, :])
                last = nc.vector.tensor_copy(place[u][:, :, :], record[u][:, :, 0:TOPK])
                last.then_inc(placed.sem, 1)
                chain.close()

            loop(dve, step, 2, 2, BATCHES // 2 - 1, BATCHES)

            links = [0]

            def then(ins):
                ins.then_inc(table_sem, 1)
                links[0] += 1
                dve.wait_ge(table_sem, links[0])

            dve.wait_ge(totals, 1)
            then(nc.vector.tensor_copy(count_i[:, :], psC[:, 0:EXPERTS]))
            then(nc.vector.tensor_scalar(tiles_i[:, :], count_i[:, :], P - 1, None, ALU.add))
            then(nc.vector.tensor_scalar(tiles_i[:, :], tiles_i[:, :], 7, None, ALU.arith_shift_right))
            then(nc.vector.tensor_copy(tiles_f[:, :], tiles_i[:, :]))
            nc.vector.tensor_scalar(jump[:, :], tiles_f[:, :], -float(P), float(REGION), ALU.mult, ALU.add)
            then(nc.vector.tensor_tensor_scan(upto[:, :], tiles_f[:, :], k.zeros[:, 0:EXPERTS], 0.0, ALU.add, ALU.add))
            steps = k.const[0:1, C_STEP:C_ROOT]
            wide = [1, STEPS, EXPERTS]
            then(nc.vector.tensor_tensor(past[:, :, :], steps.unsqueeze(2).to_broadcast(wide),
                                         upto[0:1, :].unsqueeze(1).to_broadcast(wide), ALU.is_ge))
            then(nc.vector.tensor_tensor(far[:, :, :], past[:, :, :], jump[0:1, :].unsqueeze(1).to_broadcast(wide), ALU.mult))
            nc.vector.tensor_reduce(row_f[:, :], far[:, :, :], X, ALU.add)
            then(nc.vector.tensor_reduce(expert_f[:, :], past[:, :, :], X, ALU.add))
            then(nc.vector.scalar_tensor_tensor(row_f[:, :], steps, float(P), row_f[:, :], ALU.mult, ALU.add))
            nc.vector.tensor_copy(k.table[:, :, 0], row_f[:, :])
            nc.vector.tensor_scalar(k.table[:, :, 1], expert_f[:, :], float(EXPERTS - 1), None, ALU.min)
            then(nc.vector.tensor_tensor(shift[:, :], upto[:, :], tiles_f[:, :], ALU.subtract))
            then(nc.vector.scalar_tensor_tensor(shift[:, :], shift[:, :], float(P), base, ALU.mult, ALU.subtract))
            whole = [P, TILES * TOPK, EXPERTS]
            for j in range(TOPK):
                last = nc.vector.tensor_tensor(
                    hots[:, j * TILES:(j + 1) * TILES, :], records[:, :, 4 + j].unsqueeze(2).to_broadcast([P, TILES, EXPERTS]),
                    number.unsqueeze(1).to_broadcast([P, TILES, EXPERTS]), ALU.is_equal)
            then(last)
            then(nc.vector.tensor_tensor(hots[:, :, :], hots[:, :, :], shift[:, :].unsqueeze(1).to_broadcast(whole), ALU.mult))
            then(nc.vector.tensor_reduce(moves[:, :], hots[:, :, :], X, ALU.add))
            for j in range(TOPK):
                last = nc.vector.tensor_tensor(records[:, :, j], records[:, :, j], moves[:, j * TILES:(j + 1) * TILES], ALU.add)
            last.then_inc(settled, 1)


def experts(k, d, layer):
    nc = k.nc
    tag = "ab"[layer]
    sem = lambda name, per=1: Signal(k.sem(f"moe_{tag}_{name}"), per)
    turned, high, low, gated, upped, glowing, hidden = (sem(x) for x in ("turned", "high", "low", "gated", "upped", "glowing", "hidden"))
    crossed, crossed_copied, downed, out_ready = sem("crossed"), sem("crossed_copied"), sem("downed"), sem("out_ready")
    loaded = [k.sem(f"moe_{tag}_loaded{u}") for u in range(2)]
    stored = [k.sem(f"moe_{tag}_stored{u}") for u in range(2)]
    psG, psU = k.bank[0:2], k.bank[2:4]
    psH, psX, psY = k.bank[4], k.bank[5], k.bank[6]
    FIRST, PASSES = 3, (STEPS - 4) // 2
    with ExitStack() as ctx:
        sb = lambda name, shape, dt=F32: ctx.enter_context(nc.sbuf_tensor(f"moe_{tag}_{name}", shape, dt))
        rows = [sb(f"rows{u}", [P, D]) for u in range(2)]
        hi = [sb(f"hi{u}", [P, P], F32R) for u in range(2)]
        lo = [sb(f"lo{u}", [P, P], F32R) for u in range(2)]
        glow = [sb(f"glow{u}", [P, HIDDEN]) for u in range(2)]
        hid = [sb(f"hid{u}", [P, HIDDEN]) for u in range(2)]
        hidT = [sb(f"hidT{u}", [P, HIDDEN]) for u in range(2)]
        out = [sb(f"out{u}", [P, D]) for u in range(2)]
        block = ctx.enter_context(nc.Block())

        @block.sync
        def _(sp):
            def step(n, s):
                u = s % 2
                row = sp.value_load(k.table[0:1, bass.ds(n, 1), 0:1].rearrange("p a c -> p (a c)"), min_val=0, max_val=REGION_ROWS - P)
                if s >= 2:
                    turned.before(sp, n, 2)
                sp.dma_start(rows[u][:, :], d.routed[bass.ds(row, P), :]).then_inc(loaded[u], 16)

            loop(sp, step, FIRST, 2, PASSES, STEPS)

        @block.gpsimd
        def _(pool):
            def step(n, s):
                u = s % 2
                out_ready.wait(pool, n)
                settle(k, pool)
                pool.dma_start(d.expert[bass.ds(n * P, P), :], out[u][:, :]).then_inc(stored[u], 16)

            loop(pool, step, FIRST, 2, PASSES, STEPS)
            for u in range(2):
                pool.wait_ge(stored[u], 16 * STEPS // 2)

        @block.tensor
        def _(pe):
            for x in (turned, gated, upped, crossed, downed):
                x.start(pe)

            def turn(n, s):
                u = s % 2
                pe.wait_ge(loaded[u], (n - s % 2) * 8 + 16)
                low.before(pe, n, 1)
                nc.tensor.transpose(psX[:, 0:P], rows[u][:, :], k.ident).then_inc(turned.sem, 1)

            def up(n, s):
                u = s % 2
                e = pe.value_load(k.table[0:1, bass.ds(n, 1), 1:2].rearrange("p a c -> p (a c)"), min_val=0, max_val=EXPERTS - 1)
                w = lambda j, part: k.wgu[:, bass.ds(e, 1), j, part, :].rearrange("p a c -> p (a c)")
                high.wait(pe, n)
                low.wait(pe, n)
                for j, (ps, free, done) in enumerate(((psG, glowing, gated), (psU, hidden, upped))):
                    free.before(pe, n, 2)
                    for i, (x, part) in enumerate(((hi, 0), (hi, 1), (lo, 0))):
                        last = nc.tensor.matmul(ps[u][:, :], x[u][:, :], w(j, part), start=i == 0, stop=i == 2)
                    last.then_inc(done.sem, 1)

            def cross(n, s):
                u = s % 2
                hidden.wait(pe, n)
                crossed_copied.before(pe, n, 1)
                for c in range(CHUNKS):
                    last = nc.tensor.transpose(psH[:, c * P:(c + 1) * P], hid[u][:, c * P:(c + 1) * P], k.ident)
                last.then_inc(crossed.sem, 1)

            def down(n, s):
                u = s % 2
                e = pe.value_load(k.table[0:1, bass.ds(n, 1), 1:2].rearrange("p a c -> p (a c)"), min_val=0, max_val=EXPERTS - 1)
                crossed_copied.wait(pe, n)
                out_ready.before(pe, n, 1)
                for c in range(CHUNKS):
                    last = nc.tensor.matmul(psY[:, 0:D], hidT[u][:, c * P:(c + 1) * P],
                                            k.wd[:, bass.ds(e, 1), c, :].rearrange("p a c -> p (a c)"),
                                            start=c == 0, stop=c == CHUNKS - 1)
                last.then_inc(downed.sem, 1)

            turn(0, 0)

            def step(n, s):
                if s < STEPS:
                    up(n, s)
                if s >= 1:
                    down(n - 1, s - 1)
                if s + 1 < STEPS:
                    turn(n + 1, s + 1)
                if s < STEPS:
                    cross(n, s)

            loop(pe, step, FIRST, 2, PASSES, STEPS + 1)

        @block.scalar
        def _(act):
            for x in (high, glowing, crossed_copied):
                x.start(act)

            def halve(n, s):
                u = s % 2
                turned.wait(act, n)
                upped.before(act, n, 2)
                nc.scalar.activation(hi[u][:, :], psX[:, 0:P], ACT.Copy).then_inc(high.sem, 1)

            halve(0, 0)

            def step(n, s):
                u = s % 2
                gated.wait(act, n)
                hidden.before(act, n, 2)
                nc.scalar.activation(glow[u][:, :], psG[u][:, :], ACT.Silu).then_inc(glowing.sem, 1)
                if s + 1 < STEPS:
                    halve(n + 1, s + 1)
                crossed.wait(act, n)
                downed.before(act, n, 2)
                nc.scalar.activation(hidT[u][:, :], psH[:, :], ACT.Copy).then_inc(crossed_copied.sem, 1)

            loop(act, step, FIRST, 2, PASSES, STEPS)

        @block.vector
        def _(dve):
            for x in (low, hidden, out_ready):
                x.start(dve)

            def halve(n, s):
                u = s % 2
                high.wait(dve, n)
                upped.before(dve, n, 2)
                nc.vector.tensor_tensor(lo[u][:, :], psX[:, 0:P], hi[u][:, :].bitcast(F32), ALU.subtract).then_inc(low.sem, 1)

            def give(n, s):
                u = s % 2
                downed.wait(dve, n)
                emptied(dve, stored[u], n, s, 16)
                nc.vector.tensor_copy(out[u][:, :], psY[:, 0:D]).then_inc(out_ready.sem, 1)

            halve(0, 0)

            def step(n, s):
                u = s % 2
                if s < STEPS:
                    upped.wait(dve, n)
                    glowing.wait(dve, n)
                    crossed.before(dve, n, 2)
                    nc.vector.tensor_tensor(hid[u][:, :], psU[u][:, :], glow[u][:, :], ALU.mult).then_inc(hidden.sem, 1)
                if s + 1 < STEPS:
                    halve(n + 1, s + 1)
                if s >= 1:
                    give(n - 1, s - 1)

            loop(dve, step, FIRST, 2, PASSES, STEPS + 1)


def combine(k, d, layer):
    nc = k.nc
    tag = "ab"[layer]
    last_layer = layer == 1
    sem = lambda name, per=1: Signal(k.sem(f"join_{tag}_{name}"), per)
    placed, first, joined = sem("placed"), sem("first"), sem("joined")
    loaded = [k.sem(f"join_{tag}_loaded{u}") for u in range(4)]
    fetched = [k.sem(f"join_{tag}_fetched{u}") for u in range(4)]
    stored = [k.sem(f"join_{tag}_stored{u}") for u in range(4)]
    by_position = lambda ap, n: ap.rearrange("(s b) c -> b s c", s=ROWS)[bass.ds(n * (P // ROWS), P // ROWS), :, :]
    with ExitStack() as ctx:
        sb = lambda name, shape, dt=F32: ctx.enter_context(nc.sbuf_tensor(f"join_{tag}_{name}", shape, dt))
        kept = [sb(f"kept{u}", [P, D]) for u in range(4)]
        record = [sb(f"record{u}", [P, 4]) for u in range(4)]
        place = [sb(f"place{u}", [P, TOPK], U32) for u in range(4)]
        got = [sb(f"got{u}", [P, TOPK, D]) for u in range(4)]
        block = ctx.enter_context(nc.Block())

        @block.sync
        def _(sp):
            def step(n, s):
                u = s % 4
                if last_layer:
                    at = bass.ds(n * P, P)
                    src = [(kept[u], d.kept[at, :]), (record[u], d.route[at, :])]
                else:
                    src = [(kept[u], by_position(d.kept, n)), (record[u], by_position(d.route, n))]
                if s >= 4:
                    sp.wait_ge(joined.sem, n - 1)
                if last_layer and s >= 4:
                    sp.wait_ge(stored[u], (n - s % 4) * 4)
                for dst, ap in src:
                    sp.dma_start(dst[:, :], ap).then_inc(loaded[u], 16)

            loop(sp, step, 4, 4, (TILES - 4) // 4, TILES)

        if last_layer:
            @block.scalar
            def _(act):
                def step(n, s):
                    u = s % 4
                    joined.wait(act, n)
                    act.dma_start(by_position(d.out, n), kept[u][:, :]).then_inc(stored[u], 16)

                loop(act, step, 0, 4, TILES // 4, TILES)
                for u in range(4):
                    act.wait_ge(stored[u], 16 * TILES // 4)

        @block.gpsimd
        def _(pool):
            def step(n, s):
                u = s % 4
                placed.wait(pool, n)
                if s >= 4:
                    pool.wait_ge(joined.sem, n - 1)
                settle(k, pool)
                for j in range(TOPK):
                    pool.indirect_dma_start(got[u][:, j, :], None, d.expert[:, :],
                                            bass.IndirectOffsetOnAxis(ap=place[u][:, j:j + 1], axis=0)).then_inc(fetched[u], 16)

            loop(pool, step, 4, 4, (TILES - 4) // 4, TILES)

        @block.vector
        def _(dve):
            for x in (placed, first, joined):
                x.start(dve)

            def ready(n, s):
                u = s % 4
                dve.wait_ge(loaded[u], (n - s % 4) * 8 + 32)
                nc.vector.tensor_copy(place[u][:, :], record[u][:, 0:TOPK]).then_inc(placed.sem, 1)

            def join(n, s):
                u = s % 4
                dve.wait_ge(fetched[u], (n - s % 4) * 8 + 32)
                nc.vector.scalar_tensor_tensor(kept[u][:, :], got[u][:, 0, :], record[u][:, 2:3], kept[u][:, :],
                                               ALU.mult, ALU.add).then_inc(first.sem, 1)
                first.wait(dve, n)
                to = kept[u][:, :] if last_layer else k.stream[:, bass.ds(n, 1), :].rearrange("p a c -> p (a c)")
                nc.vector.scalar_tensor_tensor(to, got[u][:, 1, :], record[u][:, 3:4], kept[u][:, :],
                                               ALU.mult, ALU.add).then_inc(joined.sem, 1)

            def step(n, s):
                if s < TILES:
                    ready(n, s)
                if s >= 2:
                    join(n - 2, s - 2)

            loop(dve, step, 4, 4, (TILES - 4) // 4, TILES + 2)



def finish(k):
    k.nc.clear_and_free_semaphores(k.used)
    k.used = []
    k.nc.all_engine_barrier()


def build(nc, d):
    with ExitStack() as ctx:
        k = allocate(nc, ctx)
        stages = [(setup,), (project, 0), (attend, 0), (route, 0), (experts, 0), (combine, 0),
                  (project, 1), (attend, 1), (route, 1), (experts, 1), (combine, 1)]
        for stage, *half in stages:
            stage(k, d, *half)
            finish(k)


class Arrays:
    pass


_P = "L0_attn_a_", "L0_attn_b_", "L0_ffn_"


def kernel(**inputs):
    import numpy as _np
    import concourse.bacc as _bacc
    from concourse import mybir as _mybir
    from concourse.bass_utils import run_bass_kernel_spmd as _run

    a, b, f = ({n[len(p):]: _np.asarray(v) for n, v in inputs.items() if n.startswith(p)} for p in _P)
    E_ = D
    wq, wk, wv = (b["in_proj_w"][j * E_:(j + 1) * E_].T for j in range(3))
    bq, bk, bv = (b["in_proj_b"][j * E_:(j + 1) * E_] for j in range(3))
    given = {
        "x": a["x"].reshape(TOKENS, D),
        "w_split": _np.stack([a["Wq"], a["Wk"], b["w_tor"].T, wq, wk]),
        "wv_a": a["Wv"], "wv_b": wv, "wout": b["out_w"].T, "wr": f["Wr"],
        "cols": _np.stack([a["bq"], a["bk"], b["b_tor"], bq, bk], axis=1),
        "rows": _np.stack([a["bv"], bv, b["out_b"]]),
        "wg": f["Wg"], "wu": f["Wu"], "wd": f["Wd"],
        "const": constants(),
    }
    nc = _bacc.Bacc("TRN2", target_bir_lowering=False, num_devices=1)
    d, arrays = Arrays(), {}
    ap = {}
    for name, v in given.items():
        v = _np.ascontiguousarray(v)
        arrays[f"in_{name}"] = v
        ap[name] = nc.dram_tensor(f"in_{name}", v.shape, _mybir.dt.from_np(v.dtype), kind="ExternalInput").ap()
    d.x, d.w_split, d.wout, d.wr, d.cols, d.rows = (ap[n] for n in ("x", "w_split", "wout", "wr", "cols", "rows"))
    d.wv, d.wg, d.wu, d.wd, d.const = [ap["wv_a"], ap["wv_b"]], ap["wg"], ap["wu"], ap["wd"], ap["const"]
    scratch = lambda name, shape, dt: nc.dram_tensor(name, shape, dt).ap()
    d.stack = scratch("stack", (2, D, SLOTS, TOKENS), BF16)
    d.v = scratch("v_rows", (TOKENS, D), F32)
    d.routed = scratch("routed", (REGION_ROWS, D), F32)
    d.expert = scratch("expert_out", (STEPS * P, D), F32)
    d.kept = scratch("kept", (TOKENS, D), F32)
    d.route = scratch("route", (TOKENS, 4), F32)
    d.out = nc.dram_tensor("out", (TOKENS, D), _mybir.dt.float32, kind="ExternalOutput").ap()
    build(nc, d)
    r = _run(nc, [arrays], core_ids=[0])
    return _np.asarray(r.results[0]["out"]).reshape(ROWS, POSITIONS, D)
```

```python
from contextlib import ExitStack

import numpy as np
import concourse.bass as bass
from concourse import mybir

F32 = mybir.dt.float32
F32R = mybir.dt.float32r
BF16 = mybir.dt.bfloat16
I32 = mybir.dt.int32
U32 = mybir.dt.uint32
ALU = mybir.AluOpType
ACT = mybir.ActivationFunctionType
X = mybir.AxisListType.X

P = 128
ROWS, POSITIONS, D = 16, 256, 128
TOKENS = ROWS * POSITIONS
TILES = TOKENS // P
HEADS, HD = 16, 8
SCALE = 1.0 / float(np.sqrt(np.float32(HD)))
EPS = 1e-5
BATCH = 4
TB = BATCH * P
BATCHES = TILES // BATCH
SLOTS = 6
STACK = SLOTS * HD
EXPERTS, HIDDEN, TOPK = 8, 512, 2
CHUNKS = HIDDEN // P
DEPTH_SCALE = float(1.0 / np.sqrt(12))
REGION = TOKENS + P
STEPS = 72
SPARE = STEPS - TOPK * TOKENS // P
REGION_ROWS = EXPERTS * REGION + SPARE * P

C_IDENT, C_UPPER, C_BIAS, C_MASK_A, C_MASK_B, C_EXPERT, C_BASE, C_STEP, C_ROOT, C_END = (int(x) for x in np.cumsum(
    [0, P, P, 32, 64, 64, EXPERTS, EXPERTS, STEPS, 1]))


def constants():
    c = np.zeros((P, C_END), np.float32)
    p = np.arange(P)
    c[:, C_IDENT:C_UPPER] = np.eye(P)
    c[:, C_UPPER:C_BIAS] = p[:, None] < p[None, :]
    key = np.arange(32)
    same = (p[:, None] // 16) % 2 == key[None, :] // 16
    turn = (key[None, :] % 16 - p[:, None] % 16) % 16
    near = (turn == 0).astype(np.float32) + (turn == 1) + (turn == 15)
    c[:, C_BIAS:C_MASK_A] = np.where(same, near, np.float32(-1e30))
    head = np.repeat(np.arange(8), HD)
    c[:, C_MASK_A:C_MASK_B] = p[:, None] // 64 == head[None, :] % 2
    c[:, C_MASK_B:C_EXPERT] = p[:, None] // 32 == head[None, :] % 4
    c[:, C_EXPERT:C_BASE] = np.arange(EXPERTS)
    c[:, C_BASE:C_STEP] = np.arange(EXPERTS) * REGION
    c[:, C_STEP:C_ROOT] = np.arange(STEPS)
    c[:, C_ROOT] = -0.5
    return c


class Signal:

    def __init__(self, sem, per=1):
        self.sem, self.per = sem, per

    def start(self, eng):
        eng.sem_inc(self.sem, 2 * self.per)

    def wait(self, eng, n, part=None):
        eng.wait_ge(self.sem, n * self.per + (2 * self.per + (self.per if part is None else part)))

    def before(self, eng, n, back):
        eng.wait_ge(self.sem, n * self.per + (3 - back) * self.per)


class Chain:

    def __init__(self, sem, eng, per):
        self.sem, self.eng, self.per = sem, eng, per
        self.count = 0

    def item(self, n):
        self.n, self.count = n, 0

    def link(self, ins):
        ins.then_inc(self.sem, 1)
        self.count += 1
        self.eng.wait_ge(self.sem, self.n * self.per + self.count)

    def close(self):
        assert self.count == self.per, (self.count, self.per)


def settle(k, eng):
    eng.sem_inc(k.idle, 1)


def emptied(eng, sem, n, s, per):
    if s >= 2:
        eng.wait_ge(sem, (n - s % 2) * (per // 2))


def loop(eng, step, first, unroll, passes, end):
    for t in range(first):
        step(t, t)
    if passes:
        with eng.Fori(0, passes) as i:
            for v in range(unroll):
                step(i * unroll + (first + v), first + v)
    for t in range(first + unroll * passes, end):
        step(t, t)


class Kernel:
    pass


def allocate(nc, ctx):
    k = Kernel()
    k.nc = nc

    def sb(name, shape, dt=F32):
        return ctx.enter_context(nc.sbuf_tensor(name, shape, dt))

    k.idle = ctx.enter_context(nc.semaphore("idle"))
    k.used = []

    def sem(name):
        k.used.append(nc.alloc_semaphore(name))
        return k.used[-1]

    k.sem = sem
    k.bank = [ctx.enter_context(nc.psum_tensor(f"bank{i}", [P, 512], F32)) for i in range(8)]
    k.stream = sb("stream", [P, TILES, D])
    k.const = sb("const", [P, C_END])
    k.ident = k.const[:, C_IDENT:C_UPPER]
    k.upper = sb("upper", [P, P], BF16)
    k.ones = sb("ones", [P, P], BF16)
    k.zeros = sb("zeros", [P, D])
    k.table = sb("table", [1, STEPS, 2], I32)
    k.split = sb("split", [P, 4, 2, D], F32R)
    k.wv = [sb("wv_a", [P, D]), sb("wv_b", [P, D])]
    k.wout = sb("wout", [P, D])
    k.wr = sb("wr", [P, EXPERTS])
    k.cols = sb("cols", [P, 4])
    k.rows = sb("rows", [P, 3, D])
    k.wgu = sb("wgu", [P, EXPERTS, 2, 2, HIDDEN], F32R)
    k.wd = sb("wd", [P, EXPERTS, CHUNKS, D])
    k.norm_x = [sb(f"norm_x{u}", [P, BATCH, D]) for u in range(2)]
    k.stats = [sb(f"stats{u}", [P, BATCH, 6]) for u in range(2)]
    k.moments = [sb(f"moments{u}", [P, BATCH, 2]) for u in range(2)]
    k.rstd = [sb(f"rstd{u}", [P, BATCH]) for u in range(2)]
    k.xT = [sb(f"xT{u}", [P, TB]) for u in range(2)]
    return k


def setup(k, d):
    nc = k.nc
    loaded, staged, folded, whole_ready, cleared = (
        k.sem(f"setup_{x}") for x in ("loaded", "staged", "folded", "whole", "cleared"))
    TORUS, Q, K, V = 2, 3, 4, 5
    with ExitStack() as ctx:
        sb = lambda name, shape: ctx.enter_context(nc.sbuf_tensor(f"setup_{name}", shape, F32))
        raw = sb("raw", [P, 6, D])
        whole = sb("whole", [P, 4, D])
        cols = sb("cols", [P, 5])
        spread = sb("spread", [P, P])
        block = ctx.enter_context(nc.Block())
        fixed = [(raw[:, :, :], d.w_split.rearrange("w c f -> c w f")), (cols[:, :], d.cols),
                 (k.const[:, :], d.const[:, :]),
                 (k.stream[:, :, :], d.x.rearrange("(t p) c -> p t c", p=P)),
                 (k.wv[0][:, :], d.wv), (k.wout[:, :], d.wout), (k.wr[:, :], d.wr)]
        psF, psB = k.bank[0], k.bank[1]

        @block.sync
        def _(sp):
            for r in range(3):
                sp.dma_start(k.rows[:, r, :], d.rows[r:r + 1, :].to_broadcast([P, D])).then_inc(loaded, 16)
            for dst, src in fixed:
                sp.dma_start(dst, src).then_inc(loaded, 16)
            sp.wait_ge(staged, 1)
            for j in range(SPARE):
                sp.dma_start(d.routed[EXPERTS * REGION + j * P:EXPERTS * REGION + (j + 1) * P, :],
                             k.zeros[:, :]).then_inc(cleared, 16)
            sp.wait_ge(loaded, 16 * (len(fixed) + 3))
            sp.wait_ge(cleared, 16 * SPARE)

        @block.tensor
        def _(pe):
            pe.wait_ge(staged, 2)
            nc.tensor.matmul(psF[:, 0:3 * D], raw[:, TORUS, :], raw[:, Q:V + 1, :], start=True, stop=True)
            for j, w in enumerate((Q, K)):
                nc.tensor.matmul(psB[:, j:j + 1], raw[:, w, :], cols[:, TORUS:TORUS + 1], start=True, stop=True)
            nc.tensor.matmul(psB[:, P:2 * P], spread[:, :], raw[:, V, :], start=True, stop=True).then_inc(folded, 1)

        @block.vector
        def _(dve):
            nc.vector.memset(k.ones[:, :], 1.0)
            nc.vector.memset(k.zeros[:, :], 0.0).then_inc(staged, 1)
            dve.wait_ge(loaded, 16 * (len(fixed) + 3))
            nc.vector.tensor_copy(spread[:, :], cols[:, TORUS:TORUS + 1].to_broadcast([P, P])).then_inc(staged, 1)
            nc.vector.tensor_copy(k.upper[:, :], k.const[:, C_UPPER:C_BIAS])
            nc.vector.tensor_scalar(whole[:, 0, :], raw[:, 0, :], SCALE, None, ALU.mult)
            nc.vector.tensor_copy(whole[:, 1, :], raw[:, 1, :])
            nc.vector.tensor_scalar(k.cols[:, 0:1], cols[:, 0:1], SCALE, None, ALU.mult)
            nc.vector.tensor_copy(k.cols[:, 1:2], cols[:, 1:2])
            dve.wait_ge(folded, 1)
            nc.vector.tensor_scalar(whole[:, 2, :], psF[:, 0:D], SCALE, None, ALU.mult)
            nc.vector.tensor_copy(whole[:, 3, :], psF[:, D:2 * D]).then_inc(whole_ready, 1)
            nc.vector.tensor_copy(k.wv[1][:, :], psF[:, 2 * D:3 * D])
            nc.vector.tensor_tensor(k.rows[:, 1, :], k.rows[:, 1, :], psB[:, P:2 * P], ALU.add)
            nc.vector.tensor_scalar(k.cols[:, 2:3], psB[:, 0:1], cols[:, Q:Q + 1], SCALE, ALU.add, ALU.mult)
            nc.vector.tensor_tensor(k.cols[:, 3:4], psB[:, 1:2], cols[:, K:K + 1], ALU.add)
            dve.wait_ge(whole_ready, 1)
            nc.vector.tensor_copy(k.split[:, :, 0, :], whole[:, :, :]).then_inc(whole_ready, 1)
            dve.wait_ge(whole_ready, 2)
            nc.vector.tensor_tensor(k.split[:, :, 1, :], whole[:, :, :], k.split[:, :, 0, :].bitcast(F32), ALU.subtract)


def measure(k, chain, n, u, src, moments):
    nc = k.nc
    for t in range(BATCH):
        last = nc.vector.bn_stats(k.stats[u][:, t, :], src[:, bass.ds(n * BATCH + t, 1), :].rearrange("p a c -> p (a c)"))
    chain.link(last)
    settle(k, chain.eng)
    for t in range(BATCH):
        last = nc.vector.bn_aggr(k.moments[u][:, t, :], k.stats[u][:, t, :])
    last.then_inc(moments.sem, 1)


def normalise(k, dve, n, u, src, moments, rooted, ready, free=None):
    nc = k.nc
    moments.wait(dve, n)
    rooted.wait(dve, n)
    if free:
        free()
    for t in range(BATCH):
        last = nc.vector.tensor_scalar(
            k.norm_x[u][:, t, :], src[:, bass.ds(n * BATCH + t, 1), :].rearrange("p a c -> p (a c)"),
            k.moments[u][:, t, 0:1], k.rstd[u][:, t:t + 1], ALU.subtract, ALU.mult)
    last.then_inc(ready.sem, 1)


def root_of_variance(k, pool, n, u, moments, rooted):
    moments.wait(pool, n)
    settle(k, pool)
    k.nc.gpsimd.tensor_scalar(k.rstd[u][:, :], k.moments[u][:, :, 1], EPS, None, ALU.add).then_inc(rooted.sem, 1)
    rooted.wait(pool, n, 1)
    k.nc.gpsimd.tensor_tensor(k.rstd[u][:, :], k.rstd[u][:, :], k.const[:, C_ROOT:C_END].to_broadcast([P, BATCH]), ALU.pow).then_inc(rooted.sem, 1)


def project(k, d, half):
    nc = k.nc
    tag = "ab"[half]
    prepare = half == 0
    sem = lambda name, per=1: Signal(k.sem(f"proj_{tag}_{name}"), per)
    normed, turned, copied, high, low = (sem(x) for x in ("normed", "turned", "copied", "high", "low"))
    moments, rooted = sem("moments"), sem("rooted", 2)
    q_ready, k_ready, v_ready, v_out = sem("q"), sem("k"), sem("v"), sem("v_out")
    part0, rest1, part1, part2 = sem("part0", 2), sem("rest1", 2), sem("part1"), sem("part2")
    stored = [k.sem(f"proj_{tag}_stored{u}") for u in range(2)]
    staged = [k.sem(f"proj_{tag}_staged{u}") for u in range(2)] if prepare else None
    wd_loaded = k.sem(f"proj_{tag}_wd")
    weights_high, weights_low = sem("weights_high"), sem("weights_low")
    chain_sem = k.sem(f"proj_{tag}_chain")
    stores = 5
    psT, psq, psk, psv = (k.bank[2 * j:2 * j + 2] for j in range(4))
    FIRST, END = 4, BATCHES + 3
    PASSES = (BATCHES - FIRST) // 2
    assert EXPERTS == BATCHES
    with ExitStack() as ctx:
        sb = lambda name, shape, dt=F32: ctx.enter_context(nc.sbuf_tensor(f"proj_{tag}_{name}", shape, dt))
        hi = [sb(f"hi{u}", [P, TB], F32R) for u in range(2)]
        lo = [sb(f"lo{u}", [P, TB], F32R) for u in range(2)]
        rest = [sb(f"rest{u}", [P, 2, TB]) for u in range(2)]
        parts = [sb(f"parts{u}", [P, 3, 2, TB], BF16) for u in range(2)]
        v = [sb(f"v{u}", [P, BATCH, D]) for u in range(2)]
        stage = [sb(f"stage{u}", [P, 2, HIDDEN]) for u in range(2)] if prepare else None
        block = ctx.enter_context(nc.Block())
        bias = lambda side: k.cols[:, 2 * half + side:2 * half + side + 1]

        @block.sync
        def _(sp):
            def step(n, s):
                if prepare and s < EXPERTS:
                    if s >= 2:
                        weights_low.before(sp, n, 2)
                        settle(k, sp)
                    for j, w in enumerate((d.wg, d.wu)):
                        sp.dma_start(stage[s % 2][:, j, :], w[bass.ds(n, 1), :, :].rearrange("a c h -> (a c) h"))\
                            .then_inc(staged[s % 2], 16)
                if 2 <= s < BATCHES + 2:
                    m, u = n - 2, s % 2
                    v_out.wait(sp, m)
                    sp.dma_start(d.v[bass.ds(m * TB, TB), :].rearrange("(t p) c -> p t c", p=P), v[u][:, :, :]).then_inc(stored[u], 16)
                if s >= 3:
                    m, u = n - 3, (s - 3) % 2
                    part2.wait(sp, m)
                    part1.wait(sp, m)
                    for side in range(2):
                        for a in range(2):
                            sp.dma_start(d.parts[side, bass.ds(m, 1), a].rearrange("m j e h t -> (m e h) j t"),
                                         parts[u][64 * a:64 * (a + 1), :, side, :]).then_inc(stored[u], 16)

            loop(sp, step, FIRST, 2, PASSES, END)
            if prepare:
                sp.dma_start(k.wd[:, :, :, :], d.wd.rearrange("e (j p) c -> p e j c", p=P)).then_inc(wd_loaded, 16)
                sp.wait_ge(wd_loaded, 16)
            for u in range(2):
                sp.wait_ge(stored[u], 16 * stores * BATCHES // 2)

        @block.vector
        def _(dve):
            chain = Chain(chain_sem, dve, 1)
            for x in (moments, normed, high, rest1, weights_low):
                x.start(dve)

            def step(n, s):
                if 1 <= s < BATCHES + 1:
                    normalise(k, dve, n - 1, (s - 1) % 2, k.stream, moments, rooted, normed,
                              lambda: turned.before(dve, n - 1, 2))
                if s < BATCHES:
                    chain.item(n)
                    measure(k, chain, n, s % 2, k.stream, moments)
                    chain.close()
                if 2 <= s < BATCHES + 2:
                    m, u = n - 2, s % 2
                    part2.before(dve, m, 2)
                    part1.before(dve, m, 2)
                    for side, ps in enumerate((psq, psk)):
                        part0.wait(dve, m, side + 1)
                        nc.vector.scalar_tensor_tensor(rest[u][:, side, :], ps[u][:, :], bias(side), parts[u][:, 0, side, :],
                                                       ALU.add, ALU.subtract).then_inc(rest1.sem, 1)
                if 1 <= s < BATCHES + 1:
                    m, u = n - 1, (s - 1) % 2
                    copied.wait(dve, m)
                    q_ready.before(dve, m, 2)
                    k_ready.before(dve, m, 2)
                    nc.vector.tensor_copy(hi[u][:, :], k.xT[u][:, :]).then_inc(high.sem, 1)
                if prepare and s < EXPERTS:
                    weights_high.wait(dve, n)
                    nc.vector.tensor_tensor(k.wgu[:, bass.ds(n, 1), :, 1, :].rearrange("p a j h -> p (a j) h"), stage[s % 2][:, :, :],
                                            k.wgu[:, bass.ds(n, 1), :, 0, :].rearrange("p a j h -> p (a j) h").bitcast(F32),
                                            ALU.subtract).then_inc(weights_low.sem, 1)

            loop(dve, step, FIRST, 2, PASSES, END)

        @block.scalar
        def _(act):
            for x in (copied, part0, v_out, part1, weights_high):
                x.start(act)

            def step(n, s):
                if s >= 3:
                    m, u = n - 3, (s - 3) % 2
                    rest1.wait(act, m)
                    nc.scalar.activation(parts[u][:, 1, :, :], rest[u][:, :, :], ACT.Copy).then_inc(part1.sem, 1)
                project_side = lambda side, ps, ready: (
                    ready.wait(act, n - 2),
                    emptied(act, stored[s % 2], n - 2, s - 2, 16 * stores),
                    nc.scalar.activation(parts[s % 2][:, 0, side, :], ps[s % 2][:, :], ACT.Identity, bias=bias(side))
                    .then_inc(part0.sem, 1))
                if 2 <= s < BATCHES + 2:
                    project_side(0, psq, q_ready)
                if 1 <= s < BATCHES + 1:
                    m, u = n - 1, (s - 1) % 2
                    turned.wait(act, m)
                    low.before(act, m, 2)
                    v_ready.before(act, m, 2)
                    nc.scalar.activation(k.xT[u][:, :], psT[u][:, :], ACT.Copy).then_inc(copied.sem, 1)
                if 2 <= s < BATCHES + 2:
                    project_side(1, psk, k_ready)
                    v_ready.wait(act, n - 2)
                    nc.scalar.activation(v[s % 2][:, :, :].rearrange("p t c -> p (t c)"), psv[s % 2][:, :], ACT.Copy).then_inc(v_out.sem, 1)
                if prepare and s < EXPERTS:
                    act.wait_ge(staged[s % 2], (n - s % 2) * 16 + 32)
                    nc.scalar.activation(k.wgu[:, bass.ds(n, 1), :, 0, :].rearrange("p a j h -> p (a j) h"), stage[s % 2][:, :, :],
                                         ACT.Copy).then_inc(weights_high.sem, 1)

            loop(act, step, FIRST, 2, PASSES, END)

        @block.gpsimd
        def _(pool):
            for x in (rooted, low, part2):
                x.start(pool)

            def step(n, s):
                if s < BATCHES:
                    root_of_variance(k, pool, n, s % 2, moments, rooted)
                if s >= 3:
                    m, u = n - 3, (s - 3) % 2
                    part1.wait(pool, m)
                    nc.gpsimd.tensor_tensor(parts[u][:, 2, :, :], rest[u][:, :, :], parts[u][:, 1, :, :], ALU.subtract).then_inc(part2.sem, 1)
                if 1 <= s < BATCHES + 1:
                    m, u = n - 1, (s - 1) % 2
                    high.wait(pool, m)
                    q_ready.before(pool, m, 2)
                    k_ready.before(pool, m, 2)
                    nc.gpsimd.tensor_tensor(lo[u][:, :], k.xT[u][:, :], hi[u][:, :].bitcast(F32), ALU.subtract).then_inc(low.sem, 1)

            loop(pool, step, FIRST, 2, PASSES, END)

        @block.tensor
        def _(pe):
            for x in (turned, q_ready, k_ready, v_ready):
                x.start(pe)

            def step(n, s):
                if 2 <= s < BATCHES + 2:
                    m, u = n - 2, s % 2
                    high.wait(pe, m)
                    low.wait(pe, m)
                    part0.before(pe, m, 2)
                    rest1.before(pe, m, 2)
                    for w, (ps, ready) in enumerate(((psq, q_ready), (psk, k_ready))):
                        for j, (a, b) in enumerate(((0, hi), (1, hi), (0, lo))):
                            last = nc.tensor.matmul(ps[u][:, :], k.split[:, 2 * half + w, a, :], b[u][:, :], start=j == 0, stop=j == 2)
                        last.then_inc(ready.sem, 1)
                if 1 <= s < BATCHES + 1:
                    m, u = n - 1, (s - 1) % 2
                    normed.wait(pe, m)
                    copied.before(pe, m, 2)
                    for t in range(BATCH):
                        last = nc.tensor.transpose(psT[u][:, t * P:(t + 1) * P], k.norm_x[u][:, t, :], k.ident)
                    last.then_inc(turned.sem, 1)
                if 2 <= s < BATCHES + 2:
                    m, u = n - 2, s % 2
                    copied.wait(pe, m)
                    v_out.before(pe, m, 2)
                    for t in range(BATCH):
                        last = nc.tensor.matmul(psv[u][:, t * D:(t + 1) * D], k.xT[u][:, t * P:(t + 1) * P],
                                                k.wv[half][:, :], start=True, stop=True)
                    last.then_inc(v_ready.sem, 1)

            loop(pe, step, FIRST, 2, PASSES, END)


def attend(k, d, half):
    nc = k.nc
    tag = "ab"[half]
    second = half == 1
    blk = 32 if second else 64
    nb = P // blk
    group = P // blk
    rounds = HEADS // 2
    turns = HEADS // group
    width = HEADS * blk
    sem = lambda name, per=1: Signal(k.sem(f"att_{tag}_{name}"), per)
    scored, shifted, risen = sem("scored"), sem("shifted"), sem("risen")
    turned, turned_copied = sem("turned"), sem("turned_copied", 2)
    values, mixed, even, summed, based = sem("values"), sem("mixed"), sem("even"), sem("summed"), sem("based")
    back, back_copied, mapped, mapped_added = sem("back"), sem("back_copied"), sem("mapped"), sem("mapped_added")
    loaded = [k.sem(f"att_{tag}_loaded{u}") for u in range(2)]
    chain_sem = k.sem(f"att_{tag}_chain")
    pool_sem = k.sem(f"att_{tag}_pool")
    loads = 12 + group
    psS = [k.bank[2 * u:2 * u + 2] for u in range(2)]
    psP = k.bank[4:6]
    psO, psE = k.bank[6], k.bank[7]
    mask = k.const[:, C_MASK_B:C_EXPERT] if second else k.const[:, C_MASK_A:C_MASK_B]
    with ExitStack() as ctx:
        sb = lambda name, shape, dt=F32: ctx.enter_context(nc.sbuf_tensor(f"att_{tag}_{name}", shape, dt))
        qs = [sb(f"q{m}", [P, rounds, TB], BF16) for m in range(2)]
        ks = [sb(f"k{m}", [P, rounds, TB], BF16) for m in range(2)]
        vd = [sb(f"v{m}", [P, BATCH * nb, D]) for m in range(2)]
        vx = [sb(f"vx{u}", [P, nb, 2, rounds, HD + 1]) for u in range(2)]
        prob = [sb(f"prob{u}", [P, HEADS, blk]) for u in range(2)]
        probT = [sb(f"probT{u}", [P, turns, P]) for u in range(2)]
        most = [sb(f"most{u}", [P, HEADS]) for u in range(2)]
        inv = [sb(f"inv{u}", [P, HEADS]) for u in range(2)]
        mix = [sb(f"mix{u}", [P, D]) for u in range(2)]
        base = [sb(f"base{u}", [P, D]) for u in range(2)]
        mixT = [sb(f"mixT{u}", [P, P]) for u in range(2)]
        block = ctx.enter_context(nc.Block())

        def scores(u, a):
            return psS[u][a][:, 0:rounds * blk].rearrange("p (h c) -> p h c", c=blk)

        @block.sync
        def _(sp):
            def step(m, s):
                v = s % 2
                if s >= 2:
                    sp.wait_ge(scored.sem, m * BATCH + (2 - BATCH))
                    sp.wait_ge(values.sem, m * BATCH + (2 - BATCH))
                at = bass.ds(m * TB, TB)
                for a in range(2):
                    q_part, k_part = (d.parts[side, bass.ds(m, 1), a].rearrange("m j e h t -> (m j) e (h t)") for side in range(2))
                    for j, (slot, many) in enumerate(((0, 3), (3, 2), (5, 1))):
                        to = slice(64 * a + slot * HD, 64 * a + (slot + many) * HD)
                        sp.dma_start(qs[v][to, :, :], q_part[j:j + 1].to_broadcast([many, HD, rounds * TB])).then_inc(loaded[v], 16)
                        sp.dma_start(ks[v][to, :, :], k_part[0:many]).then_inc(loaded[v], 16)
                for g in range(group):
                    src = d.v[at, :].rearrange("(b q) c -> q b c", q=blk)
                    sp.dma_start(vd[v][blk * g:blk * (g + 1), :, :], src).then_inc(loaded[v], 16)

            loop(sp, step, 2, 2, BATCHES // 2 - 1, BATCHES)

        def batch_loaded(eng, n, s):
            eng.wait_ge(loaded[s // BATCH % 2], (n - s % 8) * (2 * loads) + 16 * loads)

        @block.gpsimd
        def _(pool):
            for x in (values, summed, based):
                x.start(pool)
            for u in range(2):
                for a in range(2):
                    for b in range(nb):
                        nc.gpsimd.tensor_copy(vx[u][:, b, a, :, HD],
                                              mask.rearrange("p (h e) -> p h e", e=HD)[:, :, 0])
            chain = Chain(pool_sem, pool, 1)

            def step(n, s):
                if s < TILES:
                    batch_loaded(pool, n, s)
                    mixed.before(pool, n, 2)
                    for a in range(2):
                        for b in range(nb):
                            vb = vd[s // BATCH % 2][:, (s % BATCH) * nb + b, :].rearrange("p (h a e) -> p a h e", a=2, e=HD)
                            last = nc.gpsimd.tensor_tensor(vx[s % 2][:, b, a, :, 0:HD], vb[:, a],
                                                           mask.rearrange("p (h e) -> p h e", e=HD), ALU.mult)
                    last.then_inc(values.sem, 1)
                if s >= 2 and s - 2 < TILES:
                    m, u = n - 2, s % 2
                    tile = k.stream[:, bass.ds(m, 1), :].rearrange("p a c -> p (a c)")
                    even.wait(pool, m)
                    if second:
                        back.before(pool, m, 2)
                        nc.gpsimd.tensor_tensor(mix[u][:, :], mix[u][:, :], k.rows[:, 1, :], ALU.add).then_inc(summed.sem, 1)
                        mapped_added.before(pool, m, 2)
                        settle(k, pool)
                        nc.gpsimd.tensor_tensor(base[u][:, :], tile, k.rows[:, 2, :], ALU.add).then_inc(based.sem, 1)
                    else:
                        chain.item(m)
                        settle(k, pool)
                        chain.link(nc.gpsimd.tensor_tensor(base[u][:, :], tile, k.rows[:, 0, :], ALU.add))
                        settle(k, pool)
                        nc.gpsimd.tensor_tensor(tile, mix[u][:, :], base[u][:, :], ALU.add).then_inc(summed.sem, 1)

            loop(pool, step, 8, 8, TILES // 8 - 1, TILES + 2)

        @block.tensor
        def _(pe):
            for x in (scored, turned, mixed, back, mapped):
                x.start(pe)

            def score(n, s):
                batch_loaded(pe, n, s)
                shifted.before(pe, n, 2)
                settle(k, pe)
                u, v = s % 2, s // BATCH % 2
                for h in range(rounds):
                    for a in range(2):
                        for b in range(nb):
                            at = slice((s % BATCH) * P + b * blk, (s % BATCH) * P + (b + 1) * blk)
                            rows = slice(64 * a, 64 * a + STACK)
                            last = nc.tensor.matmul(psS[u][a][b * blk:(b + 1) * blk, h * blk:(h + 1) * blk],
                                                    qs[v][rows, h, at], ks[v][rows, h, at], start=True, stop=True,
                                                    tile_position=(64 * a, b * blk))
                last.then_inc(scored.sem, 1)

            def mixing(n, s):
                u = s % 2
                turned_copied.wait(pe, n)
                values.wait(pe, n)
                even.before(pe, n, 1)
                flat = lambda b, i: vx[u][:, b, :, :, :].rearrange("p a h e -> p (a h e)")[
                    :, i * group * (HD + 1):(i + 1) * group * (HD + 1)]
                for b in range(nb):
                    for i in range(turns):
                        last = nc.tensor.matmul(psO[b * blk:(b + 1) * blk, i * group * (HD + 1):(i + 1) * group * (HD + 1)],
                                                probT[u][:, i, b * blk:(b + 1) * blk], flat(b, i), start=True, stop=True,
                                                tile_position=(0, b * blk))
                last.then_inc(mixed.sem, 1)

            def turn(n, s):
                u = s % 2
                risen.wait(pe, n)
                turned_copied.before(pe, n, 1)
                for i in range(turns):
                    last = nc.tensor.transpose(psP[i // 4][:, (i % 4) * P:(i % 4 + 1) * P],
                                               prob[u][:, i * group:(i + 1) * group, :].rearrange("p h c -> p (h c)"), k.ident)
                last.then_inc(turned.sem, 1)

            def turn_back(n, s):
                summed.wait(pe, n)
                back_copied.before(pe, n, 1)
                mapped_added.before(pe, n, 1)
                nc.tensor.transpose(psE[:, 0:P], mix[s % 2][:, :], k.ident).then_inc(back.sem, 1)

            def map_out(n, s):
                back_copied.wait(pe, n)
                nc.tensor.matmul(psE[:, P:2 * P], mixT[s % 2][:, :], k.wout[:, :], start=True, stop=True).then_inc(mapped.sem, 1)

            def step(n, s):
                if s < TILES:
                    score(n, s)
                if second and 3 <= s < TILES + 3:
                    turn_back(n - 3, s - 3)
                if 2 <= s < TILES + 2:
                    mixing(n - 2, s - 2)
                if 1 <= s < TILES + 1:
                    turn(n - 1, s - 1)
                if second and 3 <= s < TILES + 3:
                    map_out(n - 3, s - 3)

            loop(pe, step, 8, 8, TILES // 8 - 1, TILES + 3)

        @block.vector
        def _(dve):
            for x in (shifted, even, mapped_added):
                x.start(dve)
            chain = Chain(chain_sem, dve, 3 if second else 2)
            bias = k.const[:, C_BIAS:C_MASK_A].unsqueeze(1).to_broadcast([P, rounds, blk]) if second else None

            def soften(n, s):
                u = s % 2
                chain.item(n)
                scored.wait(dve, n)
                if second:
                    turned.before(dve, n, 2)
                    for a in range(2):
                        last = nc.vector.tensor_tensor(prob[u][:, a * rounds:(a + 1) * rounds, :], scores(u, a), bias, ALU.add)
                    chain.link(last)
                    chain.link(nc.vector.tensor_reduce(most[u][:, :], prob[u][:, :, :], X, ALU.max))
                    nc.vector.tensor_tensor(prob[u][:, :, :], prob[u][:, :, :],
                                            most[u][:, :].unsqueeze(2).to_broadcast([P, HEADS, blk]), ALU.subtract)\
                        .then_inc(shifted.sem, 1)
                else:
                    for a in range(2):
                        last = nc.vector.tensor_reduce(most[u][:, a * rounds:(a + 1) * rounds], scores(u, a), X, ALU.max)
                    chain.link(last)
                    turned.before(dve, n, 2)
                    for a in range(2):
                        last = nc.vector.tensor_tensor(
                            prob[u][:, a * rounds:(a + 1) * rounds, :], scores(u, a),
                            most[u][:, a * rounds:(a + 1) * rounds].unsqueeze(2).to_broadcast([P, rounds, blk]), ALU.subtract)
                    last.then_inc(shifted.sem, 1)

            def divide(n, s):
                u = s % 2
                mixed.wait(dve, n)
                out = psO[:, 0:HEADS * (HD + 1)].rearrange("p (a h e) -> p a h e", a=2, e=HD + 1)
                chain.link(nc.vector.reciprocal(inv[u][:, :].rearrange("p (a h) -> p a h", a=2), out[:, :, :, HD]))
                if second:
                    back.before(dve, n, 2)
                else:
                    summed.before(dve, n, 2)
                for a in range(2):
                    last = nc.vector.tensor_tensor(
                        mix[u][:, :].rearrange("p (h a e) -> p a h e", a=2, e=HD)[:, a], out[:, a, :, 0:HD],
                        inv[u][:, a * rounds:(a + 1) * rounds].unsqueeze(2).to_broadcast([P, rounds, HD]), ALU.mult)
                last.then_inc(even.sem, 1)

            def add_map(n, s):
                mapped.wait(dve, n)
                based.wait(dve, n)
                nc.vector.tensor_tensor(k.stream[:, bass.ds(n, 1), :].rearrange("p a c -> p (a c)"), psE[:, P:2 * P],
                                        base[s % 2][:, :], ALU.add).then_inc(mapped_added.sem, 1)

            def step(n, s):
                if s < TILES:
                    soften(n, s)
                if s >= TILES:
                    chain.item(n)
                if 2 <= s < TILES + 2:
                    divide(n - 2, s - 2)
                for _ in range(chain.per - chain.count):
                    dve.sem_inc(chain_sem, 1)
                if second and 3 <= s < TILES + 3:
                    add_map(n - 3, s - 3)

            loop(dve, step, 8, 8, TILES // 8 - 1, TILES + 3)

        @block.scalar
        def _(act):
            for x in (risen, turned_copied, back_copied):
                x.start(act)

            def step(n, s):
                if s < TILES:
                    shifted.wait(act, n)
                    nc.scalar.activation(prob[s % 2][:, :, :], prob[s % 2][:, :, :], ACT.Exp).then_inc(risen.sem, 1)
                if second and 3 <= s < TILES + 3:
                    m, u = n - 3, (s - 3) % 2
                    back.wait(act, m)
                    nc.scalar.activation(mixT[u][:, :], psE[:, 0:P], ACT.Copy).then_inc(back_copied.sem, 1)
                if 1 <= s < TILES + 1:
                    m, u = n - 1, (s - 1) % 2
                    turned.wait(act, m)
                    mixed.before(act, m, 2)
                    half_turns = turns // 2
                    for j in range(2):
                        b, c = (j, 0) if turns == 8 else (0, j * half_turns * P)
                        nc.scalar.activation(probT[u][:, j * half_turns:(j + 1) * half_turns, :].rearrange("p i t -> p (i t)"),
                                             psP[b][:, c:c + half_turns * P], ACT.Copy).then_inc(turned_copied.sem, 1)

            loop(act, step, 8, 8, TILES // 8 - 1, TILES + 3)


def route(k, d, layer):
    nc = k.nc
    tag = "ab"[layer]
    sem = lambda name, per=1: Signal(k.sem(f"route_{tag}_{name}"), per)
    normed, turned, copied, moments, rooted = sem("normed"), sem("turned"), sem("copied"), sem("moments"), sem("rooted", 2)
    logits, gap, risen, picked, ranked, placed, read = (sem(x) for x in ("logits", "gap", "risen", "picked", "ranked", "placed", "read"))
    sent = [k.sem(f"route_{tag}_sent{u}") for u in range(2)]
    kept = [k.sem(f"route_{tag}_kept{u}") for u in range(2)]
    chain_sem, table_sem, totals, tails, settled = (
        k.sem(f"route_{tag}_{x}") for x in ("chain", "table", "totals", "tails", "settled"))
    per_batch = TOPK * BATCH
    psT = [k.bank[0], k.bank[1]]
    psL, psR, psC = k.bank[2], k.bank[3], k.bank[4]
    with ExitStack() as ctx:
        sb = lambda name, shape, dt=F32: ctx.enter_context(nc.sbuf_tensor(f"route_{tag}_{name}", shape, dt))
        logit = [sb(f"logit{u}", [P, BATCH, EXPERTS]) for u in range(2)]
        top = [sb(f"top{u}", [P, BATCH, 8]) for u in range(2)]
        index = [sb(f"index{u}", [P, BATCH, 8], U32) for u in range(2)]
        less = [sb(f"less{u}", [P, BATCH]) for u in range(2)]
        rise = [sb(f"rise{u}", [P, BATCH]) for u in range(2)]
        total = [sb(f"total{u}", [P, BATCH]) for u in range(2)]
        hot = [sb(f"hot{u}", [P, BATCH, TOPK, EXPERTS]) for u in range(2)]
        both = [sb(f"both{u}", [P, BATCH, EXPERTS], BF16) for u in range(2)]
        seen = [sb(f"seen{u}", [P, EXPERTS], BF16) for u in range(2)]
        four = [sb(f"four{u}", [P, EXPERTS]) for u in range(2)]
        rank = [sb(f"rank{u}", [P, BATCH, EXPERTS]) for u in range(2)]
        spot = [sb(f"spot{u}", [P, BATCH, TOPK, EXPERTS]) for u in range(2)]
        record = [sb(f"record{u}", [P, BATCH, 6]) for u in range(2)]
        place = [sb(f"place{u}", [P, BATCH, TOPK], U32) for u in range(2)]
        records = sb("records", [P, TILES, 6])
        hots = sb("hots", [P, TILES * TOPK, EXPERTS])
        moves = sb("moves", [P, TILES * TOPK])
        count_i = sb("count_i", [P, EXPERTS], I32)
        tiles_i = sb("tiles_i", [P, EXPERTS], I32)
        tiles_f = sb("tiles_f", [P, EXPERTS])
        upto = sb("upto", [P, EXPERTS])
        shift = sb("shift", [P, EXPERTS])
        past = sb("past", [1, STEPS, EXPERTS])
        jump = sb("jump", [P, EXPERTS])
        far = sb("far", [1, STEPS, EXPERTS])
        row_f = sb("row_f", [1, STEPS])
        expert_f = sb("expert_f", [1, STEPS])
        block = ctx.enter_context(nc.Block())

        @block.sync
        def _(sp):
            def step(n, s):
                u = s % 2
                at = bass.ds(n * TB, TB)
                sp.dma_start(d.kept[at, :].rearrange("(t p) c -> p t c", p=P),
                             k.stream[:, bass.ds(n * BATCH, BATCH), :]).then_inc(kept[u], 16)

            loop(sp, step, 0, 2, BATCHES // 2, BATCHES)
            sp.wait_ge(table_sem, 1)
            for e in range(EXPERTS):
                end = sp.value_load(count_i[0:1, e:e + 1], min_val=0, max_val=TOKENS)
                sp.dma_start(d.routed[bass.ds(end + e * REGION, P), :], k.zeros[:, :]).then_inc(tails, 16)
            sp.wait_ge(settled, 1)
            sp.dma_start(d.route.rearrange("(t p) c -> p t c", p=P), records[:, :, 0:4]).then_inc(tails, 16)
            sp.wait_ge(tails, 16 * (EXPERTS + 1))
            for u in range(2):
                sp.wait_ge(kept[u], 16 * BATCHES // 2)

        @block.gpsimd
        def _(pool):
            rooted.start(pool)

            def step(n, s):
                u = s % 2
                root_of_variance(k, pool, n, u, moments, rooted)
                if isinstance(n, int) and n == 0:
                    return
                send(n - 1, s - 1)

            def send(n, s):
                u = s % 2
                placed.wait(pool, n)
                settle(k, pool)
                for t in range(BATCH):
                    for j in range(TOPK):
                        pool.indirect_dma_start(
                            d.routed[:, :], bass.IndirectOffsetOnAxis(ap=place[u][:, t, j:j + 1], axis=0),
                            k.norm_x[u][:, t, :], None).then_inc(sent[u], 16)

            loop(pool, step, 2, 2, (BATCHES - 2) // 2, BATCHES)
            send(BATCHES - 1, BATCHES - 1)
            for u in range(2):
                pool.wait_ge(sent[u], 16 * per_batch * BATCHES // 2)

        @block.tensor
        def _(pe):
            for x in (turned, logits, ranked):
                x.start(pe)

            def step(n, s):
                u = s % 2
                normed.wait(pe, n)
                copied.before(pe, n, 2)
                for t in range(BATCH):
                    last = nc.tensor.transpose(psT[u][:, t * P:(t + 1) * P], k.norm_x[u][:, t, :], k.ident)
                last.then_inc(turned.sem, 1)
                copied.wait(pe, n)
                read.before(pe, n, 1)
                for t in range(BATCH):
                    last = nc.tensor.matmul(psL[:, t * EXPERTS:(t + 1) * EXPERTS], k.xT[u][:, t * P:(t + 1) * P],
                                            k.wr[:, :], start=True, stop=True)
                last.then_inc(logits.sem, 1)
                picked.wait(pe, n)
                placed.before(pe, n, 1)
                for t in range(BATCH):
                    out = psR[:, t * EXPERTS:(t + 1) * EXPERTS]
                    nc.tensor.matmul(out, k.upper[:, :], both[u][:, t, :], start=True, stop=False)
                    for e in range(t):
                        nc.tensor.matmul(out, k.ones[:, :], both[u][:, e, :], start=False, stop=False)
                    last = nc.tensor.matmul(out, k.ones[:, :], seen[u][:, :], start=False, stop=True)
                last.then_inc(ranked.sem, 1)

            loop(pe, step, 0, 2, BATCHES // 2, BATCHES)
            placed.wait(pe, BATCHES - 1)
            nc.tensor.matmul(psC[:, 0:EXPERTS], k.ones[:, :], seen[BATCHES % 2][:, :], start=True, stop=True).then_inc(totals, 1)

        @block.scalar
        def _(act):
            for x in (copied, risen):
                x.start(act)

            def step(n, s):
                u = s % 2
                turned.wait(act, n)
                logits.before(act, n, 2)
                nc.scalar.activation(k.xT[u][:, :], psT[u][:, :], ACT.Copy).then_inc(copied.sem, 1)
                gap.wait(act, n)
                placed.before(act, n, 2)
                nc.scalar.activation(rise[u][:, :], less[u][:, :], ACT.Exp).then_inc(risen.sem, 1)

            loop(act, step, 0, 2, BATCHES // 2, BATCHES)

        @block.vector
        def _(dve):
            for x in (moments, normed, gap, read, picked, placed):
                x.start(dve)
            chain = Chain(chain_sem, dve, 12)
            nc.vector.memset(seen[0][:, :], 0.0)
            base = k.const[:, C_BASE:C_STEP]
            number = k.const[:, C_EXPERT:C_BASE]

            def step(n, s):
                u = s % 2
                chain.item(n)
                measure(k, chain, n, u, k.stream, moments)
                normalise(k, dve, n, u, k.stream, moments, rooted, normed,
                          lambda: emptied(dve, sent[u], n, s, 16 * per_batch))
                logits.wait(dve, n)
                ins = nc.vector.tensor_copy(logit[u][:, :, :], psL[:, 0:BATCH * EXPERTS].rearrange("p (t e) -> p t e", e=EXPERTS))
                ins.then_inc(read.sem, 1)
                read.wait(dve, n)
                settle(k, dve)
                for t in range(BATCH):
                    last = nc.vector.max(top[u][:, t, :], logit[u][:, t, :])
                chain.link(last)
                settle(k, dve)
                for t in range(BATCH):
                    last = nc.vector.max_index(index[u][:, t, :], top[u][:, t, :], logit[u][:, t, :])
                chain.link(last)
                risen.before(dve, n, 2)
                nc.vector.tensor_tensor(less[u][:, :], top[u][:, :, 1], top[u][:, :, 0], ALU.subtract).then_inc(gap.sem, 1)
                chain.link(nc.vector.tensor_copy(record[u][:, :, 4:6], index[u][:, :, 0:TOPK]))
                chain.link(nc.vector.tensor_tensor(
                    hot[u][:, :, :, :], record[u][:, :, 4:6].unsqueeze(3).to_broadcast([P, BATCH, TOPK, EXPERTS]),
                    number.unsqueeze(1).unsqueeze(1).to_broadcast([P, BATCH, TOPK, EXPERTS]), ALU.is_equal))
                ranked.before(dve, n, 2)
                chain.link(nc.vector.tensor_tensor(both[u][:, :, :], hot[u][:, :, 0, :], hot[u][:, :, 1, :], ALU.add))
                nc.vector.tensor_reduce(four[u][:, :], both[u][:, :, :].rearrange("p t e -> p e t"), X, ALU.add).then_inc(picked.sem, 1)
                risen.wait(dve, n)
                chain.link(nc.vector.tensor_scalar(total[u][:, :], rise[u][:, :], 1.0, None, ALU.add))
                ranked.before(dve, n, 1)
                picked.wait(dve, n)
                nc.vector.tensor_tensor(seen[1 - u][:, :], seen[u][:, :], four[u][:, :], ALU.add)
                chain.link(nc.vector.reciprocal(total[u][:, :], total[u][:, :]))
                chain.link(nc.vector.tensor_scalar(record[u][:, :, 2], total[u][:, :], DEPTH_SCALE, None, ALU.mult))
                nc.vector.tensor_tensor(record[u][:, :, 3], record[u][:, :, 2], rise[u][:, :], ALU.mult)
                ranked.wait(dve, n)
                chain.link(nc.vector.tensor_tensor(
                    rank[u][:, :, :], psR[:, 0:BATCH * EXPERTS].rearrange("p (t e) -> p t e", e=EXPERTS),
                    base.unsqueeze(1).to_broadcast([P, BATCH, EXPERTS]), ALU.add))
                chain.link(nc.vector.tensor_tensor(
                    spot[u][:, :, :, :], hot[u][:, :, :, :],
                    rank[u][:, :, :].unsqueeze(2).to_broadcast([P, BATCH, TOPK, EXPERTS]), ALU.mult))
                chain.link(nc.vector.tensor_reduce(record[u][:, :, 0:TOPK], spot[u][:, :, :, :], X, ALU.add))
                nc.vector.tensor_copy(records[:, bass.ds(n * BATCH, BATCH), :], record[u][:, :, :])
                last = nc.vector.tensor_copy(place[u][:, :, :], record[u][:, :, 0:TOPK])
                last.then_inc(placed.sem, 1)
                chain.close()

            loop(dve, step, 2, 2, BATCHES // 2 - 1, BATCHES)

            links = [0]

            def then(ins):
                ins.then_inc(table_sem, 1)
                links[0] += 1
                dve.wait_ge(table_sem, links[0])

            dve.wait_ge(totals, 1)
            then(nc.vector.tensor_copy(count_i[:, :], psC[:, 0:EXPERTS]))
            then(nc.vector.tensor_scalar(tiles_i[:, :], count_i[:, :], P - 1, None, ALU.add))
            then(nc.vector.tensor_scalar(tiles_i[:, :], tiles_i[:, :], 7, None, ALU.arith_shift_right))
            then(nc.vector.tensor_copy(tiles_f[:, :], tiles_i[:, :]))
            nc.vector.tensor_scalar(jump[:, :], tiles_f[:, :], -float(P), float(REGION), ALU.mult, ALU.add)
            then(nc.vector.tensor_tensor_scan(upto[:, :], tiles_f[:, :], k.zeros[:, 0:EXPERTS], 0.0, ALU.add, ALU.add))
            steps = k.const[0:1, C_STEP:C_ROOT]
            wide = [1, STEPS, EXPERTS]
            then(nc.vector.tensor_tensor(past[:, :, :], steps.unsqueeze(2).to_broadcast(wide),
                                         upto[0:1, :].unsqueeze(1).to_broadcast(wide), ALU.is_ge))
            then(nc.vector.tensor_tensor(far[:, :, :], past[:, :, :], jump[0:1, :].unsqueeze(1).to_broadcast(wide), ALU.mult))
            nc.vector.tensor_reduce(row_f[:, :], far[:, :, :], X, ALU.add)
            then(nc.vector.tensor_reduce(expert_f[:, :], past[:, :, :], X, ALU.add))
            then(nc.vector.scalar_tensor_tensor(row_f[:, :], steps, float(P), row_f[:, :], ALU.mult, ALU.add))
            nc.vector.tensor_copy(k.table[:, :, 0], row_f[:, :])
            nc.vector.tensor_scalar(k.table[:, :, 1], expert_f[:, :], float(EXPERTS - 1), None, ALU.min)
            then(nc.vector.tensor_tensor(shift[:, :], upto[:, :], tiles_f[:, :], ALU.subtract))
            then(nc.vector.scalar_tensor_tensor(shift[:, :], shift[:, :], float(P), base, ALU.mult, ALU.subtract))
            whole = [P, TILES * TOPK, EXPERTS]
            for j in range(TOPK):
                last = nc.vector.tensor_tensor(
                    hots[:, j * TILES:(j + 1) * TILES, :], records[:, :, 4 + j].unsqueeze(2).to_broadcast([P, TILES, EXPERTS]),
                    number.unsqueeze(1).to_broadcast([P, TILES, EXPERTS]), ALU.is_equal)
            then(last)
            then(nc.vector.tensor_tensor(hots[:, :, :], hots[:, :, :], shift[:, :].unsqueeze(1).to_broadcast(whole), ALU.mult))
            then(nc.vector.tensor_reduce(moves[:, :], hots[:, :, :], X, ALU.add))
            for j in range(TOPK):
                last = nc.vector.tensor_tensor(records[:, :, j], records[:, :, j], moves[:, j * TILES:(j + 1) * TILES], ALU.add)
            last.then_inc(settled, 1)


def experts(k, d, layer):
    nc = k.nc
    tag = "ab"[layer]
    sem = lambda name, per=1: Signal(k.sem(f"moe_{tag}_{name}"), per)
    turned, high, low, gated, upped, glowing, hidden = (sem(x) for x in ("turned", "high", "low", "gated", "upped", "glowing", "hidden"))
    crossed, crossed_copied, downed, out_ready = sem("crossed"), sem("crossed_copied"), sem("downed"), sem("out_ready")
    loaded = [k.sem(f"moe_{tag}_loaded{u}") for u in range(2)]
    stored = [k.sem(f"moe_{tag}_stored{u}") for u in range(2)]
    psG, psU = k.bank[0:2], k.bank[2:4]
    psH, psX, psY = k.bank[4], k.bank[5:7], k.bank[7]
    FIRST, PASSES = 4, (STEPS - 6) // 2
    with ExitStack() as ctx:
        sb = lambda name, shape, dt=F32: ctx.enter_context(nc.sbuf_tensor(f"moe_{tag}_{name}", shape, dt))
        rows = [sb(f"rows{u}", [P, D]) for u in range(2)]
        hi = [sb(f"hi{u}", [P, P], F32R) for u in range(2)]
        lo = [sb(f"lo{u}", [P, P], F32R) for u in range(2)]
        glow = [sb(f"glow{u}", [P, HIDDEN]) for u in range(2)]
        hid = [sb(f"hid{u}", [P, HIDDEN]) for u in range(2)]
        hidT = [sb(f"hidT{u}", [P, HIDDEN]) for u in range(2)]
        out = [sb(f"out{u}", [P, D]) for u in range(2)]
        block = ctx.enter_context(nc.Block())

        @block.sync
        def _(sp):
            def step(n, s):
                u = s % 2
                row = sp.value_load(k.table[0:1, bass.ds(n, 1), 0:1].rearrange("p a c -> p (a c)"), min_val=0, max_val=REGION_ROWS - P)
                if s >= 2:
                    turned.before(sp, n, 2)
                sp.dma_start(rows[u][:, :], d.routed[bass.ds(row, P), :]).then_inc(loaded[u], 16)

            loop(sp, step, FIRST, 2, PASSES, STEPS)

        @block.gpsimd
        def _(pool):
            def step(n, s):
                u = s % 2
                out_ready.wait(pool, n)
                settle(k, pool)
                pool.dma_start(d.expert[bass.ds(n * P, P), :], out[u][:, :]).then_inc(stored[u], 16)

            loop(pool, step, FIRST, 2, PASSES, STEPS)
            for u in range(2):
                pool.wait_ge(stored[u], 16 * STEPS // 2)

        @block.tensor
        def _(pe):
            for x in (turned, gated, upped, crossed, downed):
                x.start(pe)

            def turn(n, s):
                u = s % 2
                pe.wait_ge(loaded[u], (n - s % 2) * 8 + 16)
                low.before(pe, n, 2)
                nc.tensor.transpose(psX[u][:, 0:P], rows[u][:, :], k.ident).then_inc(turned.sem, 1)

            def up(n, s):
                u = s % 2
                e = pe.value_load(k.table[0:1, bass.ds(n, 1), 1:2].rearrange("p a c -> p (a c)"), min_val=0, max_val=EXPERTS - 1)
                w = lambda j, part: k.wgu[:, bass.ds(e, 1), j, part, :].rearrange("p a c -> p (a c)")
                high.wait(pe, n)
                low.wait(pe, n)
                for j, (ps, free, done) in enumerate(((psG, glowing, gated), (psU, hidden, upped))):
                    free.before(pe, n, 2)
                    for i, (x, part) in enumerate(((hi, 0), (hi, 1), (lo, 0))):
                        last = nc.tensor.matmul(ps[u][:, :], x[u][:, :], w(j, part), start=i == 0, stop=i == 2)
                    last.then_inc(done.sem, 1)

            def cross(n, s):
                u = s % 2
                hidden.wait(pe, n)
                crossed_copied.before(pe, n, 1)
                for c in range(CHUNKS):
                    last = nc.tensor.transpose(psH[:, c * P:(c + 1) * P], hid[u][:, c * P:(c + 1) * P], k.ident)
                last.then_inc(crossed.sem, 1)

            def down(n, s):
                u = s % 2
                e = pe.value_load(k.table[0:1, bass.ds(n, 1), 1:2].rearrange("p a c -> p (a c)"), min_val=0, max_val=EXPERTS - 1)
                crossed_copied.wait(pe, n)
                out_ready.before(pe, n, 1)
                for c in range(CHUNKS):
                    last = nc.tensor.matmul(psY[:, 0:D], hidT[u][:, c * P:(c + 1) * P],
                                            k.wd[:, bass.ds(e, 1), c, :].rearrange("p a c -> p (a c)"),
                                            start=c == 0, stop=c == CHUNKS - 1)
                last.then_inc(downed.sem, 1)

            turn(0, 0)
            turn(1, 1)

            def step(n, s):
                if s < STEPS:
                    up(n, s)
                if 1 <= s < STEPS + 1:
                    cross(n - 1, s - 1)
                if s + 2 < STEPS:
                    turn(n + 2, s)
                if s >= 2:
                    down(n - 2, s)

            loop(pe, step, FIRST, 2, PASSES, STEPS + 2)

        @block.scalar
        def _(act):
            for x in (high, glowing, crossed_copied):
                x.start(act)

            def halve(n, s):
                u = s % 2
                turned.wait(act, n)
                upped.before(act, n, 2)
                nc.scalar.activation(hi[u][:, :], psX[u][:, 0:P], ACT.Copy).then_inc(high.sem, 1)

            halve(0, 0)
            halve(1, 1)

            def step(n, s):
                if s < STEPS:
                    gated.wait(act, n)
                    hidden.before(act, n, 2)
                    nc.scalar.activation(glow[s % 2][:, :], psG[s % 2][:, :], ACT.Silu).then_inc(glowing.sem, 1)
                if s >= 1:
                    m, u = n - 1, (s - 1) % 2
                    crossed.wait(act, m)
                    downed.before(act, m, 2)
                    nc.scalar.activation(hidT[u][:, :], psH[:, :], ACT.Copy).then_inc(crossed_copied.sem, 1)
                if s + 2 < STEPS:
                    halve(n + 2, s)

            loop(act, step, FIRST, 2, PASSES, STEPS + 1)

        @block.vector
        def _(dve):
            for x in (low, hidden, out_ready):
                x.start(dve)

            def halve(n, s):
                u = s % 2
                high.wait(dve, n)
                upped.before(dve, n, 2)
                nc.vector.tensor_tensor(lo[u][:, :], psX[u][:, 0:P], hi[u][:, :].bitcast(F32), ALU.subtract).then_inc(low.sem, 1)

            def give(n, s):
                u = s % 2
                downed.wait(dve, n)
                emptied(dve, stored[u], n, s, 16)
                nc.vector.tensor_copy(out[u][:, :], psY[:, 0:D]).then_inc(out_ready.sem, 1)

            halve(0, 0)

            def step(n, s):
                u = s % 2
                if s + 1 < STEPS:
                    halve(n + 1, s + 1)
                if s < STEPS:
                    upped.wait(dve, n)
                    glowing.wait(dve, n)
                    crossed.before(dve, n, 2)
                    nc.vector.tensor_tensor(hid[u][:, :], psU[u][:, :], glow[u][:, :], ALU.mult).then_inc(hidden.sem, 1)
                if s >= 2:
                    give(n - 2, s - 2)

            loop(dve, step, FIRST, 2, PASSES, STEPS + 2)


def combine(k, d, layer):
    nc = k.nc
    tag = "ab"[layer]
    last_layer = layer == 1
    sem = lambda name, per=1: Signal(k.sem(f"join_{tag}_{name}"), per)
    placed, first, joined = sem("placed"), sem("first"), sem("joined")
    loaded = [k.sem(f"join_{tag}_loaded{u}") for u in range(4)]
    fetched = [k.sem(f"join_{tag}_fetched{u}") for u in range(4)]
    stored = [k.sem(f"join_{tag}_stored{u}") for u in range(4)]
    by_position = lambda ap, n: ap.rearrange("(s b) c -> b s c", s=ROWS)[bass.ds(n * (P // ROWS), P // ROWS), :, :]
    with ExitStack() as ctx:
        sb = lambda name, shape, dt=F32: ctx.enter_context(nc.sbuf_tensor(f"join_{tag}_{name}", shape, dt))
        kept = [sb(f"kept{u}", [P, D]) for u in range(4)]
        record = [sb(f"record{u}", [P, 4]) for u in range(4)]
        place = [sb(f"place{u}", [P, TOPK], U32) for u in range(4)]
        got = [sb(f"got{u}", [P, TOPK, D]) for u in range(4)]
        block = ctx.enter_context(nc.Block())

        @block.sync
        def _(sp):
            def step(n, s):
                u = s % 4
                if last_layer:
                    at = bass.ds(n * P, P)
                    src = [(kept[u], d.kept[at, :]), (record[u], d.route[at, :])]
                else:
                    src = [(kept[u], by_position(d.kept, n)), (record[u], by_position(d.route, n))]
                if s >= 4:
                    sp.wait_ge(joined.sem, n - 1)
                if last_layer and s >= 4:
                    sp.wait_ge(stored[u], (n - s % 4) * 4)
                for dst, ap in src:
                    sp.dma_start(dst[:, :], ap).then_inc(loaded[u], 16)

            loop(sp, step, 4, 4, (TILES - 4) // 4, TILES)

        if last_layer:
            @block.scalar
            def _(act):
                def step(n, s):
                    u = s % 4
                    joined.wait(act, n)
                    act.dma_start(by_position(d.out, n), kept[u][:, :]).then_inc(stored[u], 16)

                loop(act, step, 0, 4, TILES // 4, TILES)
                for u in range(4):
                    act.wait_ge(stored[u], 16 * TILES // 4)

        @block.gpsimd
        def _(pool):
            def step(n, s):
                u = s % 4
                placed.wait(pool, n)
                if s >= 4:
                    pool.wait_ge(joined.sem, n - 1)
                settle(k, pool)
                for j in range(TOPK):
                    pool.indirect_dma_start(got[u][:, j, :], None, d.expert[:, :],
                                            bass.IndirectOffsetOnAxis(ap=place[u][:, j:j + 1], axis=0)).then_inc(fetched[u], 16)

            loop(pool, step, 4, 4, (TILES - 4) // 4, TILES)

        @block.vector
        def _(dve):
            for x in (placed, first, joined):
                x.start(dve)

            def ready(n, s):
                u = s % 4
                dve.wait_ge(loaded[u], (n - s % 4) * 8 + 32)
                nc.vector.tensor_copy(place[u][:, :], record[u][:, 0:TOPK]).then_inc(placed.sem, 1)

            def join(n, s):
                u = s % 4
                dve.wait_ge(fetched[u], (n - s % 4) * 8 + 32)
                nc.vector.scalar_tensor_tensor(kept[u][:, :], got[u][:, 0, :], record[u][:, 2:3], kept[u][:, :],
                                               ALU.mult, ALU.add).then_inc(first.sem, 1)
                first.wait(dve, n)
                to = kept[u][:, :] if last_layer else k.stream[:, bass.ds(n, 1), :].rearrange("p a c -> p (a c)")
                nc.vector.scalar_tensor_tensor(to, got[u][:, 1, :], record[u][:, 3:4], kept[u][:, :],
                                               ALU.mult, ALU.add).then_inc(joined.sem, 1)

            def step(n, s):
                if s < TILES:
                    ready(n, s)
                if s >= 2:
                    join(n - 2, s - 2)

            loop(dve, step, 4, 4, (TILES - 4) // 4, TILES + 2)



def finish(k):
    k.nc.clear_and_free_semaphores(k.used)
    k.used = []
    k.nc.all_engine_barrier()


def build(nc, d):
    with ExitStack() as ctx:
        k = allocate(nc, ctx)
        stages = [(setup,), (project, 0), (attend, 0), (route, 0), (experts, 0), (combine, 0),
                  (project, 1), (attend, 1), (route, 1), (experts, 1), (combine, 1)]
        for stage, *half in stages:
            stage(k, d, *half)
            finish(k)


class Arrays:
    pass


_P = "L0_attn_a_", "L0_attn_b_", "L0_ffn_"


def kernel(**inputs):
    import numpy as _np
    import concourse.bacc as _bacc
    from concourse import mybir as _mybir
    from concourse.bass_utils import run_bass_kernel_spmd as _run

    a, b, f = ({n[len(p):]: _np.asarray(v) for n, v in inputs.items() if n.startswith(p)} for p in _P)
    E_ = D
    wq, wk, wv = (b["in_proj_w"][j * E_:(j + 1) * E_].T for j in range(3))
    bq, bk, bv = (b["in_proj_b"][j * E_:(j + 1) * E_] for j in range(3))
    order = lambda w: w.reshape(*w.shape[:-1], HEADS // 2, 2, HD).swapaxes(-3, -1).swapaxes(-3, -2).reshape(w.shape)
    given = {
        "x": a["x"].reshape(TOKENS, D),
        "w_split": _np.stack([order(a["Wq"]), order(a["Wk"]), b["w_tor"], order(wq), order(wk), wv]),
        "wv": a["Wv"], "wout": b["out_w"].T, "wr": f["Wr"],
        "cols": _np.stack([order(a["bq"]), order(a["bk"]), b["b_tor"], order(bq), order(bk)], axis=1),
        "rows": _np.stack([a["bv"], bv, b["out_b"]]),
        "wg": f["Wg"], "wu": f["Wu"], "wd": f["Wd"],
        "const": constants(),
    }
    nc = _bacc.Bacc("TRN2", target_bir_lowering=False, num_devices=1)
    d, arrays = Arrays(), {}
    ap = {}
    for name, v in given.items():
        v = _np.ascontiguousarray(v)
        arrays[f"in_{name}"] = v
        ap[name] = nc.dram_tensor(f"in_{name}", v.shape, _mybir.dt.from_np(v.dtype), kind="ExternalInput").ap()
    d.x, d.w_split, d.wout, d.wr, d.cols, d.rows = (ap[n] for n in ("x", "w_split", "wout", "wr", "cols", "rows"))
    d.wv, d.wg, d.wu, d.wd, d.const = ap["wv"], ap["wg"], ap["wu"], ap["wd"], ap["const"]
    scratch = lambda name, shape, dt: nc.dram_tensor(name, shape, dt).ap()
    d.parts = scratch("parts", (2, BATCHES, 2, 3, HD, HEADS // 2, TB), BF16)
    d.v = scratch("v_rows", (TOKENS, D), F32)
    d.routed = scratch("routed", (REGION_ROWS, D), F32)
    d.expert = scratch("expert_out", (STEPS * P, D), F32)
    d.kept = scratch("kept", (TOKENS, D), F32)
    d.route = scratch("route", (TOKENS, 4), F32)
    d.out = nc.dram_tensor("out", (TOKENS, D), _mybir.dt.float32, kind="ExternalOutput").ap()
    build(nc, d)
    r = _run(nc, [arrays], core_ids=[0])
    return _np.asarray(r.results[0]["out"]).reshape(ROWS, POSITIONS, D)
```

```python
from contextlib import ExitStack

import numpy as np
import concourse.bass as bass
from concourse import mybir

F32 = mybir.dt.float32
F32R = mybir.dt.float32r
BF16 = mybir.dt.bfloat16
I32 = mybir.dt.int32
U32 = mybir.dt.uint32
ALU = mybir.AluOpType
ACT = mybir.ActivationFunctionType
X = mybir.AxisListType.X

P = 128
ROWS, POSITIONS, D = 16, 256, 128
TOKENS = ROWS * POSITIONS
TILES = TOKENS // P
HEADS, HD = 16, 8
SCALE = 1.0 / float(np.sqrt(np.float32(HD)))
EPS = 1e-5
BATCH = 4
TB = BATCH * P
BATCHES = TILES // BATCH
SLOTS = 6
STACK = SLOTS * HD
EXPERTS, HIDDEN, TOPK = 8, 512, 2
CHUNKS = HIDDEN // P
DEPTH_SCALE = float(1.0 / np.sqrt(12))
REGION = TOKENS + P
STEPS = 72
SPARE = STEPS - TOPK * TOKENS // P
REGION_ROWS = EXPERTS * REGION + SPARE * P

C_IDENT, C_UPPER, C_BIAS, C_EXPERT, C_BASE, C_STEP, C_ROOT, C_TOKEN, C_TAIL, C_END = (int(x) for x in np.cumsum(
    [0, P, P, 32, EXPERTS, EXPERTS, STEPS, 1, TILES, EXPERTS + SPARE]))
ROW = D + 2


def constants():
    c = np.zeros((P, C_END), np.float32)
    p = np.arange(P)
    c[:, C_IDENT:C_UPPER] = np.eye(P)
    c[:, C_UPPER:C_BIAS] = p[:, None] < p[None, :]
    key = np.arange(32)
    same = (p[:, None] // 16) % 2 == key[None, :] // 16
    turn = (key[None, :] % 16 - p[:, None] % 16) % 16
    near = (turn == 0).astype(np.float32) + (turn == 1) + (turn == 15)
    c[:, C_BIAS:C_EXPERT] = np.where(same, near, np.float32(-1e30))
    c[:, C_EXPERT:C_BASE] = np.arange(EXPERTS)
    c[:, C_BASE:C_STEP] = np.arange(EXPERTS) * REGION
    c[:, C_STEP:C_ROOT] = np.arange(STEPS)
    c[:, C_ROOT] = -0.5
    c[:, C_TOKEN:C_TAIL] = 2 * (np.arange(TILES) * P + p[:, None])
    c[:, C_TAIL:] = 2 * (TOKENS + np.arange(EXPERTS + SPARE) * P + p[:, None])
    return c


class Signal:

    def __init__(self, sem, per=1):
        self.sem, self.per = sem, per

    def start(self, eng):
        eng.sem_inc(self.sem, 2 * self.per)

    def wait(self, eng, n, part=None):
        eng.wait_ge(self.sem, n * self.per + (2 * self.per + (self.per if part is None else part)))

    def before(self, eng, n, back):
        eng.wait_ge(self.sem, n * self.per + (3 - back) * self.per)


class Chain:

    def __init__(self, sem, eng, per):
        self.sem, self.eng, self.per = sem, eng, per
        self.count = 0

    def item(self, n, count=0):
        self.n, self.count = n, count

    def link(self, ins):
        ins.then_inc(self.sem, 1)
        self.count += 1
        self.eng.wait_ge(self.sem, self.n * self.per + self.count)

    def close(self):
        assert self.count == self.per, (self.count, self.per)


def settle(k, eng):
    eng.sem_inc(k.idle, 1)


def emptied(eng, sem, n, s, per):
    if s >= 2:
        eng.wait_ge(sem, (n - s % 2) * (per // 2))


def group_loop(eng, step, first, passes, end, group):
    for t in range(first):
        step(t, t, t // group, t // group)
    with eng.Fori(0, passes) as i:
        for v in range(2 * group):
            s = first + v
            step(i * (2 * group) + s, s, i * 2 + s // group, s // group)
    for t in range(first + 2 * group * passes, end):
        step(t, t, t // group, t // group)


def group_of(s, q, r, lag, group):
    back = s // group - (s - lag) // group
    return (q - back if back else q), r - back


def loop(eng, step, first, unroll, passes, end):
    for t in range(first):
        step(t, t)
    if passes:
        with eng.Fori(0, passes) as i:
            for v in range(unroll):
                step(i * unroll + (first + v), first + v)
    for t in range(first + unroll * passes, end):
        step(t, t)


class Kernel:
    pass


def allocate(nc, ctx):
    k = Kernel()
    k.nc = nc

    def sb(name, shape, dt=F32):
        return ctx.enter_context(nc.sbuf_tensor(name, shape, dt))

    k.idle = ctx.enter_context(nc.semaphore("idle"))
    k.used = []

    def sem(name):
        k.used.append(nc.alloc_semaphore(name))
        return k.used[-1]

    k.sem = sem
    k.bank = [ctx.enter_context(nc.psum_tensor(f"bank{i}", [P, 512], F32)) for i in range(8)]
    k.stream = sb("stream", [P, TILES, D])
    k.const = sb("const", [P, C_END])
    k.ident = k.const[:, C_IDENT:C_UPPER]
    k.upper = sb("upper", [P, P], BF16)
    k.ones = sb("ones", [P, P], BF16)
    k.tails = sb("tails", [P, EXPERTS, ROW])
    k.step_expert = sb("step_expert", [P, STEPS])
    k.table = sb("table", [1, STEPS, 2], I32)
    k.split = sb("split", [P, 4, 2, D], F32R)
    k.wv = [sb("wv_a", [P, D]), sb("wv_b", [P, D])]
    k.wout = sb("wout", [P, D])
    k.wr = sb("wr", [P, EXPERTS])
    k.cols = sb("cols", [P, 4])
    k.rows = sb("rows", [P, 3, D])
    k.wgu = sb("wgu", [P, EXPERTS, 2, 2, HIDDEN], F32R)
    k.wd = sb("wd", [P, EXPERTS, CHUNKS, D])
    k.norm_x = [sb(f"norm_x{u}", [P, BATCH, ROW]) for u in range(2)]
    k.stats = [sb(f"stats{u}", [P, BATCH, 6]) for u in range(2)]
    k.moments = [sb(f"moments{u}", [P, BATCH, 2]) for u in range(2)]
    k.rstd = [sb(f"rstd{u}", [P, BATCH]) for u in range(2)]
    k.xT = [sb(f"xT{u}", [P, TB]) for u in range(2)]
    return k


def setup(k, d):
    nc = k.nc
    loaded, staged, folded, whole_ready, cleared = (
        k.sem(f"setup_{x}") for x in ("loaded", "staged", "folded", "whole", "cleared"))
    TORUS, Q, K, V = 2, 3, 4, 5
    with ExitStack() as ctx:
        sb = lambda name, shape: ctx.enter_context(nc.sbuf_tensor(f"setup_{name}", shape, F32))
        raw = sb("raw", [P, 6, D])
        whole = sb("whole", [P, 4, D])
        cols = sb("cols", [P, 5])
        spread = sb("spread", [P, P])
        spare = sb("spare", [P, SPARE, ROW])
        block = ctx.enter_context(nc.Block())
        fixed = [(raw[:, :, :], d.w_split.rearrange("w c f -> c w f")), (cols[:, :], d.cols),
                 (k.const[:, :], d.const[:, :]),
                 (k.stream[:, :, :], d.x.rearrange("(t p) c -> p t c", p=P)),
                 (k.wv[0][:, :], d.wv), (k.wout[:, :], d.wout), (k.wr[:, :], d.wr)]
        psF, psB = k.bank[0], k.bank[1]

        @block.sync
        def _(sp):
            for r in range(3):
                sp.dma_start(k.rows[:, r, :], d.rows[r:r + 1, :].to_broadcast([P, D])).then_inc(loaded, 16)
            for dst, src in fixed:
                sp.dma_start(dst, src).then_inc(loaded, 16)
            sp.wait_ge(whole_ready, 1)
            for j in range(SPARE):
                sp.dma_start(d.routed[EXPERTS * REGION + j * P:EXPERTS * REGION + (j + 1) * P, :],
                             spare[:, j, :]).then_inc(cleared, 16)
            sp.wait_ge(loaded, 16 * (len(fixed) + 3))
            sp.wait_ge(cleared, 16 * SPARE)

        @block.tensor
        def _(pe):
            pe.wait_ge(staged, 2)
            nc.tensor.matmul(psF[:, 0:3 * D], raw[:, TORUS, :], raw[:, Q:V + 1, :], start=True, stop=True)
            for j, w in enumerate((Q, K)):
                nc.tensor.matmul(psB[:, j:j + 1], raw[:, w, :], cols[:, TORUS:TORUS + 1], start=True, stop=True)
            nc.tensor.matmul(psB[:, P:2 * P], spread[:, :], raw[:, V, :], start=True, stop=True).then_inc(folded, 1)

        @block.vector
        def _(dve):
            nc.vector.memset(k.ones[:, :], 1.0)
            for rows in (k.tails, spare):
                nc.vector.memset(rows[:, :, 0:D], 0.0)
                last = nc.vector.memset(rows[:, :, D + 1], -1.0)
            last.then_inc(staged, 1)
            dve.wait_ge(loaded, 16 * (len(fixed) + 3))
            nc.vector.tensor_copy(spread[:, :], cols[:, TORUS:TORUS + 1].to_broadcast([P, P])).then_inc(staged, 1)
            nc.vector.tensor_copy(k.upper[:, :], k.const[:, C_UPPER:C_BIAS])
            nc.vector.tensor_copy(k.tails[:, :, D], k.const[:, C_TAIL:C_TAIL + EXPERTS])
            nc.vector.tensor_copy(spare[:, :, D], k.const[:, C_TAIL + EXPERTS:C_END])
            nc.vector.tensor_scalar(whole[:, 0, :], raw[:, 0, :], SCALE, None, ALU.mult)
            nc.vector.tensor_copy(whole[:, 1, :], raw[:, 1, :])
            nc.vector.tensor_scalar(k.cols[:, 0:1], cols[:, 0:1], SCALE, None, ALU.mult)
            nc.vector.tensor_copy(k.cols[:, 1:2], cols[:, 1:2])
            dve.wait_ge(folded, 1)
            nc.vector.tensor_scalar(whole[:, 2, :], psF[:, 0:D], SCALE, None, ALU.mult)
            nc.vector.tensor_copy(whole[:, 3, :], psF[:, D:2 * D]).then_inc(whole_ready, 1)
            nc.vector.tensor_copy(k.wv[1][:, :].rearrange("p (g i e) -> p g i e", g=4, e=HD),
                                  psF[:, 2 * D:3 * D].rearrange("p (i g e) -> p g i e", g=4, e=HD))
            nc.vector.tensor_tensor(k.rows[:, 1, :], k.rows[:, 1, :], psB[:, P:2 * P], ALU.add)
            nc.vector.tensor_scalar(k.cols[:, 2:3], psB[:, 0:1], cols[:, Q:Q + 1], SCALE, ALU.add, ALU.mult)
            nc.vector.tensor_tensor(k.cols[:, 3:4], psB[:, 1:2], cols[:, K:K + 1], ALU.add)
            dve.wait_ge(whole_ready, 1)
            nc.vector.tensor_copy(k.split[:, :, 0, :], whole[:, :, :]).then_inc(whole_ready, 1)
            dve.wait_ge(whole_ready, 2)
            nc.vector.tensor_tensor(k.split[:, :, 1, :], whole[:, :, :], k.split[:, :, 0, :].bitcast(F32), ALU.subtract)


def measure(k, chain, n, u, moments, many=BATCH):
    nc = k.nc
    for t in range(many):
        last = nc.vector.bn_stats(k.stats[u][:, t, :], k.stream[:, bass.ds(n * many + t, 1), :].rearrange("p a c -> p (a c)"))
    chain.link(last)
    settle(k, chain.eng)
    for t in range(many):
        last = nc.vector.bn_aggr(k.moments[u][:, t, :], k.stats[u][:, t, :])
    last.then_inc(moments.sem, 1)


def normalise(k, dve, n, u, rooted, ready, many=BATCH, free=None):
    nc = k.nc
    rooted.wait(dve, n)
    if free:
        free()
    for t in range(many):
        last = nc.vector.tensor_scalar(
            k.norm_x[u][:, t, 0:D], k.stream[:, bass.ds(n * many + t, 1), :].rearrange("p a c -> p (a c)"),
            k.moments[u][:, t, 0:1], k.rstd[u][:, t:t + 1], ALU.subtract, ALU.mult)
    last.then_inc(ready.sem, 1)


def root_of_variance(k, pool, n, u, moments, rooted, many=BATCH):
    moments.wait(pool, n)
    settle(k, pool)
    rstd = k.rstd[u][:, 0:many]
    k.nc.gpsimd.tensor_scalar(rstd, k.moments[u][:, 0:many, 1], EPS, None, ALU.add).then_inc(rooted.sem, 1)
    rooted.wait(pool, n, 1)
    k.nc.gpsimd.tensor_tensor(rstd, rstd, k.const[:, C_ROOT:C_TOKEN].to_broadcast([P, many]), ALU.pow).then_inc(rooted.sem, 1)


def project(k, d, half):
    nc = k.nc
    tag = "ab"[half]
    prepare = half == 0
    COUPLE = 2
    TC = COUPLE * P
    ITEMS = TILES // COUPLE
    FIRST, END = 8, ITEMS + 4
    PASSES = (ITEMS - FIRST) // 4
    assert 2 * EXPERTS == ITEMS
    sem = lambda name, per=1: Signal(k.sem(f"proj_{tag}_{name}"), per)
    normed, turned, copied, high, low = (sem(x) for x in ("normed", "turned", "copied", "high", "low"))
    moments, rooted = sem("moments"), sem("rooted", 2)
    q_ready, k_ready, v_ready, v_out = sem("q"), sem("k"), sem("v"), sem("v_out")
    part0, rest1, part1, part2 = sem("part0", 2), sem("rest1", 2), sem("part1"), sem("part2")
    stored = [k.sem(f"proj_{tag}_stored{u}") for u in range(4)]
    staged = [k.sem(f"proj_{tag}_staged{u}") for u in range(2)] if prepare else None
    wd_loaded = k.sem(f"proj_{tag}_wd")
    ones_there = k.sem(f"proj_{tag}_ones")
    weights_high, weights_low = sem("weights_high"), sem("weights_low")
    chain_sem = k.sem(f"proj_{tag}_chain")
    stores = 3
    psT, psq, psk, psv = (k.bank[2 * j:2 * j + 2] for j in range(4))
    with ExitStack() as ctx:
        sb = lambda name, shape, dt=F32: ctx.enter_context(nc.sbuf_tensor(f"proj_{tag}_{name}", shape, dt))
        hi = [sb(f"hi{u}", [P, TC], F32R) for u in range(2)]
        lo = [sb(f"lo{u}", [P, TC], F32R) for u in range(2)]
        rest = [sb(f"rest{u}", [P, 2, TC]) for u in range(2)]
        parts = [sb(f"parts{u}", [P, 3, 2, TC], BF16) for u in range(4)]
        v = [sb(f"v{u}", [P, COUPLE, HEADS, HD + 1]) for u in range(4)]
        stage = [sb(f"stage{u}", [P, HIDDEN]) for u in range(2)] if prepare else None
        block = ctx.enter_context(nc.Block())
        bias = lambda side: k.cols[:, 2 * half + side:2 * half + side + 1]
        inside = lambda s, lag: 0 <= s - lag < ITEMS
        weights = lambda q, s, part: k.wgu[:, bass.ds(q, 1), s % 2, part, :].rearrange("p a h -> p (a h)")

        @block.sync
        def _(sp):
            def step(n, s, q, r):
                if prepare and inside(s, 0):
                    if s >= 2:
                        weights_low.before(sp, n, 2)
                        settle(k, sp)
                    sp.dma_start(stage[s % 2][:, :], (d.wg, d.wu)[s % 2][bass.ds(q, 1), :, :].rearrange("a c h -> (a c) h"))\
                        .then_inc(staged[s % 2], 16)
                if inside(s, 5):
                    m, u = n - 5, (s - 5) % 4
                    v_out.wait(sp, m)
                    settle(k, sp)
                    sp.dma_start(d.v[bass.ds(m * TC, TC), :].rearrange("(t p) c -> p t c", p=P),
                                 v[u][:, :, :, :].rearrange("p t h e -> p t (h e)")).then_inc(stored[u], 16)
                    part2.wait(sp, m)
                    settle(k, sp)
                    at = bass.ds(group_of(s, q, r, 5, 2)[0], 1)
                    for side in range(2):
                        sp.dma_start(d.parts[side, at, :, :, (s - 5) % 2 * TC:((s - 5) % 2 + 1) * TC].rearrange("m j f t -> f (m j) t"),
                                     parts[u][:, :, side, :]).then_inc(stored[u], 16)

            group_loop(sp, step, FIRST, PASSES, END + 1, 2)
            if prepare:
                sp.dma_start(k.wd[:, :, :, :], d.wd.rearrange("e (j p) c -> p e j c", p=P)).then_inc(wd_loaded, 16)
                sp.wait_ge(wd_loaded, 16)
            for u in range(4):
                sp.wait_ge(stored[u], 16 * stores * ITEMS // 4)

        @block.vector
        def _(dve):
            chain = Chain(chain_sem, dve, 1)
            for x in (moments, normed, high, rest1, weights_low):
                x.start(dve)

            def step(n, s, q, r):
                if inside(s, 0):
                    chain.item(n)
                    measure(k, chain, n, s % 2, moments, COUPLE)
                    chain.close()
                if inside(s, 2):
                    copied.wait(dve, n - 2)
                    nc.vector.tensor_copy(hi[s % 2][:, :], k.xT[s % 2][:, 0:TC]).then_inc(high.sem, 1)
                if inside(s, 3):
                    m, u = n - 3, (s - 3) % 2
                    part2.before(dve, m, 2)
                    for side, ps in enumerate((psq, psk)):
                        part0.wait(dve, m, side + 1)
                        nc.vector.scalar_tensor_tensor(
                            rest[u][:, side, :], ps[u][:, 0:TC], bias(side),
                            parts[(s - 3) % 4][:, 0, side, :], ALU.add, ALU.subtract).then_inc(rest1.sem, 1)
                if inside(s, 1):
                    normalise(k, dve, n - 1, (s - 1) % 2, rooted, normed, COUPLE, lambda: turned.before(dve, n - 1, 2))
                if prepare and inside(s, 0):
                    weights_high.wait(dve, n)
                    nc.vector.tensor_tensor(weights(q, s, 1), stage[s % 2][:, :], weights(q, s, 0).bitcast(F32),
                                            ALU.subtract).then_inc(weights_low.sem, 1)

            group_loop(dve, step, FIRST, PASSES, END, 2)

        @block.scalar
        def _(act):
            for x in (copied, part0, v_out, part1, weights_high):
                x.start(act)
            act.wait_ge(ones_there, 1)

            def step(n, s, q, r):
                if inside(s, 2):
                    turned.wait(act, n - 2)
                    low.before(act, n - 2, 2)
                    nc.scalar.activation(k.xT[s % 2][:, 0:TC], psT[s % 2][:, 0:TC], ACT.Copy).then_inc(copied.sem, 1)
                if inside(s, 3):
                    m, u = n - 3, (s - 3) % 2
                    b = (s - 3) % 4
                    if s - 3 >= 4:
                        act.wait_ge(stored[b], (m - b) * (4 * stores))
                    for side, (ps, ready) in enumerate(((psq, q_ready), (psk, k_ready))):
                        ready.wait(act, m)
                        nc.scalar.activation(parts[b][:, 0, side, :], ps[u][:, 0:TC], ACT.Identity, bias=bias(side))\
                            .then_inc(part0.sem, 1)
                    v_ready.wait(act, m)
                    nc.scalar.activation(v[b][:, :, :, 0:HD], psv[u][:, 0:TC].rearrange("p (t h e) -> p t h e", h=HEADS, e=HD),
                                         ACT.Copy).then_inc(v_out.sem, 1)
                if prepare and inside(s, 0):
                    act.wait_ge(staged[s % 2], (n - s % 2) * 8 + 16)
                    nc.scalar.activation(weights(q, s, 0), stage[s % 2][:, :], ACT.Copy).then_inc(weights_high.sem, 1)
                if inside(s, 4):
                    u, b = s % 2, s % 4
                    rest1.wait(act, n - 4)
                    nc.scalar.activation(parts[b][:, 1, :, :], rest[u][:, :, :], ACT.Copy).then_inc(part1.sem, 1)

            group_loop(act, step, FIRST, PASSES, END, 2)

        @block.gpsimd
        def _(pool):
            for x in (rooted, low, part2):
                x.start(pool)
            for u in range(4):
                last = nc.gpsimd.memset(v[u][:, :, :, :], 1.0)
            last.then_inc(ones_there, 1)

            def step(n, s, q, r):
                if inside(s, 0):
                    root_of_variance(k, pool, n, s % 2, moments, rooted, COUPLE)
                if inside(s, 2):
                    u = s % 2
                    high.wait(pool, n - 2)
                    nc.gpsimd.tensor_tensor(lo[u][:, :], k.xT[u][:, 0:TC], hi[u][:, :].bitcast(F32), ALU.subtract).then_inc(low.sem, 1)
                if inside(s, 4):
                    u, b = s % 2, s % 4
                    part1.wait(pool, n - 4)
                    nc.gpsimd.tensor_tensor(parts[b][:, 2, :, :], rest[u][:, :, :],
                                            parts[b][:, 1, :, :], ALU.subtract).then_inc(part2.sem, 1)

            group_loop(pool, step, FIRST, PASSES, END, 2)

        @block.tensor
        def _(pe):
            for x in (turned, q_ready, k_ready, v_ready):
                x.start(pe)

            def step(n, s, q, r):
                if inside(s, 2):
                    m, u = n - 2, s % 2
                    normed.wait(pe, m)
                    copied.before(pe, m, 2)
                    for t in range(COUPLE):
                        last = nc.tensor.transpose(psT[u][:, t * P:(t + 1) * P], k.norm_x[u][:, t, 0:D], k.ident)
                    last.then_inc(turned.sem, 1)
                if inside(s, 3):
                    m, u = n - 3, (s - 3) % 2
                    low.wait(pe, m)
                    rest1.before(pe, m, 2)
                    for w, (ps, ready) in enumerate(((psq, q_ready), (psk, k_ready))):
                        for j, (a, b) in enumerate(((0, hi), (1, hi), (0, lo))):
                            last = nc.tensor.matmul(ps[u][:, 0:TC], k.split[:, 2 * half + w, a, :], b[u][:, :], start=j == 0, stop=j == 2)
                        last.then_inc(ready.sem, 1)
                    v_out.before(pe, m, 2)
                    for t in range(COUPLE):
                        last = nc.tensor.matmul(psv[u][:, t * D:(t + 1) * D], k.xT[u][:, t * P:(t + 1) * P],
                                                k.wv[half][:, :], start=True, stop=True)
                    last.then_inc(v_ready.sem, 1)

            group_loop(pe, step, FIRST, PASSES, END, 2)


class Router:

    LAG = 7
    FIRST = 16
    PASSES = (TILES - FIRST) // 8
    END = TILES + LAG + 4

    def __init__(self, k, d, layer, ps, final):
        nc = self.nc = k.nc
        self.k, self.d, self.ps, self.final = k, d, ps, final
        self.tag = tag = "ab"[layer]
        sem = lambda name, per=1: Signal(k.sem(f"route_{tag}_{name}"), per)
        self.normed, self.turned, self.copied, self.moments, self.rooted = (
            sem("normed"), sem("turned"), sem("copied"), sem("moments"), sem("rooted", 2))
        self.logits, self.gap, self.risen, self.picked, self.ranked, self.placed, self.read = (
            sem(x) for x in ("logits", "gap", "risen", "picked", "ranked", "placed", "read"))
        self.sent = [k.sem(f"route_{tag}_sent{u}") for u in range(2)]
        self.kept, chain_sem, self.table_sem, self.totals, self.tails = (
            k.sem(f"route_{tag}_{x}") for x in ("kept", "chain", "table", "totals", "tails"))
        self.chain_sem = chain_sem

    def allocate(self, ctx, spare):
        self.row_f = spare[:, 0:STEPS]
        nc, tag = self.nc, self.tag
        sb = lambda name, shape, dt=F32: ctx.enter_context(nc.sbuf_tensor(f"route_{tag}_{name}", shape, dt))
        two = lambda name, shape, dt=F32: [sb(f"{name}{u}", shape, dt) for u in range(2)]
        self.logit = two("logit", [P, BATCH, EXPERTS])
        self.top = two("top", [P, BATCH, 8])
        self.index = two("index", [P, BATCH, 8], U32)
        self.less, self.rise, self.total = two("less", [P, BATCH]), two("rise", [P, BATCH]), two("total", [P, BATCH])
        self.hot = two("hot", [P, BATCH, TOPK, EXPERTS])
        self.both = two("both", [P, BATCH, EXPERTS], BF16)
        self.seen = two("seen", [P, EXPERTS], BF16)
        self.four = two("four", [P, EXPERTS])
        self.rank = two("rank", [P, BATCH, EXPERTS])
        self.spot = two("spot", [P, BATCH, TOPK, EXPERTS])
        self.record = two("record", [P, BATCH, 6])
        self.place = two("place", [P, BATCH, TOPK], U32)
        self.weights = sb("weights", [P, TILES, TOPK])
        self.count_i, self.tiles_i = sb("count_i", [P, EXPERTS], I32), sb("tiles_i", [P, EXPERTS], I32)
        self.tiles_f, self.upto, self.jump = (sb(x, [P, EXPERTS]) for x in ("tiles_f", "upto", "jump"))
        self.past = sb("past", [P, STEPS, EXPERTS])

    def piece(self, s, q, r, lag):
        if (s - lag) % BATCH or not 0 <= (s - lag) // BATCH < BATCHES:
            return None
        return group_of(s, q, r, lag, BATCH)

    def keep(self, sp, n, s):
        sp.wait_ge(self.final.sem, n * BATCH + (2 + BATCH))
        settle(self.k, sp)
        sp.dma_start(self.d.kept[bass.ds(n * TB, TB), 0:D].rearrange("(t p) c -> p t c", p=P),
                     self.k.stream[:, bass.ds(n * BATCH, BATCH), :]).then_inc(self.kept, 16)

    def finish_sync(self, sp):
        k, d = self.k, self.d
        sp.wait_ge(self.table_sem, 1)
        for e in range(EXPERTS):
            end = sp.value_load(self.count_i[0:1, e:e + 1], min_val=0, max_val=TOKENS)
            sp.dma_start(d.routed[bass.ds(end + e * REGION, P), :], k.tails[:, e, :]).then_inc(self.tails, 16)
        sp.dma_start(d.kept[:, D:ROW].rearrange("(t p) c -> p t c", p=P), self.weights[:, :, :]).then_inc(self.tails, 16)
        sp.wait_ge(self.tails, 16 * (EXPERTS + 1))
        sp.wait_ge(self.kept, 16 * BATCHES)

    def start_pool(self, pool):
        self.rooted.start(pool)

    def pool(self, pool, s, q, r):
        at = self.piece(s, q, r, self.LAG)
        if at:
            root_of_variance(self.k, pool, at[0], at[1] % 2, self.moments, self.rooted)
        for t in range(BATCH):
            at = self.piece(s, q, r, self.LAG + 4 + t)
            if at:
                n, u = at[0], at[1] % 2
                self.placed.wait(pool, n)
                settle(self.k, pool)
                for j in range(TOPK):
                    pool.indirect_dma_start(
                        self.d.routed[:, :], bass.IndirectOffsetOnAxis(ap=self.place[u][:, t, j:j + 1], axis=0),
                        self.k.norm_x[u][:, t, :], None).then_inc(self.sent[u], 16)

    def finish_pool(self, pool):
        for u in range(2):
            pool.wait_ge(self.sent[u], 16 * TOPK * TILES // 2)

    def start_tensor(self, pe):
        for x in (self.turned, self.logits, self.ranked):
            x.start(pe)

    def tensor(self, pe, s, q, r):
        k, nc, ps = self.k, self.nc, self.ps
        at = self.piece(s, q, r, self.LAG + 4)
        if at:
            n, u = at[0], at[1] % 2
            self.picked.wait(pe, n)
            for t in range(BATCH):
                out = ps[:, t * EXPERTS:(t + 1) * EXPERTS]
                nc.tensor.matmul(out, k.upper[:, :], self.both[u][:, t, :], start=True, stop=False)
                for e in range(t):
                    nc.tensor.matmul(out, k.ones[:, :], self.both[u][:, e, :], start=False, stop=False)
                last = nc.tensor.matmul(out, k.ones[:, :], self.seen[u][:, :], start=False, stop=True)
            last.then_inc(self.ranked.sem, 1)
        at = self.piece(s, q, r, self.LAG + 2)
        if at:
            n, u = at[0], at[1] % 2
            self.normed.wait(pe, n)
            self.placed.before(pe, n, 1)
            for t in range(BATCH):
                last = nc.tensor.transpose(ps[:, t * P:(t + 1) * P], k.norm_x[u][:, t, 0:D], k.ident)
            last.then_inc(self.turned.sem, 1)

        at = self.piece(s, q, r, self.LAG + 3)
        if at:
            n, u = at[0], at[1] % 2
            self.copied.wait(pe, n)
            for t in range(BATCH):
                last = nc.tensor.matmul(ps[:, t * EXPERTS:(t + 1) * EXPERTS], k.xT[u][:, t * P:(t + 1) * P],
                                        k.wr[:, :], start=True, stop=True)
            last.then_inc(self.logits.sem, 1)

    def finish_tensor(self, pe):
        self.placed.wait(pe, BATCHES - 1)
        self.nc.tensor.matmul(self.ps[:, 0:EXPERTS], self.k.ones[:, :], self.seen[BATCHES % 2][:, :],
                              start=True, stop=True).then_inc(self.totals, 1)

    def start_scalar(self, act):
        for x in (self.copied, self.risen):
            x.start(act)

    def scalar(self, act, s, q, r):
        k, nc = self.k, self.nc
        at = self.piece(s, q, r, self.LAG + 2)
        if at:
            n, u = at[0], at[1] % 2
            self.turned.wait(act, n)
            nc.scalar.activation(k.xT[u][:, :], self.ps[:, :], ACT.Copy).then_inc(self.copied.sem, 1)
        at = self.piece(s, q, r, self.LAG + 4)
        if at:
            n, u = at[0], at[1] % 2
            self.gap.wait(act, n)
            nc.scalar.activation(self.rise[u][:, :], self.less[u][:, :], ACT.Exp).then_inc(self.risen.sem, 1)

    def start_vector(self, dve):
        for x in (self.moments, self.normed, self.gap, self.read, self.picked, self.placed):
            x.start(dve)
        self.chain = Chain(self.chain_sem, dve, 12)
        self.nc.vector.memset(self.seen[0][:, :], 0.0)

    def take_moments(self, dve, s, q, r):
        at = self.piece(s, q, r, self.LAG)
        if at:
            n = at[0]
            self.chain.item(n)
            dve.wait_ge(self.final.sem, n * BATCH + (2 + BATCH))
            settle(self.k, dve)
            measure(self.k, self.chain, n, at[1] % 2, self.moments)

    def vector(self, dve, s, q, r):
        k, nc, chain, ps = self.k, self.nc, self.chain, self.ps
        number = k.const[:, C_EXPERT:C_BASE]
        base = k.const[:, C_BASE:C_STEP]
        at = self.piece(s, q, r, self.LAG + 1)
        if at:
            normalise(k, dve, at[0], at[1] % 2, self.rooted, self.normed, BATCH,
                      lambda: emptied(dve, self.sent[at[1] % 2], *at, 16 * TOPK * BATCH))
        at = self.piece(s, q, r, self.LAG + 3)
        if at:
            n, u = at[0], at[1] % 2
            logit, top, index, record, hot, both = (x[u] for x in (self.logit, self.top, self.index, self.record, self.hot, self.both))
            chain.item(n, 1)
            self.logits.wait(dve, n)
            nc.vector.tensor_copy(logit[:, :, :], ps[:, 0:BATCH * EXPERTS].rearrange("p (t e) -> p t e", e=EXPERTS))\
                .then_inc(self.read.sem, 1)
            self.read.wait(dve, n)
            settle(k, dve)
            for t in range(BATCH):
                last = nc.vector.max(top[:, t, :], logit[:, t, :])
            chain.link(last)
            settle(k, dve)
            for t in range(BATCH):
                last = nc.vector.max_index(index[:, t, :], top[:, t, :], logit[:, t, :])
            chain.link(last)
            nc.vector.tensor_tensor(self.less[u][:, :], top[:, :, 1], top[:, :, 0], ALU.subtract).then_inc(self.gap.sem, 1)
            chain.link(nc.vector.tensor_copy(record[:, :, 4:6], index[:, :, 0:TOPK]))
            chain.link(nc.vector.tensor_tensor(
                hot[:, :, :, :], record[:, :, 4:6].unsqueeze(3).to_broadcast([P, BATCH, TOPK, EXPERTS]),
                number.unsqueeze(1).unsqueeze(1).to_broadcast([P, BATCH, TOPK, EXPERTS]), ALU.is_equal))
            chain.link(nc.vector.tensor_tensor(both[:, :, :], hot[:, :, 0, :], hot[:, :, 1, :], ALU.add))
            nc.vector.tensor_reduce(self.four[u][:, :], both[:, :, :].rearrange("p t e -> p e t"), X, ALU.add)\
                .then_inc(self.picked.sem, 1)
            self.ranked.before(dve, n, 1)
            self.picked.wait(dve, n)
            nc.vector.tensor_tensor(self.seen[1 - u][:, :], self.seen[u][:, :], self.four[u][:, :], ALU.add)
        at = self.piece(s, q, r, self.LAG + 4)
        if at:
            n, u = at[0], at[1] % 2
            record, total, rise, rank, spot = (x[u] for x in (self.record, self.total, self.rise, self.rank, self.spot))
            chain.item(n, 6)
            self.risen.wait(dve, n)
            chain.link(nc.vector.tensor_scalar(total[:, :], rise[:, :], 1.0, None, ALU.add))
            chain.link(nc.vector.reciprocal(total[:, :], total[:, :]))
            chain.link(nc.vector.tensor_scalar(record[:, :, 2], total[:, :], DEPTH_SCALE, None, ALU.mult))
            nc.vector.tensor_tensor(record[:, :, 3], record[:, :, 2], rise[:, :], ALU.mult)
            self.ranked.wait(dve, n)
            chain.link(nc.vector.tensor_tensor(
                rank[:, :, :], ps[:, 0:BATCH * EXPERTS].rearrange("p (t e) -> p t e", e=EXPERTS),
                base.unsqueeze(1).to_broadcast([P, BATCH, EXPERTS]), ALU.add))
            chain.link(nc.vector.tensor_tensor(
                spot[:, :, :, :], self.hot[u][:, :, :, :],
                rank[:, :, :].unsqueeze(2).to_broadcast([P, BATCH, TOPK, EXPERTS]), ALU.mult))
            chain.link(nc.vector.tensor_reduce(record[:, :, 0:TOPK], spot[:, :, :, :], X, ALU.add))
            nc.vector.tensor_copy(self.weights[:, bass.ds(n * BATCH, BATCH), :], record[:, :, 2:4])
            nc.vector.tensor_copy(k.norm_x[u][:, :, D], k.const[:, bass.ds(n * BATCH + C_TOKEN, BATCH)])
            nc.vector.tensor_copy(k.norm_x[u][:, :, D + 1], record[:, :, 4])
            nc.vector.tensor_copy(self.place[u][:, :, :], record[:, :, 0:TOPK]).then_inc(self.placed.sem, 1)
            chain.close()

    def finish_vector(self, dve):
        k, nc = self.k, self.nc
        links = [0]

        def then(ins):
            ins.then_inc(self.table_sem, 1)
            links[0] += 1
            dve.wait_ge(self.table_sem, links[0])

        dve.wait_ge(self.totals, 1)
        then(nc.vector.tensor_copy(self.count_i[:, :], self.ps[:, 0:EXPERTS]))
        then(nc.vector.tensor_scalar(self.tiles_i[:, :], self.count_i[:, :], P - 1, None, ALU.add))
        then(nc.vector.tensor_scalar(self.tiles_i[:, :], self.tiles_i[:, :], 7, None, ALU.arith_shift_right))
        then(nc.vector.tensor_copy(self.tiles_f[:, :], self.tiles_i[:, :]))
        nc.vector.tensor_scalar(self.jump[:, :], self.tiles_f[:, :], -float(P), float(REGION), ALU.mult, ALU.add)
        then(nc.vector.tensor_tensor_scan(self.upto[:, :], self.tiles_f[:, :], k.tails[:, 0, 0:EXPERTS], 0.0, ALU.add, ALU.add))
        steps = k.const[:, C_STEP:C_ROOT]
        wide = [P, STEPS, EXPERTS]
        then(nc.vector.tensor_tensor(self.past[:, :, :], steps.unsqueeze(2).to_broadcast(wide),
                                     self.upto[:, :].unsqueeze(1).to_broadcast(wide), ALU.is_ge))
        then(nc.vector.tensor_reduce(k.step_expert[:, :], self.past[:, :, :], X, ALU.add))
        then(nc.vector.tensor_tensor(self.past[:, :, :], self.past[:, :, :], self.jump[:, :].unsqueeze(1).to_broadcast(wide), ALU.mult))
        then(nc.vector.tensor_reduce(self.row_f[:, :], self.past[:, :, :], X, ALU.add))
        then(nc.vector.scalar_tensor_tensor(self.row_f[:, :], steps, float(P), self.row_f[:, :], ALU.mult, ALU.add))
        nc.vector.tensor_copy(k.table[:, :, 0], self.row_f[0:1, :])
        nc.vector.tensor_scalar(k.table[:, :, 1], k.step_expert[0:1, :], float(EXPERTS - 1), None, ALU.min)


def attend(k, d, half):
    nc = k.nc
    tag = "ab"[half]
    second = half == 1
    blk = 32 if second else 64
    nb = P // blk
    group = P // blk
    rounds = HEADS // 2
    turns = HEADS // group
    banks = HEADS * blk // 512
    lane = 64 if second else 32
    stacked = 64 + STACK
    sem = lambda name, per=1: Signal(k.sem(f"att_{tag}_{name}"), per)
    scored, shifted, risen = sem("scored"), sem("shifted"), sem("risen")
    turned, turned_copied = sem("turned"), sem("turned_copied", 2)
    mixed, mixed_copied, flipped = sem("mixed"), sem("mixed_copied"), sem("flipped")
    even, summed, based, standing = sem("even"), sem("summed"), sem("based"), sem("standing")
    cleared = k.sem(f"att_{tag}_cleared")
    back, back_copied, mapped, mapped_added = sem("back"), sem("back_copied"), sem("mapped"), sem("mapped_added")
    loaded = [k.sem(f"att_{tag}_loaded{u}") for u in range(2)]
    chain_sem = k.sem(f"att_{tag}_chain")
    pool_sem = k.sem(f"att_{tag}_pool")
    loads = 12 + group
    psS = [k.bank[banks * u:banks * (u + 1)] for u in range(2)]
    psP = k.bank[4:6]
    psO = k.bank[6]
    psE, psR = (k.bank[7], k.bank[5]) if second else (None, k.bank[7])
    final = mapped_added if second else summed
    route = Router(k, d, half, psR, final)
    with ExitStack() as ctx:
        sb = lambda name, shape, dt=F32: ctx.enter_context(nc.sbuf_tensor(f"att_{tag}_{name}", shape, dt))
        qs = [sb(f"q{m}", [P, rounds, TB], BF16) for m in range(2)]
        ks = [sb(f"k{m}", [P, 2, rounds, TB], BF16) for m in range(2)]
        vx = [sb(f"v{m}", [P, BATCH * nb, group, turns * (HD + 1)]) for m in range(2)]
        stand = [sb(f"stand{u}", [P, nb, turns, group * (HD + 1)]) for u in range(2)]
        prob = [sb(f"prob{u}", [P, HEADS, blk]) for u in range(2)]
        probT = [sb(f"probT{u}", [P, turns, P]) for u in range(2)]
        most = [sb(f"most{u}", [P, HEADS]) for u in range(2)]
        inv = [sb(f"inv{u}", [P, HEADS]) for u in range(2)]
        side = [sb(f"side{u}", [P, 2 * P]) for u in range(2)]
        mix = [sb(f"mix{u}", [P, D]) for u in range(2)]
        base = [sb(f"base{u}", [P, D]) for u in range(2)]
        mixT = [sb(f"mixT{u}", [P, P]) for u in range(2)]
        route.allocate(ctx, side[0])
        block = ctx.enter_context(nc.Block())
        last_step = 4 if second else 3

        def scores(u, a):
            return psS[u][a][:, :].rearrange("p (h c) -> p h c", c=blk)

        def heads(a):
            return slice(a * HEADS // banks, (a + 1) * HEADS // banks)

        @block.sync
        def _(sp):
            def step(m, s):
                v = s % 2
                if s >= 2:
                    sp.wait_ge(mixed.sem, m * BATCH + (2 - BATCH))
                at = bass.ds(m * TB, TB)
                for a in range(2):
                    q_part, k_part = (d.parts[j, bass.ds(m, 1), :, 64 * a:64 * (a + 1), :]
                                      .rearrange("m j (e h) t -> (m j) e (h t)", e=HD) for j in range(2))
                    for j, (slot, many) in enumerate(((0, 3), (3, 2), (5, 1))):
                        to = slice(64 * a + slot * HD, 64 * a + (slot + many) * HD)
                        sp.dma_start(qs[v][to, :, :], q_part[j:j + 1].to_broadcast([many, HD, rounds * TB])).then_inc(loaded[v], 16)
                        sp.dma_start(ks[v][to, a, :, :], k_part[0:many]).then_inc(loaded[v], 16)
                for g in range(group):
                    src = d.v[at, :].rearrange("(b q) (g c) -> g q b c", q=blk, g=group)[g]
                    sp.dma_start(vx[v][blk * g:blk * (g + 1), :, g, :], src).then_inc(loaded[v], 16)

            sp.wait_ge(cleared, 4)
            step(0, 0)
            step(1, 1)

            def later(m, s):
                step(m, s)
                route.keep(sp, m - 2, s - 2)

            with sp.Fori(0, BATCHES // 2 - 1) as i:
                for v in range(2):
                    later(i * 2 + (2 + v), 2 + v)
            for m in range(BATCHES - 2, BATCHES):
                route.keep(sp, m, m)
            route.finish_sync(sp)

        def batch_loaded(eng, n, s):
            eng.wait_ge(loaded[s // BATCH % 2], (n - s % 8) * (2 * loads) + 16 * loads)

        @block.gpsimd
        def _(pool):
            for x in (summed, based):
                x.start(pool)
            route.start_pool(pool)
            for m in range(2):
                last = nc.gpsimd.memset(vx[m][:, :, :, :], 0.0)
            last.then_inc(cleared, 1)
            nc.gpsimd.memset(ks[1][:, :, :, :].bitcast(F32), 0.0).then_inc(cleared, 1)
            chain = Chain(pool_sem, pool, 1)

            def step(n, s, q, r):
                if 3 <= s < TILES + 3:
                    m, u = n - 3, (s - 3) % 2
                    tile = k.stream[:, bass.ds(m, 1), :].rearrange("p a c -> p (a c)")
                    if second:
                        even.wait(pool, m)
                        nc.gpsimd.tensor_tensor(mix[u][:, :], mix[u][:, :], k.rows[:, 1, :], ALU.add).then_inc(summed.sem, 1)
                        mapped_added.before(pool, m, 2)
                        settle(k, pool)
                        nc.gpsimd.tensor_tensor(base[u][:, :], tile, k.rows[:, 2, :], ALU.add).then_inc(based.sem, 1)
                    else:
                        chain.item(m)
                        chain.link(nc.gpsimd.tensor_tensor(base[u][:, :], tile, k.rows[:, 0, :], ALU.add))
                        even.wait(pool, m)
                        settle(k, pool)
                        nc.gpsimd.tensor_tensor(tile, mix[u][:, :], base[u][:, :], ALU.add).then_inc(summed.sem, 1)
                route.pool(pool, s, q, r)

            group_loop(pool, step, route.FIRST, route.PASSES, route.END, BATCH)
            route.finish_pool(pool)

        @block.tensor
        def _(pe):
            for x in (scored, turned, mixed, flipped, back, mapped):
                x.start(pe)
            pe.wait_ge(cleared, 4)

            def score(n, s):
                batch_loaded(pe, n, s)
                shifted.before(pe, n, 2)
                settle(k, pe)
                u, v = s % 2, s // BATCH % 2
                for h in range(rounds):
                    bank, c = divmod(h * 2 * blk, 512)
                    for b in range(nb):
                        at = slice((s % BATCH) * P + b * blk, (s % BATCH) * P + (b + 1) * blk)
                        last = nc.tensor.matmul(psS[u][bank][b * blk:(b + 1) * blk, c:c + 2 * blk],
                                                qs[v][0:stacked, h, at], ks[v][0:stacked, :, h, at], start=True, stop=True,
                                                tile_position=(0, b * blk))
                last.then_inc(scored.sem, 1)

            def mixing(n, s):
                u = s % 2
                turned_copied.wait(pe, n)
                standing.wait(pe, n)
                even.before(pe, n, 1)
                for i in range(turns):
                    lanes, c = i % (P // lane), i // (P // lane)
                    for b in range(nb):
                        last = nc.tensor.matmul(
                            psO[lanes * lane:lanes * lane + group * (HD + 1), c * P + b * blk:c * P + (b + 1) * blk],
                            stand[u][:, b, i, :],
                            probT[u][:, i, b * blk:(b + 1) * blk], start=True, stop=True, tile_position=(0, lanes * lane))
                last.then_inc(mixed.sem, 1)

            def flip(n, s):
                mixed_copied.wait(pe, n)
                for c in range(2):
                    last = nc.tensor.transpose(psO[:, (2 + c) * P:(3 + c) * P], side[s % 2][:, c * P:(c + 1) * P], k.ident)
                last.then_inc(flipped.sem, 1)

            def turn(n, s):
                u = s % 2
                risen.wait(pe, n)
                turned_copied.before(pe, n, 1)
                for i in range(turns):
                    last = nc.tensor.transpose(psP[i // 4][:, (i % 4) * P:(i % 4 + 1) * P],
                                               prob[u][:, i * group:(i + 1) * group, :].rearrange("p h c -> p (h c)"), k.ident)
                last.then_inc(turned.sem, 1)

            def turn_back(n, s):
                summed.wait(pe, n)
                back_copied.before(pe, n, 1)
                mapped_added.before(pe, n, 1)
                nc.tensor.transpose(psE[:, 0:P], mix[s % 2][:, :], k.ident).then_inc(back.sem, 1)

            def map_out(n, s):
                back_copied.wait(pe, n)
                nc.tensor.matmul(psE[:, P:2 * P], mixT[s % 2][:, :], k.wout[:, :], start=True, stop=True).then_inc(mapped.sem, 1)

            def step(n, s, q, r):
                if s < TILES:
                    score(n, s)
                if 3 <= s < TILES + 3:
                    flip(n - 3, s - 3)
                if second and 4 <= s < TILES + 4:
                    turn_back(n - 4, s - 4)
                if 1 <= s < TILES + 1:
                    turn(n - 1, s - 1)
                route.tensor(pe, s, q, r)
                if 2 <= s < TILES + 2:
                    mixing(n - 2, s - 2)
                if second and 4 <= s < TILES + 4:
                    map_out(n - 4, s - 4)

            route.start_tensor(pe)
            group_loop(pe, step, route.FIRST, route.PASSES, route.END, BATCH)
            route.finish_tensor(pe)

        @block.vector
        def _(dve):
            for x in (shifted, even, mapped_added):
                x.start(dve)
            for m in range(2):
                nc.vector.memset(qs[m][32:64, :, :].bitcast(F32), 0.0)
            nc.vector.memset(psO[:, :], 0.0)
            nc.vector.memset(ks[0][:, :, :, :].bitcast(F32), 0.0).then_inc(cleared, 2)
            chain = Chain(chain_sem, dve, 3 if second else 2)
            bias = k.const[:, C_BIAS:C_EXPERT].unsqueeze(1).to_broadcast([P, HEADS // banks, blk]) if second else None

            def soften(n, s):
                u = s % 2
                scored.wait(dve, n)
                if second:
                    turned.before(dve, n, 2)
                    for a in range(banks):
                        last = nc.vector.tensor_tensor(prob[u][:, heads(a), :], scores(u, a), bias, ALU.add)
                    chain.link(last)
                    chain.link(nc.vector.tensor_reduce(most[u][:, :], prob[u][:, :, :], X, ALU.max))
                    nc.vector.tensor_tensor(prob[u][:, :, :], prob[u][:, :, :],
                                            most[u][:, :].unsqueeze(2).to_broadcast([P, HEADS, blk]), ALU.subtract)\
                        .then_inc(shifted.sem, 1)
                else:
                    for a in range(banks):
                        last = nc.vector.tensor_reduce(most[u][:, heads(a)], scores(u, a), X, ALU.max)
                    chain.link(last)
                    turned.before(dve, n, 2)
                    for a in range(banks):
                        last = nc.vector.tensor_tensor(
                            prob[u][:, heads(a), :], scores(u, a),
                            most[u][:, heads(a)].unsqueeze(2).to_broadcast([P, HEADS // banks, blk]), ALU.subtract)
                    last.then_inc(shifted.sem, 1)

            def divide(n, s):
                u = s % 2
                flipped.wait(dve, n)
                out = psO[:, 2 * P:4 * P].rearrange("p (i w) -> p i w", w=lane)[:, :, 0:group * (HD + 1)]\
                    .rearrange("p i (g e) -> p i g e", e=HD + 1)
                inverse = inv[u][:, :].rearrange("p (i g) -> p i g", g=group)
                chain.link(nc.vector.reciprocal(inverse, out[:, :, :, HD]))
                if second:
                    back.before(dve, n, 2)
                else:
                    summed.before(dve, n, 2)
                nc.vector.tensor_tensor(mix[u][:, :].rearrange("p (i g e) -> p i g e", g=group, e=HD), out[:, :, :, 0:HD],
                                        inverse.unsqueeze(3).to_broadcast([P, turns, group, HD]), ALU.mult).then_inc(even.sem, 1)

            def add_map(n, s):
                mapped.wait(dve, n)
                based.wait(dve, n)
                nc.vector.tensor_tensor(k.stream[:, bass.ds(n, 1), :].rearrange("p a c -> p (a c)"), psE[:, P:2 * P],
                                        base[s % 2][:, :], ALU.add).then_inc(mapped_added.sem, 1)

            def step(n, s, q, r):
                chain.item(n)
                if 3 <= s < TILES + 3:
                    divide(n - 3, s - 3)
                if s < TILES:
                    soften(n, s)
                for _ in range(chain.per - chain.count):
                    dve.sem_inc(chain_sem, 1)
                route.vector(dve, s, q, r)
                if second and 4 <= s < TILES + 4:
                    add_map(n - 4, s - 4)
                route.take_moments(dve, s, q, r)

            route.start_vector(dve)
            group_loop(dve, step, route.FIRST, route.PASSES, route.END, BATCH)
            route.finish_vector(dve)

        @block.scalar
        def _(act):
            for x in (risen, turned_copied, mixed_copied, back_copied, standing):
                x.start(act)

            def step(n, s, q, r):
                if 3 <= s < TILES + 3:
                    m, u = n - 3, (s - 3) % 2
                    mixed.wait(act, m)
                    flipped.before(act, m, 2)
                    nc.scalar.activation(side[u][:, :], psO[:, 0:2 * P], ACT.Copy).then_inc(mixed_copied.sem, 1)
                if second and 4 <= s < TILES + 4:
                    m, u = n - 4, s % 2
                    back.wait(act, m)
                    nc.scalar.activation(mixT[u][:, :], psE[:, 0:P], ACT.Copy).then_inc(back_copied.sem, 1)
                if 1 <= s < TILES + 1:
                    m, u = n - 1, (s - 1) % 2
                    batch_loaded(act, m, s - 1)
                    mixed.before(act, m, 2)
                    at = (s - 1) % BATCH * nb
                    for g in range(group):
                        last = nc.scalar.activation(
                            stand[u][:, :, :, g * (HD + 1):(g + 1) * (HD + 1)],
                            vx[(s - 1) // BATCH % 2][:, at:at + nb, g, :].rearrange("p b (i e) -> p b i e", e=HD + 1), ACT.Copy)
                    last.then_inc(standing.sem, 1)
                    turned.wait(act, m)
                    half_turns = turns // 2
                    for j in range(2):
                        b, c = (j, 0) if turns == 8 else (0, j * half_turns * P)
                        nc.scalar.activation(probT[u][:, j * half_turns:(j + 1) * half_turns, :].rearrange("p i t -> p (i t)"),
                                             psP[b][:, c:c + half_turns * P], ACT.Copy).then_inc(turned_copied.sem, 1)
                route.scalar(act, s, q, r)
                if s < TILES:
                    shifted.wait(act, n)
                    nc.scalar.activation(prob[s % 2][:, :, :], prob[s % 2][:, :, :], ACT.Exp).then_inc(risen.sem, 1)

            route.start_scalar(act)
            group_loop(act, step, route.FIRST, route.PASSES, route.END, BATCH)


def experts(k, d, layer):
    nc = k.nc
    tag = "ab"[layer]
    sem = lambda name, per=1: Signal(k.sem(f"moe_{tag}_{name}"), per)
    turned, high, low, gated, upped, glowing, hidden = (sem(x) for x in ("turned", "high", "low", "gated", "upped", "glowing", "hidden"))
    crossed, crossed_copied, downed, out_ready = sem("crossed"), sem("crossed_copied"), sem("downed"), sem("out_ready")
    loaded = [k.sem(f"moe_{tag}_loaded{u}") for u in range(4)]
    placed = sem("placed")
    stored = [k.sem(f"moe_{tag}_stored{u}") for u in range(2)]
    psG, psU = k.bank[0:2], k.bank[2:4]
    psH, psX, psY = k.bank[4], k.bank[5:7], k.bank[7]
    FIRST, PASSES = 4, (STEPS - 6) // 4
    with ExitStack() as ctx:
        sb = lambda name, shape, dt=F32: ctx.enter_context(nc.sbuf_tensor(f"moe_{tag}_{name}", shape, dt))
        rows = [sb(f"rows{u}", [P, ROW]) for u in range(4)]
        place = [sb(f"place{u}", [P, 1], U32) for u in range(4)]
        hi = [sb(f"hi{u}", [P, P], F32R) for u in range(2)]
        lo = [sb(f"lo{u}", [P, P], F32R) for u in range(2)]
        glow = [sb(f"glow{u}", [P, HIDDEN]) for u in range(2)]
        hid = [sb(f"hid{u}", [P, HIDDEN]) for u in range(2)]
        hidT = [sb(f"hidT{u}", [P, HIDDEN]) for u in range(2)]
        out = [sb(f"out{u}", [P, D]) for u in range(2)]
        block = ctx.enter_context(nc.Block())

        @block.sync
        def _(sp):
            def step(n, s):
                row = sp.value_load(k.table[0:1, bass.ds(n, 1), 0:1].rearrange("p a c -> p (a c)"), min_val=0, max_val=REGION_ROWS - P)
                if s >= 4:
                    sp.wait_ge(placed.sem, n - 1)
                    settle(k, sp)
                u = s % 4
                sp.dma_start(rows[u][:, :], d.routed[bass.ds(row, P), :]).then_inc(loaded[u], 16)

            loop(sp, step, FIRST, 4, PASSES, STEPS)

        @block.gpsimd
        def _(pool):
            def step(n, s):
                u = s % 2
                out_ready.wait(pool, n)
                settle(k, pool)
                pool.indirect_dma_start(d.expert[:, :], bass.IndirectOffsetOnAxis(ap=place[s % 4][:, 0:1], axis=0),
                                        out[u][:, :], None).then_inc(stored[u], 16)

            loop(pool, step, FIRST, 4, PASSES, STEPS)
            for u in range(2):
                pool.wait_ge(stored[u], 16 * STEPS // 2)

        @block.tensor
        def _(pe):
            for x in (turned, gated, upped, crossed, downed):
                x.start(pe)

            def turn(n, s):
                u = s % 2
                pe.wait_ge(loaded[s % 4], (n - s % 4) * 4 + 16)
                low.before(pe, n, 2)
                nc.tensor.transpose(psX[u][:, 0:P], rows[s % 4][:, 0:D], k.ident).then_inc(turned.sem, 1)

            def up(n, s):
                u = s % 2
                e = pe.value_load(k.table[0:1, bass.ds(n, 1), 1:2].rearrange("p a c -> p (a c)"), min_val=0, max_val=EXPERTS - 1)
                w = lambda j, part: k.wgu[:, bass.ds(e, 1), j, part, :].rearrange("p a c -> p (a c)")
                low.wait(pe, n)
                for j, (ps, done) in enumerate(((psG, gated), (psU, upped))):
                    for i, (x, part) in enumerate(((hi, 0), (hi, 1), (lo, 0))):
                        last = nc.tensor.matmul(ps[u][:, :], x[u][:, :], w(j, part), start=i == 0, stop=i == 2)
                    last.then_inc(done.sem, 1)

            def cross(n, s):
                u = s % 2
                hidden.wait(pe, n)
                crossed_copied.before(pe, n, 1)
                for c in range(CHUNKS):
                    last = nc.tensor.transpose(psH[:, c * P:(c + 1) * P], hid[u][:, c * P:(c + 1) * P], k.ident)
                last.then_inc(crossed.sem, 1)

            def down(n, s):
                u = s % 2
                e = pe.value_load(k.table[0:1, bass.ds(n, 1), 1:2].rearrange("p a c -> p (a c)"), min_val=0, max_val=EXPERTS - 1)
                crossed_copied.wait(pe, n)
                out_ready.before(pe, n, 1)
                for c in range(CHUNKS):
                    last = nc.tensor.matmul(psY[:, 0:D], hidT[u][:, c * P:(c + 1) * P],
                                            k.wd[:, bass.ds(e, 1), c, :].rearrange("p a c -> p (a c)"),
                                            start=c == 0, stop=c == CHUNKS - 1)
                last.then_inc(downed.sem, 1)

            turn(0, 0)
            turn(1, 1)

            def step(n, s):
                if s < STEPS:
                    up(n, s)
                if s + 2 < STEPS:
                    turn(n + 2, s + 2)
                if 1 <= s < STEPS + 1:
                    cross(n - 1, s - 1)
                if s >= 2:
                    down(n - 2, s)

            loop(pe, step, FIRST, 4, PASSES, STEPS + 2)

        @block.scalar
        def _(act):
            for x in (high, glowing, crossed_copied):
                x.start(act)

            def halve(n, s):
                u = s % 2
                turned.wait(act, n)
                nc.scalar.activation(hi[u][:, :], psX[u][:, 0:P], ACT.Copy).then_inc(high.sem, 1)

            halve(0, 0)
            halve(1, 1)

            def step(n, s):
                if s < STEPS:
                    gated.wait(act, n)
                    nc.scalar.activation(glow[s % 2][:, :], psG[s % 2][:, :], ACT.Silu).then_inc(glowing.sem, 1)
                if s + 2 < STEPS:
                    halve(n + 2, s + 2)
                if s >= 1:
                    m, u = n - 1, (s - 1) % 2
                    crossed.wait(act, m)
                    nc.scalar.activation(hidT[u][:, :], psH[:, :], ACT.Copy).then_inc(crossed_copied.sem, 1)

            loop(act, step, FIRST, 4, PASSES, STEPS + 1)

        @block.vector
        def _(dve):
            for x in (low, hidden, out_ready, placed):
                x.start(dve)

            def halve(n, s):
                u = s % 2
                high.wait(dve, n)
                nc.vector.tensor_tensor(lo[u][:, :], psX[u][:, 0:P], hi[u][:, :].bitcast(F32), ALU.subtract).then_inc(low.sem, 1)

            def find_places(n, s):
                v = s % 4
                turned.wait(dve, n)
                if s >= 4:
                    dve.wait_ge(stored[s % 2], (n - s % 2) * 8 - 16)
                settle(k, dve)
                nc.vector.scalar_tensor_tensor(place[v][:, :], rows[v][:, D + 1:ROW], k.step_expert[:, bass.ds(n, 1)],
                                               rows[v][:, D:D + 1], ALU.not_equal, ALU.add).then_inc(placed.sem, 1)

            def give(n, s):
                u = s % 2
                downed.wait(dve, n)
                emptied(dve, stored[u], n, s, 16)
                nc.vector.tensor_copy(out[u][:, :], psY[:, 0:D]).then_inc(out_ready.sem, 1)

            halve(0, 0)
            halve(1, 1)

            def step(n, s):
                u = s % 2
                if s < STEPS:
                    find_places(n, s)
                    upped.wait(dve, n)
                    glowing.wait(dve, n)
                    nc.vector.tensor_tensor(hid[u][:, :], psU[u][:, :], glow[u][:, :], ALU.mult).then_inc(hidden.sem, 1)
                if s + 2 < STEPS:
                    halve(n + 2, s + 2)
                if s >= 2:
                    give(n - 2, s - 2)

            loop(dve, step, FIRST, 4, PASSES, STEPS + 2)


def combine(k, d, layer):
    nc = k.nc
    tag = "ab"[layer]
    last_layer = layer == 1
    first = Signal(k.sem(f"join_{tag}_first"))
    joined = k.sem(f"join_{tag}_joined")
    loaded = [k.sem(f"join_{tag}_loaded{u}") for u in range(4)]
    stored = [k.sem(f"join_{tag}_stored{u}") for u in range(4)]
    crossed = lambda ap, n: ap.rearrange("(s b m t) c -> m b s (t c)", s=ROWS, b=8, t=BATCH)[bass.ds(n, 1)]\
        .rearrange("m b s x -> (m b) s x")
    straight = lambda ap, n: ap[bass.ds(n * TB, TB), :].rearrange("(t p) c -> p t c", p=P)
    with ExitStack() as ctx:
        sb = lambda name, shape, dt=F32: ctx.enter_context(nc.sbuf_tensor(f"join_{tag}_{name}", shape, dt))
        kept = [sb(f"kept{u}", [P, BATCH, ROW]) for u in range(4)]
        outs = [sb(f"outs{u}", [P, BATCH, TOPK * D]) for u in range(4)]
        final = [sb(f"final{u}", [P, BATCH, D]) for u in range(4)] if last_layer else None
        block = ctx.enter_context(nc.Block())

        @block.sync
        def _(sp):
            def step(n, s):
                u = s % 4
                sp.wait_ge(joined, n + 1)
                settle(k, sp)
                for dst, src in ((kept[u], d.kept), (outs[u], d.outputs)):
                    if last_layer:
                        sp.dma_start(dst[:, :, :], straight(src, n)).then_inc(loaded[u], 16)
                    else:
                        sp.dma_start(dst[:, :, :].rearrange("p t c -> p (t c)"), crossed(src, n)).then_inc(loaded[u], 16)

            loop(sp, step, 0, 4, BATCHES // 4, BATCHES)

        if last_layer:
            @block.scalar
            def _(act):
                for u in range(4):
                    act.sem_inc(stored[u], 16)

                def step(n, s):
                    u = s % 4
                    act.wait_ge(joined, n + 5)
                    settle(k, act)
                    act.dma_start(crossed(d.out, n), final[u][:, :, :].rearrange("p t c -> p (t c)")).then_inc(stored[u], 16)

                loop(act, step, 0, 4, BATCHES // 4, BATCHES)
                for u in range(4):
                    act.wait_ge(stored[u], 16 + 16 * BATCHES // 4)

        @block.vector
        def _(dve):
            first.start(dve)
            dve.sem_inc(joined, 4)

            def step(n, s):
                u = s % 4
                dve.wait_ge(loaded[u], (n - s % 4) * 8 + 32)
                for t in range(BATCH):
                    last = nc.vector.scalar_tensor_tensor(kept[u][:, t, 0:D], outs[u][:, t, 0:D], kept[u][:, t, D:D + 1],
                                                          kept[u][:, t, 0:D], ALU.mult, ALU.add)
                last.then_inc(first.sem, 1)
                first.wait(dve, n)
                if last_layer:
                    dve.wait_ge(stored[u], (n - s % 4) * 4 + 16)
                for t in range(BATCH):
                    to = final[u][:, t, :] if last_layer else k.stream[:, bass.ds(n * BATCH + t, 1), :].rearrange("p a c -> p (a c)")
                    last = nc.vector.scalar_tensor_tensor(to, outs[u][:, t, D:2 * D], kept[u][:, t, D + 1:ROW],
                                                          kept[u][:, t, 0:D], ALU.mult, ALU.add)
                last.then_inc(joined, 1)

            loop(dve, step, 0, 4, BATCHES // 4, BATCHES)


def finish(k):
    k.nc.clear_and_free_semaphores(k.used)
    k.used = []
    k.nc.all_engine_barrier()


def build(nc, d):
    with ExitStack() as ctx:
        k = allocate(nc, ctx)
        stages = [(setup,), (project, 0), (attend, 0), (experts, 0), (combine, 0),
                  (project, 1), (attend, 1), (experts, 1), (combine, 1)]
        for stage, *half in stages:
            stage(k, d, *half)
            finish(k)


class Arrays:
    pass


_P = "L0_attn_a_", "L0_attn_b_", "L0_ffn_"


def kernel(**inputs):
    import numpy as _np
    import concourse.bacc as _bacc
    from concourse import mybir as _mybir
    from concourse.bass_utils import run_bass_kernel_spmd as _run

    a, b, f = ({n[len(p):]: _np.asarray(v) for n, v in inputs.items() if n.startswith(p)} for p in _P)
    E_ = D
    wq, wk, wv = (b["in_proj_w"][j * E_:(j + 1) * E_].T for j in range(3))
    bq, bk, bv = (b["in_proj_b"][j * E_:(j + 1) * E_] for j in range(3))
    order = lambda w: w.reshape(*w.shape[:-1], HEADS // 2, 2, HD).swapaxes(-3, -1).swapaxes(-3, -2).reshape(w.shape)
    by_class = lambda w: w.reshape(D, HEADS // 2, 2, HD).transpose(0, 2, 1, 3).reshape(w.shape)
    given = {
        "x": a["x"].reshape(TOKENS, D),
        "w_split": _np.stack([order(a["Wq"]), order(a["Wk"]), b["w_tor"], order(wq), order(wk), wv]),
        "wv": by_class(a["Wv"]), "wout": b["out_w"].T, "wr": f["Wr"],
        "cols": _np.stack([order(a["bq"]), order(a["bk"]), b["b_tor"], order(bq), order(bk)], axis=1),
        "rows": _np.stack([a["bv"], bv, b["out_b"]]),
        "wg": f["Wg"], "wu": f["Wu"], "wd": f["Wd"],
        "const": constants(),
    }
    nc = _bacc.Bacc("TRN2", target_bir_lowering=False, num_devices=1)
    d, arrays = Arrays(), {}
    ap = {}
    for name, v in given.items():
        v = _np.ascontiguousarray(v)
        arrays[f"in_{name}"] = v
        ap[name] = nc.dram_tensor(f"in_{name}", v.shape, _mybir.dt.from_np(v.dtype), kind="ExternalInput").ap()
    d.x, d.w_split, d.wout, d.wr, d.cols, d.rows = (ap[n] for n in ("x", "w_split", "wout", "wr", "cols", "rows"))
    d.wv, d.wg, d.wu, d.wd, d.const = ap["wv"], ap["wg"], ap["wu"], ap["wd"], ap["const"]
    scratch = lambda name, shape, dt: nc.dram_tensor(name, shape, dt).ap()
    d.parts = scratch("parts", (2, BATCHES, 3, D, TB), BF16)
    d.v = scratch("v_rows", (TOKENS, HEADS * (HD + 1)), F32)
    d.routed = scratch("routed", (REGION_ROWS, ROW), F32)
    d.expert = scratch("expert_out", (2 * (TOKENS + (EXPERTS + SPARE) * P), D), F32)
    d.outputs = d.expert[0:2 * TOKENS, :].rearrange("(t j) c -> t (j c)", j=TOPK)
    d.kept = scratch("kept", (TOKENS, ROW), F32)
    d.out = nc.dram_tensor("out", (TOKENS, D), _mybir.dt.float32, kind="ExternalOutput").ap()
    build(nc, d)
    r = _run(nc, [arrays], core_ids=[0])
    return _np.asarray(r.results[0]["out"]).reshape(ROWS, POSITIONS, D)
```
